# Optimizing a Trainium2 kernel written in Bass

```python
import numpy as np
import jax
import jax.numpy as jnp

def _softmax(x, axis=-1):
    return jax.nn.softmax(x, axis=axis)

def _gelu(x):
    return jax.nn.gelu(x, approximate=True)

def _silu(x):
    return jax.nn.silu(x)

def _sigmoid(x):
    return jax.nn.sigmoid(x)

def _layernorm(x, axis=-1, eps=1e-05):
    m = jnp.mean(x, axis=axis, keepdims=True)
    v = jnp.var(x, axis=axis, keepdims=True)
    return (x - m) / jnp.sqrt(v + eps)

def _scatter_add(tgt, idx, src, axis=0):
    return tgt.at[idx].add(src)

def _segment_sum(src, seg, n):
    return jax.ops.segment_sum(src, seg, n)
kernel_name = 'mk_seq_postln_d2_jaxref_r8_4a8bcc'

def setup_inputs(seed: int=0):
    np.random.seed(seed)
    _w = jnp.asarray

    def _L0_attn_setup():
        import jax, jax.numpy as jnp
        import numpy as np
        HIDDEN = 128
        STATE = 16
        DT_RANK = 64
        key = jax.random.key(seed)
        ks = jax.random.split(key, 5)
        B, S = (2, 256)
        x = jax.random.normal(ks[0], (B, S, HIDDEN), dtype=jnp.float32)
        W_xproj = jax.random.normal(ks[1], (HIDDEN, STATE * 2 + DT_RANK), dtype=jnp.float32) / np.sqrt(HIDDEN)
        W_dt = jax.random.normal(ks[2], (DT_RANK, HIDDEN), dtype=jnp.float32) / np.sqrt(DT_RANK)
        b_dt = jnp.zeros((HIDDEN,), dtype=jnp.float32)
        A_log = jax.random.normal(ks[3], (STATE, HIDDEN), dtype=jnp.float32) / np.sqrt(STATE)
        return {'x': x, 'W_xproj': W_xproj, 'W_dt': W_dt, 'b_dt': b_dt, 'A_log': A_log}
    _L0_attn_in = _L0_attn_setup()

    def _L0_ffn_setup():
        import jax, jax.numpy as jnp
        import numpy as np
        D_IN, D_HID = (128, 512)

        def _ternary(key, shape):
            return jax.random.randint(key, shape, -1, 2).astype(jnp.float32)

        def _tlin(x, w, s):
            return jnp.einsum('bsi,oi->bso', x, w) * s
        key = jax.random.key(seed)
        ks = jax.random.split(key, 12)
        inv = lambda fan: 1.0 / np.sqrt(fan).astype(np.float32)
        return {'x': jax.random.normal(ks[0], (4, 256, D_IN), dtype=jnp.float32), 'w1_w': _ternary(ks[1], (D_HID, D_IN)), 'w1_s': jax.random.uniform(ks[2], (D_HID,), dtype=jnp.float32) * inv(D_IN), 'w2_w': _ternary(ks[3], (D_HID, D_IN)), 'w2_s': jax.random.uniform(ks[4], (D_HID,), dtype=jnp.float32) * inv(D_IN), 'h1_w': _ternary(ks[5], (D_HID, D_HID)), 'h1_s': jax.random.uniform(ks[6], (D_HID,), dtype=jnp.float32) * inv(D_HID), 'h2_w': _ternary(ks[7], (D_HID, D_HID)), 'h2_s': jax.random.uniform(ks[8], (D_HID,), dtype=jnp.float32) * inv(D_HID), 'w3_w': _ternary(ks[9], (D_IN, D_HID)), 'w3_s': jax.random.uniform(ks[10], (D_IN,), dtype=jnp.float32) * inv(D_HID)}
    _L0_ffn_in = _L0_ffn_setup()

    def _L1_attn_setup():
        import jax, jax.numpy as jnp
        import numpy as np
        import math
        B, L, D = (2, 512, 128)
        H, DK, DV = (4, 32, 32)
        CS = 32
        CONV = 4
        FIR_S, FIR_L = (3, 31)
        GIN = D + 3 * DV
        GH = D * 2 // 2
        MIN_LOCAL = 0.05

        def dwconv(x, w):
            k = w.shape[-1]
            xf = jnp.pad(jnp.swapaxes(x, 1, 2), ((0, 0), (0, 0), (k - 1, 0)))
            y = jax.lax.conv_general_dilated(xf, w[:, None, :], (1,), 'VALID', dimension_numbers=('NCH', 'OIH', 'NCH'), feature_group_count=w.shape[0])
            return jnp.swapaxes(y, 1, 2)

        def l2n(x):
            return x * jax.lax.rsqrt(jnp.sum(x * x, -1, keepdims=True) + 1e-12)

        def delta_rule(q, k, v, beta):
            b, h, Lq, dk = q.shape
            dv = v.shape[-1]
            n = Lq // CS
            q, k = (l2n(q), l2n(k))
            v = v * beta[..., None]
            kb = k * beta[..., None]
            rs = lambda t: t.reshape(b, h, n, CS, t.shape[-1])
            q, k, v, kb = (rs(q), rs(k), rs(v), rs(kb))
            strict_lo = jnp.tril(jnp.ones((CS, CS), bool), -1)
            A = jnp.where(strict_lo, kb @ jnp.swapaxes(k, -1, -2), 0.0)
            eye = jnp.eye(CS, dtype=q.dtype)
            Tinv = jax.scipy.linalg.solve_triangular(eye + A, jnp.broadcast_to(eye, A.shape), lower=True, unit_diagonal=True)
            u = Tinv @ v
            w = Tinv @ kb
            strict_up = jnp.triu(jnp.ones((CS, CS), bool), 1)

            def step(S, xs):
                q_i, k_i, u_i, w_i = xs
                attn = jnp.where(strict_up, 0.0, q_i @ jnp.swapaxes(k_i, -1, -2))
                u_i = u_i - w_i @ S
                o_i = q_i @ S + attn @ u_i
                S = S + jnp.swapaxes(k_i, -1, -2) @ u_i
                return (S, o_i)
            mv = lambda t: jnp.moveaxis(t, 2, 0)
            S0 = jnp.zeros((b, h, dk, dv), q.dtype)
            _, out = jax.lax.scan(step, S0, (mv(q), mv(k), mv(u), mv(w)))
            return jnp.moveaxis(out, 0, 2).reshape(b, h, Lq, dv)

        def _forward(hidden_states, q_proj_w, k_proj_w, v_proj_w, b_proj_w, q_conv_w, k_conv_w, v_conv_w, fir_short_w, fir_long_w, fg_w1, fg_b1, fg_w2, fg_b2, logit_temp, o_norm_w, o_proj_w):
            b, l, _ = hidden_states.shape
            hs = hidden_states
            q = jax.nn.silu(dwconv(hs @ q_proj_w.T, q_conv_w)).reshape(b, l, H, DK)
            k = jax.nn.silu(dwconv(hs @ k_proj_w.T, k_conv_w)).reshape(b, l, H, DK)
            v = jax.nn.silu(dwconv(hs @ v_proj_w.T, v_conv_w)).reshape(b, l, H, DV)
            beta = jax.nn.sigmoid(hs @ b_proj_w.T)
            tr = lambda t: jnp.swapaxes(t, 1, 2)
            delta = tr(delta_rule(tr(q), tr(k), tr(v), jnp.swapaxes(beta, 1, 2)))
            fir = lambda x, w: dwconv(x.reshape(b, l, H * DV), w.reshape(H * DV, -1)).reshape(b, l, H, DV)
            short = fir(v, fir_short_w)
            long_ = fir(v, fir_long_w)
            gate_in = jnp.concatenate([hs, short.mean(2), long_.mean(2), delta.mean(2)], -1)
            logits = jax.nn.gelu(gate_in @ fg_w1.T + fg_b1, approximate=False) @ fg_w2.T + fg_b2
            temp = jax.nn.softplus(logit_temp) + 0.0001
            wgt = jax.nn.softmax(logits / temp, -1)[:, :, None, :]
            wgt = jnp.broadcast_to(wgt, (b, l, H, 4))
            floor = MIN_LOCAL * wgt[..., 3:4]
            wloc = jnp.maximum(wgt[..., :2], floor)
            wgt = jnp.concatenate([wloc, wgt[..., 2:]], -1)
            wgt = wgt / wgt.sum(-1, keepdims=True)
            o = wgt[..., 0:1] * short + wgt[..., 1:2] * long_ + wgt[..., 2:3] * delta + wgt[..., 3:4] * v
            o = o * jax.lax.rsqrt(jnp.mean(o * o, -1, keepdims=True) + 1e-05) * o_norm_w
            return o.reshape(b, l, H * DV) @ o_proj_w.T
        key = jax.random.key(seed)
        ks = jax.random.split(key, 12)
        s = 0.02
        return {'hidden_states': jax.random.normal(ks[0], (B, L, D), jnp.float32), 'q_proj_w': jax.random.normal(ks[1], (H * DK, D), jnp.float32) * s, 'k_proj_w': jax.random.normal(ks[2], (H * DK, D), jnp.float32) * s, 'v_proj_w': jax.random.normal(ks[3], (H * DV, D), jnp.float32) * s, 'b_proj_w': jax.random.normal(ks[4], (H, D), jnp.float32) * s, 'q_conv_w': jax.random.normal(ks[5], (H * DK, CONV), jnp.float32) * s, 'k_conv_w': jax.random.normal(ks[6], (H * DK, CONV), jnp.float32) * s, 'v_conv_w': jax.random.normal(ks[7], (H * DV, CONV), jnp.float32) * s, 'fir_short_w': jnp.zeros((H, DV, FIR_S), jnp.float32).at[..., -1].set(1.0), 'fir_long_w': jnp.zeros((H, DV, FIR_L), jnp.float32).at[..., -1].set(1.0), 'fg_w1': jax.random.normal(ks[8], (GH, GIN), jnp.float32) * s, 'fg_b1': jnp.zeros((GH,), jnp.float32), 'fg_w2': jax.random.normal(ks[9], (4, GH), jnp.float32) * s, 'fg_b2': jnp.array([-0.2, -0.2, 1.0, 3.0], jnp.float32), 'logit_temp': jnp.full((1,), math.log(math.expm1(0.7)), jnp.float32), 'o_norm_w': jnp.ones((DV,), jnp.float32), 'o_proj_w': jax.random.normal(ks[10], (D, H * DV), jnp.float32) * s}
    _L1_attn_in = _L1_attn_setup()

    def _L1_ffn_setup():
        import jax, jax.numpy as jnp
        import numpy as np
        H = 128
        I = 256
        E = 32
        B, S = (4, 256)

        def _grouped_mm(a, w, group_sizes):
            return jax.lax.ragged_dot(a, w, group_sizes)

        def _swiglu(x, gw, uw, dw):
            return jax.nn.silu(x @ gw) * (x @ uw) @ dw
        key = jax.random.key(seed)
        ks = jax.random.split(key, 8)
        scale = 0.02
        inp = {'hidden_states': jax.random.normal(ks[0], (B, S, H), dtype=jnp.float32), 'gate_w': jax.random.normal(ks[1], (H, E), dtype=jnp.float32) * scale, 'shared_gate_w': jax.random.normal(ks[2], (H, I), dtype=jnp.float32) * scale, 'shared_up_w': jax.random.normal(ks[3], (H, I), dtype=jnp.float32) * scale, 'shared_down_w': jax.random.normal(ks[4], (I, H), dtype=jnp.float32) * scale, 'routed_gate_w': jax.random.normal(ks[5], (E, H, I), dtype=jnp.float32) * scale, 'routed_up_w': jax.random.normal(ks[6], (E, H, I), dtype=jnp.float32) * scale, 'routed_down_w': jax.random.normal(ks[7], (E, I, H), dtype=jnp.float32) * scale}
        return inp
    _L1_ffn_in = _L1_ffn_setup()
    _d = {'L0_attn_x': _L0_attn_in['x'], 'L0_attn_W_xproj': _L0_attn_in['W_xproj'], 'L0_attn_W_dt': _L0_attn_in['W_dt'], 'L0_attn_b_dt': _L0_attn_in['b_dt'], 'L0_attn_A_log': _L0_attn_in['A_log'], 'L0_ffn_w1_w': _L0_ffn_in['w1_w'], 'L0_ffn_w1_s': _L0_ffn_in['w1_s'], 'L0_ffn_w2_w': _L0_ffn_in['w2_w'], 'L0_ffn_w2_s': _L0_ffn_in['w2_s'], 'L0_ffn_h1_w': _L0_ffn_in['h1_w'], 'L0_ffn_h1_s': _L0_ffn_in['h1_s'], 'L0_ffn_h2_w': _L0_ffn_in['h2_w'], 'L0_ffn_h2_s': _L0_ffn_in['h2_s'], 'L0_ffn_w3_w': _L0_ffn_in['w3_w'], 'L0_ffn_w3_s': _L0_ffn_in['w3_s'], 'L1_attn_q_proj_w': _L1_attn_in['q_proj_w'], 'L1_attn_k_proj_w': _L1_attn_in['k_proj_w'], 'L1_attn_v_proj_w': _L1_attn_in['v_proj_w'], 'L1_attn_b_proj_w': _L1_attn_in['b_proj_w'], 'L1_attn_q_conv_w': _L1_attn_in['q_conv_w'], 'L1_attn_k_conv_w': _L1_attn_in['k_conv_w'], 'L1_attn_v_conv_w': _L1_attn_in['v_conv_w'], 'L1_attn_fir_short_w': _L1_attn_in['fir_short_w'], 'L1_attn_fir_long_w': _L1_attn_in['fir_long_w'], 'L1_attn_fg_w1': _L1_attn_in['fg_w1'], 'L1_attn_fg_b1': _L1_attn_in['fg_b1'], 'L1_attn_fg_w2': _L1_attn_in['fg_w2'], 'L1_attn_fg_b2': _L1_attn_in['fg_b2'], 'L1_attn_logit_temp': _L1_attn_in['logit_temp'], 'L1_attn_o_norm_w': _L1_attn_in['o_norm_w'], 'L1_attn_o_proj_w': _L1_attn_in['o_proj_w'], 'L1_ffn_gate_w': _L1_ffn_in['gate_w'], 'L1_ffn_shared_gate_w': _L1_ffn_in['shared_gate_w'], 'L1_ffn_shared_up_w': _L1_ffn_in['shared_up_w'], 'L1_ffn_shared_down_w': _L1_ffn_in['shared_down_w'], 'L1_ffn_routed_gate_w': _L1_ffn_in['routed_gate_w'], 'L1_ffn_routed_up_w': _L1_ffn_in['routed_up_w'], 'L1_ffn_routed_down_w': _L1_ffn_in['routed_down_w']}
    _x0 = _d['L0_attn_x']
    _d['L0_attn_x'] = jax.random.normal(jax.random.fold_in(jax.random.key(seed), 1), (8, 1024, 128), dtype=_x0.dtype)
    del _x0
    return _d

def reference(L0_attn_x, L0_attn_W_xproj, L0_attn_W_dt, L0_attn_b_dt, L0_attn_A_log, L0_ffn_w1_w, L0_ffn_w1_s, L0_ffn_w2_w, L0_ffn_w2_s, L0_ffn_h1_w, L0_ffn_h1_s, L0_ffn_h2_w, L0_ffn_h2_s, L0_ffn_w3_w, L0_ffn_w3_s, L1_attn_q_proj_w, L1_attn_k_proj_w, L1_attn_v_proj_w, L1_attn_b_proj_w, L1_attn_q_conv_w, L1_attn_k_conv_w, L1_attn_v_conv_w, L1_attn_fir_short_w, L1_attn_fir_long_w, L1_attn_fg_w1, L1_attn_fg_b1, L1_attn_fg_w2, L1_attn_fg_b2, L1_attn_logit_temp, L1_attn_o_norm_w, L1_attn_o_proj_w, L1_ffn_gate_w, L1_ffn_shared_gate_w, L1_ffn_shared_up_w, L1_ffn_shared_down_w, L1_ffn_routed_gate_w, L1_ffn_routed_up_w, L1_ffn_routed_down_w):

    def _L0_attn_ref(x, W_xproj, W_dt, b_dt, A_log):
        import jax, jax.numpy as jnp
        import numpy as np
        HIDDEN = 128
        STATE = 16
        DT_RANK = 64
        xp = x @ W_xproj
        Bm = xp[..., :STATE]
        Cm = xp[..., STATE:2 * STATE]
        dt = jax.nn.softplus(xp[..., 2 * STATE:] @ W_dt + b_dt)
        A = -jnp.exp(A_log)
        A_bar = jnp.exp(A[None, None] * dt[:, :, None, :])
        Bu = Bm[:, :, :, None] * dt[:, :, None, :] * x[:, :, None, :]

        def scan_fn(h, inp):
            A_t, Bu_t = inp
            h = A_t * h + Bu_t
            return (h, h)
        h0 = jnp.zeros(Bu.shape[:1] + Bu.shape[2:], dtype=x.dtype)
        _, h_all = jax.lax.scan(scan_fn, h0, (A_bar.transpose(1, 0, 2, 3), Bu.transpose(1, 0, 2, 3)))
        y = jnp.einsum('bsn,sbnd->bsd', Cm, h_all)
        return y

    def _L0_ffn_ref(x, w1_w, w1_s, w2_w, w2_s, h1_w, h1_s, h2_w, h2_s, w3_w, w3_s):
        import jax, jax.numpy as jnp
        import numpy as np
        D_IN, D_HID = (128, 512)

        def _ternary(key, shape):
            return jax.random.randint(key, shape, -1, 2).astype(jnp.float32)

        def _tlin(x, w, s):
            return jnp.einsum('bsi,oi->bso', x, w) * s
        h = jax.nn.silu(_tlin(x, w1_w, w1_s)) * _tlin(x, w2_w, w2_s)
        h = jax.nn.gelu(_tlin(h, h1_w, h1_s), approximate=False)
        h = jax.nn.gelu(_tlin(h, h2_w, h2_s), approximate=False)
        return _tlin(h, w3_w, w3_s)

    def _L1_attn_ref(hidden_states, q_proj_w, k_proj_w, v_proj_w, b_proj_w, q_conv_w, k_conv_w, v_conv_w, fir_short_w, fir_long_w, fg_w1, fg_b1, fg_w2, fg_b2, logit_temp, o_norm_w, o_proj_w):
        import jax, jax.numpy as jnp
        import numpy as np
        import math
        B, L, D = (2, 512, 128)
        H, DK, DV = (4, 32, 32)
        CS = 32
        CONV = 4
        FIR_S, FIR_L = (3, 31)
        GIN = D + 3 * DV
        GH = D * 2 // 2
        MIN_LOCAL = 0.05

        def dwconv(x, w):
            k = w.shape[-1]
            xf = jnp.pad(jnp.swapaxes(x, 1, 2), ((0, 0), (0, 0), (k - 1, 0)))
            y = jax.lax.conv_general_dilated(xf, w[:, None, :], (1,), 'VALID', dimension_numbers=('NCH', 'OIH', 'NCH'), feature_group_count=w.shape[0])
            return jnp.swapaxes(y, 1, 2)

        def l2n(x):
            return x * jax.lax.rsqrt(jnp.sum(x * x, -1, keepdims=True) + 1e-12)

        def delta_rule(q, k, v, beta):
            b, h, Lq, dk = q.shape
            dv = v.shape[-1]
            n = Lq // CS
            q, k = (l2n(q), l2n(k))
            v = v * beta[..., None]
            kb = k * beta[..., None]
            rs = lambda t: t.reshape(b, h, n, CS, t.shape[-1])
            q, k, v, kb = (rs(q), rs(k), rs(v), rs(kb))
            strict_lo = jnp.tril(jnp.ones((CS, CS), bool), -1)
            A = jnp.where(strict_lo, kb @ jnp.swapaxes(k, -1, -2), 0.0)
            eye = jnp.eye(CS, dtype=q.dtype)
            Tinv = jax.scipy.linalg.solve_triangular(eye + A, jnp.broadcast_to(eye, A.shape), lower=True, unit_diagonal=True)
            u = Tinv @ v
            w = Tinv @ kb
            strict_up = jnp.triu(jnp.ones((CS, CS), bool), 1)

            def step(S, xs):
                q_i, k_i, u_i, w_i = xs
                attn = jnp.where(strict_up, 0.0, q_i @ jnp.swapaxes(k_i, -1, -2))
                u_i = u_i - w_i @ S
                o_i = q_i @ S + attn @ u_i
                S = S + jnp.swapaxes(k_i, -1, -2) @ u_i
                return (S, o_i)
            mv = lambda t: jnp.moveaxis(t, 2, 0)
            S0 = jnp.zeros((b, h, dk, dv), q.dtype)
            _, out = jax.lax.scan(step, S0, (mv(q), mv(k), mv(u), mv(w)))
            return jnp.moveaxis(out, 0, 2).reshape(b, h, Lq, dv)

        def _forward(hidden_states, q_proj_w, k_proj_w, v_proj_w, b_proj_w, q_conv_w, k_conv_w, v_conv_w, fir_short_w, fir_long_w, fg_w1, fg_b1, fg_w2, fg_b2, logit_temp, o_norm_w, o_proj_w):
            b, l, _ = hidden_states.shape
            hs = hidden_states
            q = jax.nn.silu(dwconv(hs @ q_proj_w.T, q_conv_w)).reshape(b, l, H, DK)
            k = jax.nn.silu(dwconv(hs @ k_proj_w.T, k_conv_w)).reshape(b, l, H, DK)
            v = jax.nn.silu(dwconv(hs @ v_proj_w.T, v_conv_w)).reshape(b, l, H, DV)
            beta = jax.nn.sigmoid(hs @ b_proj_w.T)
            tr = lambda t: jnp.swapaxes(t, 1, 2)
            delta = tr(delta_rule(tr(q), tr(k), tr(v), jnp.swapaxes(beta, 1, 2)))
            fir = lambda x, w: dwconv(x.reshape(b, l, H * DV), w.reshape(H * DV, -1)).reshape(b, l, H, DV)
            short = fir(v, fir_short_w)
            long_ = fir(v, fir_long_w)
            gate_in = jnp.concatenate([hs, short.mean(2), long_.mean(2), delta.mean(2)], -1)
            logits = jax.nn.gelu(gate_in @ fg_w1.T + fg_b1, approximate=False) @ fg_w2.T + fg_b2
            temp = jax.nn.softplus(logit_temp) + 0.0001
            wgt = jax.nn.softmax(logits / temp, -1)[:, :, None, :]
            wgt = jnp.broadcast_to(wgt, (b, l, H, 4))
            floor = MIN_LOCAL * wgt[..., 3:4]
            wloc = jnp.maximum(wgt[..., :2], floor)
            wgt = jnp.concatenate([wloc, wgt[..., 2:]], -1)
            wgt = wgt / wgt.sum(-1, keepdims=True)
            o = wgt[..., 0:1] * short + wgt[..., 1:2] * long_ + wgt[..., 2:3] * delta + wgt[..., 3:4] * v
            o = o * jax.lax.rsqrt(jnp.mean(o * o, -1, keepdims=True) + 1e-05) * o_norm_w
            return o.reshape(b, l, H * DV) @ o_proj_w.T
        return _forward(hidden_states, q_proj_w, k_proj_w, v_proj_w, b_proj_w, q_conv_w, k_conv_w, v_conv_w, fir_short_w, fir_long_w, fg_w1, fg_b1, fg_w2, fg_b2, logit_temp, o_norm_w, o_proj_w)

    def _L1_ffn_ref(hidden_states, gate_w, shared_gate_w, shared_up_w, shared_down_w, routed_gate_w, routed_up_w, routed_down_w):
        import jax, jax.numpy as jnp
        import numpy as np
        H = 128
        I = 256
        E = 32
        B, S = (4, 256)

        def _grouped_mm(a, w, group_sizes):
            return jax.lax.ragged_dot(a, w, group_sizes)

        def _swiglu(x, gw, uw, dw):
            return jax.nn.silu(x @ gw) * (x @ uw) @ dw
        b, s, h = hidden_states.shape
        x = hidden_states.reshape(-1, h)
        shared_out = _swiglu(x, shared_gate_w, shared_up_w, shared_down_w)
        logits = x @ gate_w
        topk_ids = jnp.argmax(logits, axis=-1)
        topk_val = jnp.max(logits, axis=-1)
        scores = jax.nn.sigmoid(topk_val)[:, None]
        xs = x * scores
        tokens_per_expert = jnp.zeros((E,), jnp.int32).at[topk_ids].add(1)
        order = jnp.argsort(topk_ids)
        sorted_x = xs[order]
        g = _grouped_mm(sorted_x, routed_gate_w, tokens_per_expert)
        u = _grouped_mm(sorted_x, routed_up_w, tokens_per_expert)
        d = _grouped_mm(jax.nn.silu(g) * u, routed_down_w, tokens_per_expert)
        inv = jnp.argsort(order)
        routed_out = d[inv]
        return (shared_out + routed_out).reshape(b, s, h)
    x = L0_attn_x
    x = _layernorm(x + _L0_attn_ref(x, L0_attn_W_xproj, L0_attn_W_dt, L0_attn_b_dt, L0_attn_A_log), axis=-1)
    x = _layernorm(x + _L0_ffn_ref(x, L0_ffn_w1_w, L0_ffn_w1_s, L0_ffn_w2_w, L0_ffn_w2_s, L0_ffn_h1_w, L0_ffn_h1_s, L0_ffn_h2_w, L0_ffn_h2_s, L0_ffn_w3_w, L0_ffn_w3_s), axis=-1)
    x = _layernorm(x + _L1_attn_ref(x, L1_attn_q_proj_w, L1_attn_k_proj_w, L1_attn_v_proj_w, L1_attn_b_proj_w, L1_attn_q_conv_w, L1_attn_k_conv_w, L1_attn_v_conv_w, L1_attn_fir_short_w, L1_attn_fir_long_w, L1_attn_fg_w1, L1_attn_fg_b1, L1_attn_fg_w2, L1_attn_fg_b2, L1_attn_logit_temp, L1_attn_o_norm_w, L1_attn_o_proj_w), axis=-1)
    x = _layernorm(x + _L1_ffn_ref(x, L1_ffn_gate_w, L1_ffn_shared_gate_w, L1_ffn_shared_up_w, L1_ffn_shared_down_w, L1_ffn_routed_gate_w, L1_ffn_routed_up_w, L1_ffn_routed_down_w), axis=-1)
    return x

_drawn_inputs = setup_inputs


def setup_inputs(seed=0):
    import zlib

    import numpy as np

    out = dict(_drawn_inputs(seed))
    spreads = {'L0_attn_b_dt': (0.0, 0.1), 'L1_attn_fg_b1': (0.0, 2.0), 'L1_attn_o_norm_w': (1.0, 0.2)}
    factors = {'L0_ffn_w1_w': 8.0,
     'L0_ffn_w1_s': 8.0,
     'L0_ffn_w2_w': 8.0,
     'L0_ffn_w2_s': 8.0,
     'L0_ffn_h1_w': 8.0,
     'L0_ffn_h1_s': 8.0,
     'L0_ffn_h2_w': 8.0,
     'L0_ffn_h2_s': 8.0,
     'L0_ffn_w3_w': 8.0,
     'L0_ffn_w3_s': 8.0,
     'L1_attn_q_proj_w': 64.0,
     'L1_attn_k_proj_w': 64.0,
     'L1_attn_b_proj_w': 64.0,
     'L1_attn_q_conv_w': 64.0,
     'L1_attn_k_conv_w': 64.0,
     'L1_attn_fir_long_w': 8.0,
     'L1_attn_fg_w1': 64.0,
     'L1_attn_fg_w2': 64.0,
     'L1_attn_fg_b2': 8.0,
     'L1_ffn_gate_w': 8.0,
     'L1_ffn_shared_gate_w': 6.883,
     'L1_ffn_shared_up_w': 6.802,
     'L1_ffn_shared_down_w': 6.881,
     'L1_ffn_routed_gate_w': 8.0,
     'L1_ffn_routed_up_w': 8.0,
     'L1_ffn_routed_down_w': 8.0}
    for name, (base, spread) in spreads.items():
        noise = np.random.default_rng([zlib.crc32(name.encode()), seed]).standard_normal(out[name].shape)
        drawn = base * np.exp(spread * noise) if base else spread * noise
        out[name] = jnp.asarray(drawn.astype(out[name].dtype))
    for name, factor in factors.items():
        out[name] = (out[name] * factor).astype(out[name].dtype)
    return out
```

```python
from contextlib import ExitStack

import numpy as np

import concourse.bass as bass
from concourse import mybir

F32 = mybir.dt.float32
BF16 = mybir.dt.bfloat16
I32 = mybir.dt.int32
U32 = mybir.dt.uint32
U16 = mybir.dt.uint16
ALU = mybir.AluOpType
ACT = mybir.ActivationFunctionType
AX = mybir.AxisListType

D = 128
B = 8
S = 1024
T = 512
TILES = B * S // T
HALVES = S // T
PAD = 4
ROW = PAD + S
LAG = 3
READS = 4
NSTATE = 16
DTR = 64
HID = 512
KT = HID // 128
EPS = 1e-5
LN_EXP = "natural_log_exp_and_others"


def alloc(nc, ctx):
    def sb(name, shape, dt=F32):
        return ctx.enter_context(nc.sbuf_tensor(name, shape, dt))

    def ps(name, shape, dt=F32):
        return ctx.enter_context(nc.psum_tensor(name, shape, dt))

    def sem(name):
        return ctx.enter_context(nc.semaphore(name))

    return sb, ps, sem


def loop(eng, n, body):
    body(0)
    with eng.Fori(1, n) as i:
        body(i)


def is_first(i):
    return isinstance(i, int) and i == 0


def tile_cols(X, t):
    if isinstance(t, int):
        b, h = t // HALVES, t % HALVES
        return X[:, b * ROW + PAD + h * T:b * ROW + PAD + (h + 1) * T]
    raise TypeError


def seq_cols(X, b, lo, n):
    return X[:, bass.ds(b * ROW + (PAD + lo), n)]


def scan_inputs(nc, X, dt, dtx, parts, w):
    with ExitStack() as ctx:
        sb, ps, sem = alloc(nc, ctx)
        wbc, wr, wdt = sb("wbc", [D, 96]), sb("wr", [D, DTR]), sb("wdt", [DTR, D])
        bdt = sb("bdt", [D, 1])
        low = sb("low", [DTR, T])
        rest, rest2, mid = sb("rest", [96, T]), sb("rest2", [96, T]), sb("mid", [96, T], BF16)
        absz, expz, lnz, posz = (sb(n, [D, T]) for n in ("absz", "expz", "lnz", "posz"))
        p_bc, p_low, p_z = ps("p_bc", [96, T]), ps("p_low", [DTR, T]), ps("p_z", [D, T])
        s_w, s_x, s_pad = sem("a_weights"), sem("a_x"), sem("a_pad")
        s_proj, s_low, s_z = sem("a_proj"), sem("a_low"), sem("a_z")
        s_hi, s_rest, s_mid, s_rest2, s_parts = sem("a_hi"), sem("a_rest"), sem("a_mid"), sem("a_rest2"), sem("a_parts")
        s_abs, s_exp, s_ln, s_pos, s_dt, s_dtx = (sem(n) for n in ("a_abs", "a_exp", "a_ln", "a_pos", "a_dt", "a_dtx"))
        block = ctx.enter_context(nc.Block())

        @block.sync
        def _(sp):
            for dst, src in ((wbc, w["bc"]), (wr, w["low"]), (wdt, w["dt"]), (bdt, w["b_dt"])):
                sp.dma_start(dst[:, :], src[:, :]).then_inc(s_w, 16)
            sp.dma_start(X[:, :].rearrange("p (b c) -> p b c", c=ROW)[:, :, PAD:ROW],
                         w["x"].rearrange("p (b c) -> p b c", c=S)).then_inc(s_x, 16)

        @block.gpsimd
        def _(pool):
            nc.gpsimd.memset(X[:, :].rearrange("p (b c) -> p b c", c=ROW)[:, :, 0:PAD], 0.0).then_inc(s_pad, 1)

        @block.tensor
        def _(pe):
            pe.wait_ge(s_w, 64)
            pe.wait_ge(s_x, 16)

            def body(b):
                for h in range(HALVES):
                    t = b * HALVES + h
                    x = seq_cols(X, b, h * T, T)
                    first = is_first(b) and h == 0
                    if not first:
                        pe.wait_ge(s_hi, t)
                        pe.wait_ge(s_rest, t)
                        pe.wait_ge(s_low, t)
                    nc.tensor.matmul(p_bc[:, :], wbc[:, :], x, start=True, stop=True)
                    nc.tensor.matmul(p_low[:, :], wr[:, :], x, start=True, stop=True).then_inc(s_proj, 1)
                    pe.wait_ge(s_low, t + 1)
                    if not first:
                        pe.wait_ge(s_abs, t)
                        pe.wait_ge(s_pos, t)
                    nc.tensor.matmul(p_z[:, :], wdt[:, :], low[:, :], start=True, stop=True).then_inc(s_z, 1)

            loop(pe, B, body)

        @block.scalar
        def _(act):
            nc.scalar.preload_act_table_set(LN_EXP)
            act.wait_ge(s_w, 64)

            def body(b):
                for h in range(HALVES):
                    t = b * HALVES + h
                    first = is_first(b) and h == 0
                    cols = bass.ds(b * S + h * T, T)
                    act.wait_ge(s_proj, t + 1)
                    nc.scalar.copy(low[:, :], p_low[:, :]).then_inc(s_low, 1)
                    act.nop()
                    nc.scalar.copy(parts[:, cols], p_bc[:, :]).then_inc(s_hi, 1)
                    act.wait_ge(s_rest, t + 1)
                    if not first:
                        act.wait_ge(s_rest2, t)
                    nc.scalar.copy(mid[:, :], rest[:, :]).then_inc(s_mid, 1)
                    act.wait_ge(s_mid, t + 1)
                    act.nop()
                    nc.scalar.copy(parts[32:64, cols], mid[32:64, :]).then_inc(s_parts, 1)
                    act.wait_ge(s_rest2, t + 1)
                    act.nop()
                    nc.scalar.copy(parts[64:96, cols], rest2[64:96, :]).then_inc(s_parts, 1)
                    act.wait_ge(s_z, t + 1)
                    nc.scalar.activation(absz[:, :], p_z[:, :], ACT.Abs, bias=bdt[:, 0:1]).then_inc(s_abs, 1)
                    act.wait_ge(s_abs, t + 1)
                    nc.scalar.activation(expz[:, :], absz[:, :], ACT.Exp, scale=-1.0).then_inc(s_exp, 1)
                    act.wait_ge(s_exp, t + 1)
                    if not first:
                        act.wait_ge(s_dt, t)
                    nc.scalar.activation(lnz[:, :], expz[:, :], ACT.Ln, bias=1.0).then_inc(s_ln, 1)

            loop(act, B, body)

        @block.vector
        def _(dve):
            dve.wait_ge(s_w, 64)
            dve.wait_ge(s_x, 16)

            def body(b):
                for h in range(HALVES):
                    t = b * HALVES + h
                    first = is_first(b) and h == 0
                    cols = bass.ds(b * S + h * T, T)
                    dve.wait_ge(s_hi, t + 1)
                    if not first:
                        dve.wait_ge(s_parts, 2 * t)
                    nc.vector.tensor_tensor(rest[:, :], p_bc[:, :], parts[:, cols], ALU.subtract).then_inc(s_rest, 1)
                    dve.wait_ge(s_mid, t + 1)
                    nc.vector.tensor_tensor(rest2[:, :], rest[:, :], mid[:, :], ALU.subtract).then_inc(s_rest2, 1)
                    dve.wait_ge(s_abs, t + 1)
                    nc.vector.tensor_scalar(posz[:, :], p_z[:, :], bdt[:, 0:1], 0.0, ALU.add, ALU.max).then_inc(s_pos, 1)
                    dve.wait_ge(s_pos, t + 1)
                    dve.wait_ge(s_ln, t + 1)
                    nc.vector.tensor_tensor(dt[:, cols], posz[:, :], lnz[:, :], ALU.add).then_inc(s_dt, 1)
                    dve.wait_ge(s_dt, t + 1)
                    nc.vector.tensor_tensor(dtx[:, cols], dt[:, cols], seq_cols(X, b, h * T, T),
                                            ALU.mult).then_inc(s_dtx, 1)

            loop(dve, B, body)


def selective_scan(nc, X, dt, dtx, parts, w):
    with ExitStack() as ctx:
        sb, ps, sem = alloc(nc, ctx)
        select = sb("select", [96, 2 * NSTATE, D], BF16)
        ident = sb("ident_a", [D, D])
        alog, negA = sb("alog", [D, NSTATE]), sb("negA", [D, NSTATE])
        dtseq = sb("dtseq", [D, S])
        decay = sb("decay", [D, 2, S])
        inject = sb("inject", [D, 2, S])
        state = sb("state", [D, 2, S])
        crow = sb("crow", [D, 2, S])
        read = sb("read", [D, READS, S])
        p_b, p_c, p_y = ps("p_b", [D, 2, HALVES, T]), ps("p_c", [D, HALVES, T]), ps("p_y", [D, HALVES, T])
        s_w, s_ea, s_a, s_dtcopy = sem("b_weights"), sem("b_expA"), sem("b_negA"), sem("b_dtcopy")
        s_bready, s_inject, s_decay, s_state = (sem(n) for n in ("b_bready", "b_inject", "b_decay", "b_state"))
        s_cready, s_crow, s_read, s_summed = (sem(n) for n in ("b_cready", "b_crow", "b_read", "b_summed"))
        s_yused = sem("b_yused")
        block = ctx.enter_context(nc.Block())

        @block.sync
        def _(sp):
            sp.dma_start(select[:, :, :].bitcast(U16), w["select"][:, :, :]).then_inc(s_w, 16)
            sp.dma_start(ident[:, :], w["ident"][:, :]).then_inc(s_w, 16)
            sp.dma_start(alog[:, :], w["A_log"][:, :]).then_inc(s_w, 16)

        @block.tensor
        def _(pe):
            pe.wait_ge(s_w, 48)

            def sum_states(b, n):
                pe.wait_ge(s_read, b * NSTATE + n + 1)
                if n == 0 and not is_first(b):
                    pe.wait_ge(s_yused, HALVES * b)
                for h in range(HALVES):
                    mm = nc.tensor.matmul(p_y[:, h, :], ident[:, :], read[:, n % READS, h * T:(h + 1) * T],
                                          start=(n == 0), stop=(n == NSTATE - 1))
                mm.then_inc(s_summed, 1)

            def body(b):
                for n in range(NSTATE):
                    k = b * NSTATE + n
                    first = is_first(b) and n == 0
                    for h in range(HALVES):
                        rhs = parts[:, bass.ds(b * S + h * T, T)]
                        if not is_first(b) or n >= 2:
                            pe.wait_ge(s_inject, HALVES * (k - 2) + h + 1)
                        nc.tensor.matmul(p_b[:, n % 2, h, :], select[:, n, :], rhs, start=True, stop=True).then_inc(s_bready, 1)
                    for h in range(HALVES):
                        rhs = parts[:, bass.ds(b * S + h * T, T)]
                        if not first:
                            pe.wait_ge(s_crow, HALVES * (k - 1) + h + 1)
                        nc.tensor.matmul(p_c[:, h, :], select[:, NSTATE + n, :], rhs,
                                         start=True, stop=True).then_inc(s_cready, 1)
                    if n >= LAG:
                        sum_states(b, n - LAG)
                    elif not is_first(b):
                        sum_states(b - 1, NSTATE - LAG + n)

            loop(pe, B, body)
            for n in range(NSTATE - LAG, NSTATE):
                sum_states(B - 1, n)

        @block.scalar
        def _(act):
            act.wait_ge(s_w, 48)
            nc.scalar.activation(alog[:, :], alog[:, :], ACT.Exp).then_inc(s_ea, 1)
            act.wait_ge(s_a, 1)

            def body(b):
                if not is_first(b):
                    act.wait_ge(s_decay, NSTATE * b)
                nc.scalar.copy(dtseq[:, :], dt[:, bass.ds(b * S, S)]).then_inc(s_dtcopy, 1)
                for n in range(NSTATE):
                    k = b * NSTATE + n
                    warm = not is_first(b) or n >= 2
                    if warm:
                        act.wait_ge(s_state, k - 1)
                    if n == 0:
                        act.wait_ge(s_dtcopy, b + 1)
                    nc.scalar.activation(decay[:, n % 2, :], dtseq[:, :], ACT.Exp,
                                         scale=negA[:, n:n + 1]).then_inc(s_decay, 1)
                    if warm:
                        act.wait_ge(s_read, k - 1)
                    for h in range(HALVES):
                        act.wait_ge(s_cready, HALVES * k + h + 1)
                        nc.scalar.copy(crow[:, n % 2, h * T:(h + 1) * T], p_c[:, h, :]).then_inc(s_crow, 1)

            loop(act, B, body)

        @block.gpsimd
        def _(pool):
            def body(b):
                for n in range(NSTATE):
                    k = b * NSTATE + n
                    pool.wait_ge(s_state, k + 1)
                    pool.wait_ge(s_crow, HALVES * (k + 1))
                    if not is_first(b) or n >= READS:
                        pool.wait_ge(s_summed, k - READS + 1)
                    nc.gpsimd.tensor_tensor(read[:, n % READS, :], state[:, n % 2, :], crow[:, n % 2, :],
                                            ALU.mult).then_inc(s_read, 1)

            loop(pool, B, body)

        @block.vector
        def _(dve):
            dve.wait_ge(s_ea, 1)
            nc.vector.tensor_scalar(negA[:, :], alog[:, :], -1.0, None, ALU.mult).then_inc(s_a, 1)

            def body(b):
                def make_inject(n):
                    k = b * NSTATE + n
                    if not is_first(b) or n >= 2:
                        dve.wait_ge(s_state, k - 1)
                    for h in range(HALVES):
                        dve.wait_ge(s_bready, HALVES * k + h + 1)
                        nc.vector.tensor_tensor(inject[:, n % 2, h * T:(h + 1) * T], p_b[:, n % 2, h, :],
                                                dtx[:, bass.ds(b * S + h * T, T)], ALU.mult).then_inc(s_inject, 1)

                make_inject(0)
                for n in range(NSTATE):
                    k = b * NSTATE + n
                    if n + 1 < NSTATE:
                        make_inject(n + 1)
                    dve.wait_ge(s_inject, HALVES * (k + 1))
                    dve.wait_ge(s_decay, k + 1)
                    if not is_first(b) or n >= 2:
                        dve.wait_ge(s_read, k - 1)
                    nc.vector.tensor_tensor_scan(state[:, n % 2, :], decay[:, n % 2, :], inject[:, n % 2, :], 0.0,
                                                 ALU.mult, ALU.add).then_inc(s_state, 1)
                    if n == LAG - 1 and not is_first(b):
                        add_sums(b - 1)

            def add_sums(b):
                dve.wait_ge(s_summed, NSTATE * (b + 1))
                for h in range(HALVES):
                    x = seq_cols(X, b, h * T, T)
                    nc.vector.tensor_tensor(x, p_y[:, h, :], x, ALU.add).then_inc(s_yused, 1)

            loop(dve, B, body)
            add_sums(B - 1)


def layer_norm(nc, X, w, tag):
    with ExitStack() as ctx:
        sb, ps, sem = alloc(nc, ctx)
        mean_w = sb(tag + "mean_w", [D, D])
        eps = sb(tag + "eps", [D, 1])
        centred, square = sb(tag + "centred", [D, 2, T]), sb(tag + "square", [D, 2, T])
        logv, rstd = sb(tag + "logv", [D, 2, T]), sb(tag + "rstd", [D, 2, T])
        p_mean, p_var = ps(tag + "p_mean", [D, 2, T]), ps(tag + "p_var", [D, 2, T])
        s_w, s_eps = sem(tag + "weights"), sem(tag + "eps_set")
        s_mean, s_centred, s_square, s_var, s_log, s_rstd, s_out = (
            sem(tag + n) for n in ("mean", "centred", "square", "var", "log", "rstd", "out"))
        block = ctx.enter_context(nc.Block())

        @block.sync
        def _(sp):
            sp.dma_start(mean_w[:, :], w["mean_w"][:, :]).then_inc(s_w, 16)

        @block.tensor
        def _(pe):
            pe.wait_ge(s_w, 16)

            def mean(b, h):
                t = b * HALVES + h
                if not is_first(b):
                    pe.wait_ge(s_centred, t - 1)
                nc.tensor.matmul(p_mean[:, h, :], mean_w[:, :], seq_cols(X, b, h * T, T),
                                 start=True, stop=True).then_inc(s_mean, 1)

            def var(b, h):
                t = b * HALVES + h
                pe.wait_ge(s_square, t + 1)
                if not is_first(b):
                    pe.wait_ge(s_log, t - 1)
                nc.tensor.matmul(p_var[:, h, :], mean_w[:, :], square[:, h, :],
                                 start=True, stop=True).then_inc(s_var, 1)

            def body(b):
                mean(b, 0)
                mean(b, 1)
                var(b, 0)
                var(b, 1)

            loop(pe, B, body)

        @block.scalar
        def _(act):
            nc.scalar.preload_act_table_set(LN_EXP)
            act.wait_ge(s_eps, 1)

            def body(b):
                for h in range(HALVES):
                    t = b * HALVES + h
                    act.wait_ge(s_centred, t + 1)
                    if not is_first(b):
                        act.wait_ge(s_var, t - 1)
                    nc.scalar.activation(square[:, h, :], centred[:, h, :], ACT.Square).then_inc(s_square, 1)
                for h in range(HALVES):
                    t = b * HALVES + h
                    act.wait_ge(s_var, t + 1)
                    nc.scalar.activation(logv[:, h, :], p_var[:, h, :], ACT.Ln, bias=eps[:, 0:1]).then_inc(s_log, 1)
                    act.wait_ge(s_log, t + 1)
                    if not is_first(b):
                        act.wait_ge(s_out, t - 1)
                    nc.scalar.activation(rstd[:, h, :], logv[:, h, :], ACT.Exp, scale=-0.5).then_inc(s_rstd, 1)

            loop(act, B, body)

        @block.vector
        def _(dve):
            nc.vector.memset(eps[:, :], EPS).then_inc(s_eps, 1)

            def body(b):
                for h in range(HALVES):
                    t = b * HALVES + h
                    dve.wait_ge(s_mean, t + 1)
                    if not is_first(b):
                        dve.wait_ge(s_square, t - 1)
                        dve.wait_ge(s_out, t - 1)
                    nc.vector.tensor_tensor(centred[:, h, :], seq_cols(X, b, h * T, T), p_mean[:, h, :],
                                            ALU.subtract).then_inc(s_centred, 1)
                for h in range(HALVES):
                    t = b * HALVES + h
                    dve.wait_ge(s_rstd, t + 1)
                    dve.wait_ge(s_centred, t + 1)
                    nc.vector.tensor_tensor(seq_cols(X, b, h * T, T), centred[:, h, :], rstd[:, h, :],
                                            ALU.mult).then_inc(s_out, 1)

            loop(dve, B, body)


def ternary_ffn(nc, X, w):
    with ExitStack() as ctx:
        sb, ps, sem = alloc(nc, ctx)
        w1, w2 = sb("w1", [D, HID]), sb("w2", [D, HID])
        h1, h2, w3 = sb("h1", [128, KT, HID]), sb("h2", [128, KT, HID]), sb("w3", [128, KT, D])
        scales = sb("scales", [128, 4 * KT + 1])
        gate = sb("gate", [128, 2, KT, T])
        act0 = sb("act0", [128, 2, KT, T])
        p_hid = ps("p_hid", [128, 4, T])
        p_out = ps("p_out", [128, 2, T])
        s_w = sem("f_weights")
        s_g, s_u, s_gate, s_prod = sem("f_g"), sem("f_u"), sem("f_gate"), sem("f_prod")
        s_mm1, s_mm2, s_act1, s_act2, s_mm3, s_out = (sem("f_" + n) for n in ("mm1", "mm2", "act1", "act2", "mm3", "out"))
        block = ctx.enter_context(nc.Block())

        @block.sync
        def _(sp):
            sp.dma_start(w1[:, :], w["w1"][:, :]).then_inc(s_w, 16)
            sp.dma_start(w2[:, :], w["w2"][:, :]).then_inc(s_w, 16)
            sp.dma_start(h1[:, :, :], w["h1"].rearrange("(k p) n -> p k n", p=128)).then_inc(s_w, 16)
            sp.dma_start(h2[:, :, :], w["h2"].rearrange("(k p) n -> p k n", p=128)).then_inc(s_w, 16)
            sp.dma_start(w3[:, :, :], w["w3"].rearrange("(k p) n -> p k n", p=128)).then_inc(s_w, 16)
            sp.dma_start(scales[:, :], w["ffn_scales"][:, :]).then_inc(s_w, 16)

        N = 2 * KT

        @block.tensor
        def _(pe):
            pe.wait_ge(s_w, 96)

            def body(b):
                base = b * N
                for h in range(2):
                    x = seq_cols(X, b, h * T, T)
                    for m in range(KT):
                        i = h * KT + m
                        bank = 2 * (i % 2)
                        if i >= 2:
                            pe.wait_ge(s_gate, base + i - 1)
                            pe.wait_ge(s_prod, base + i - 1)
                        elif not is_first(b):
                            pe.wait_ge(s_act2, base)
                        nc.tensor.matmul(p_hid[:, bank, :], w1[:, m * 128:(m + 1) * 128], x,
                                         start=True, stop=True).then_inc(s_g, 1)
                        nc.tensor.matmul(p_hid[:, bank + 1, :], w2[:, m * 128:(m + 1) * 128], x,
                                         start=True, stop=True).then_inc(s_u, 1)
                for layer, (wt, src, s_src, s_mm, s_free) in enumerate((
                        (h1, act0, s_prod, s_mm1, s_act1), (h2, gate, s_act1, s_mm2, s_act2))):
                    for h in range(2):
                        pe.wait_ge(s_src, base + KT * (h + 1))
                        for m in range(KT):
                            i = h * KT + m
                            if i >= 4:
                                pe.wait_ge(s_free, base + i - 3)
                            elif layer == 0:
                                pe.wait_ge(s_gate, base + N)
                                pe.wait_ge(s_prod, base + N)
                            else:
                                pe.wait_ge(s_act1, base + N - 3 + i)
                            for k in range(KT):
                                mm = nc.tensor.matmul(p_hid[:, i % 4, :], wt[:, k, m * 128:(m + 1) * 128],
                                                      src[:, h, k, :], start=(k == 0), stop=(k == KT - 1))
                            mm.then_inc(s_mm, 1)
                for h in range(2):
                    pe.wait_ge(s_act2, base + KT * (h + 1))
                    if not is_first(b):
                        pe.wait_ge(s_out, 2 * b)
                    for k in range(KT):
                        mm = nc.tensor.matmul(p_out[:, h, :], w3[:, k, :], act0[:, h, k, :],
                                              start=(k == 0), stop=(k == KT - 1))
                    mm.then_inc(s_mm3, 1)

            loop(pe, B, body)

        @block.scalar
        def _(act):
            act.wait_ge(s_w, 96)

            def body(b):
                base = b * N
                for i in range(N):
                    h, m = i // KT, i % KT
                    act.wait_ge(s_g, base + i + 1)
                    if i == 0 and not is_first(b):
                        act.wait_ge(s_mm2, base)
                    nc.scalar.activation(gate[:, h, m, :], p_hid[:, 2 * (i % 2), :], ACT.Silu,
                                         scale=scales[:, m:m + 1]).then_inc(s_gate, 1)
                for i in range(N):
                    h, m = i // KT, i % KT
                    act.wait_ge(s_mm1, base + i + 1)
                    if i == 0:
                        act.wait_ge(s_prod, base + N)
                    nc.scalar.activation(gate[:, h, m, :], p_hid[:, i % 4, :], ACT.Gelu,
                                         scale=scales[:, 2 * KT + m:2 * KT + m + 1]).then_inc(s_act1, 1)
                for i in range(N):
                    h, m = i // KT, i % KT
                    act.wait_ge(s_mm2, base + i + 1)
                    if m == 0:
                        act.wait_ge(s_mm1, base + KT * (h + 1))
                    nc.scalar.activation(act0[:, h, m, :], p_hid[:, i % 4, :], ACT.Gelu,
                                         scale=scales[:, 3 * KT + m:3 * KT + m + 1]).then_inc(s_act2, 1)

            loop(act, B, body)

        @block.vector
        def _(dve):
            dve.wait_ge(s_w, 96)

            def body(b):
                base = b * N
                for i in range(N):
                    h, m = i // KT, i % KT
                    dve.wait_ge(s_u, base + i + 1)
                    dve.wait_ge(s_gate, base + i + 1)
                    if i == 0 and not is_first(b):
                        dve.wait_ge(s_mm3, 2 * b)
                    nc.vector.scalar_tensor_tensor(out=act0[:, h, m, :], in0=p_hid[:, 2 * (i % 2) + 1, :],
                                                   scalar=scales[:, KT + m:KT + m + 1], in1=gate[:, h, m, :],
                                                   op0=ALU.mult, op1=ALU.mult).then_inc(s_prod, 1)
                for h in range(2):
                    x = seq_cols(X, b, h * T, T)
                    dve.wait_ge(s_mm3, 2 * b + h + 1)
                    nc.vector.scalar_tensor_tensor(out=x, in0=p_out[:, h, :], scalar=scales[:, 4 * KT:4 * KT + 1],
                                                   in1=x, op0=ALU.mult, op1=ALU.add).then_inc(s_out, 1)

            loop(dve, B, body)


H = 4
DH = 32
CS = 32
NC_ = S // CS
CONV = 4
SHORT, LONG = 3, 31
BRANCHES = 4
GH = 128
GM = GH // 128
KB, Q, K, ATT, VB, INV = (DH * i for i in range(6))
REC = 6 * DH
HALF_B = 4


def delta_inputs(nc, X, V, L, w, scratch):
    chunks, recs = scratch["upper"], scratch["records"]
    with ExitStack() as ctx:
        sb, ps, sem = alloc(nc, ctx)
        wconv = sb("wconv", [D, 3, CONV, D])
        wproj = sb("wproj", [D, D])
        taps = sb("taps", [D, CONV, D])
        wbeta, headsum = sb("wbeta", [D, D]), sb("headsum", [D, D])
        ident, ltaps = sb("ident_c", [D, D]), sb("ltaps", [D, LONG])
        diag = sb("diag", [D, LONG, D])
        keep_lt, keep_le = sb("keep_lt", [D, CS]), sb("keep_le", [D, CS])
        tiny = sb("tiny", [D, 1])
        qs, ks, kn = sb("qs", [D, S]), sb("ks", [D, S]), sb("kn", [D, S])
        vs = sb("vs", [D, DH + S])
        beta, rq, rk = sb("beta", [D, S]), sb("rq", [D, S]), sb("rk", [D, S])
        kdiag = sb("kdiag", [D, NC_, H, CS])
        rec = sb("rec", [D, NC_, INV])
        upper = sb("upper", [D, NC_, CS])
        umat, rmat = sb("umat", [D, CS, CS]), sb("rmat", [D, CS, CS])
        prod = sb("prod", [D, (CS - 1) * (CS - 1)])
        lconv = sb("lconv", [D, S])
        p_z = ps("p_zc", [D, 2, T])
        p_att = ps("p_att", [D, 4, T])
        p_fir = ps("p_fir", [D, 2, T])
        s_w, s_raw, s_tap, s_ready = sem("c_weights"), sem("c_raw"), sem("c_tap"), sem("c_ready")
        s_z, s_zread, s_sq, s_rs = sem("c_z"), sem("c_zread"), sem("c_sq"), sem("c_rs")
        s_qn, s_kn, s_kb, s_vb, s_kt, s_kdiag = (sem("c_" + n) for n in ("qn", "kn", "kb", "vb", "kt", "kdiag"))
        s_att, s_masked, s_fir, s_lconv = (sem("c_" + n) for n in ("att", "masked", "fir", "lconv"))
        s_uout, s_uin, s_solve, s_rout, s_recout, s_vout, s_lout = (
            sem("c_" + n) for n in ("uout", "uin", "solve", "rout", "recout", "vout", "lout"))
        block = ctx.enter_context(nc.Block())
        SOLVE = 2 * (CS - 1)

        @block.sync
        def _(sp):
            loads = ((wbeta, w["b_proj"]), (headsum, w["headsum"]), (ident, w["ident"]), (ltaps, w["fir_long"]),
                     (keep_lt, w["keep_lt"]), (keep_le, w["keep_le"]))
            for dst, src in loads:
                sp.dma_start(dst[:, :], src[:, :]).then_inc(s_w, 16)
            sp.dma_start(rmat[:, :, :], w["eye32"].rearrange("p (j i) -> p j i", i=CS)).then_inc(s_w, 16)
            for p, n in enumerate("qkv"):
                if p:
                    sp.wait_ge(s_tap, CONV * p)
                sp.dma_start(wproj[:, :], w[n + "_proj"][:, :]).then_inc(s_raw, 16)
                sp.dma_start(taps[:, :, :], w[n + "_conv"].rearrange("p (j n) -> p j n", j=CONV)).then_inc(s_raw, 16)

            def results(b):
                sp.wait_ge(s_solve, SOLVE * (b + 1))
                for h in range(H):
                    dst = recs[:, h * CS:(h + 1) * CS, bass.ds(b * REC + INV, CS)]
                    sp.dma_start(dst, rmat[h * NC_:(h + 1) * NC_, :, :]).then_inc(s_rout, 16)
                sp.wait_ge(s_lconv, 2 * (b + 1))
                sp.dma_start(L[:, bass.ds(b * S, S)], lconv[:, :]).then_inc(s_lout, 16)

            def front(b):
                sp.wait_ge(s_zread, 12 * b + 6)
                sp.dma_start(V[:, bass.ds(b * ROW + PAD, S)], vs[:, DH:]).then_inc(s_vout, 16)
                sp.wait_ge(s_masked, 8 * (b + 1))
                for h in range(H):
                    sp.dma_start(chunks[h].rearrange("n j i -> j n i"),
                                 upper[h * CS:(h + 1) * CS, :, :]).then_inc(s_uout, 16)
                sp.wait_ge(s_vb, b + 1)
                sp.wait_ge(s_kt, b + 1)
                dst = recs[:, :, bass.ds(b * REC, INV)].rearrange("n p c -> p n c")
                sp.dma_start(dst, rec[:, :, :]).then_inc(s_recout, 16)

            def reload(b):
                sp.wait_ge(s_uout, 64 * (b + 1))
                sp.dma_start(umat[:, :, :], chunks.rearrange("h n j i -> (h n) j i")).then_inc(s_uin, 16)

            front(0)
            reload(0)
            with sp.Fori(1, B) as b:
                front(b)
                results(b - 1)
                reload(b)
            results(B - 1)
            for s, n in ((s_rout, 64 * B), (s_lout, 16 * B), (s_vout, 16 * B), (s_recout, 16 * B)):
                sp.wait_ge(s, n)

        @block.tensor
        def _(pe):
            pe.wait_ge(s_w, 112)
            pe.wait_ge(s_ready, 3 + LONG)
            pe.wait_ge(s_tap, 3 * CONV)

            def body(b):
                first = is_first(b)

                def bank_free(i):
                    if i >= 2 or not first:
                        pe.wait_ge(s_zread, 12 * b + i - 1)

                for i in range(6):
                    bank_free(i)
                    p, h = i // 2, i % 2
                    for j in range(CONV):
                        mm = nc.tensor.matmul(p_z[:, i % 2, :], wconv[:, p, j, :],
                                              seq_cols(X, b, h * T - (CONV - 1) + j, T),
                                              start=(j == 0), stop=(j == CONV - 1))
                    mm.then_inc(s_z, 1)
                for h in range(2):
                    bank_free(6 + h)
                    nc.tensor.matmul(p_z[:, h, :], wbeta[:, :], seq_cols(X, b, h * T, T),
                                     start=True, stop=True).then_inc(s_z, 1)
                for i in range(8, 12):
                    bank_free(i)
                    pe.wait_ge(s_sq, 2 * b + (i - 8) // 2 + 1)
                    src = rq if i < 10 else rk
                    nc.tensor.matmul(p_z[:, i % 2, :], headsum[:, :], src[:, (i % 2) * T:(i % 2 + 1) * T],
                                     start=True, stop=True).then_inc(s_z, 1)
                pe.wait_ge(s_kdiag, H * (b + 1))
                pe.wait_ge(s_kb, b + 1)
                pe.wait_ge(s_qn, b + 1)
                for g in range(4):
                    if not first:
                        pe.wait_ge(s_masked, 8 * b)
                    for c in range(8):
                        n = 8 * g + c
                        mm = nc.tensor.matmul(p_att[:, g, c * 64:(c + 1) * 64], kdiag[:, n, :, :],
                                              rec[:, n, KB:KB + 2 * DH], start=True, stop=True)
                    mm.then_inc(s_att, 1)
                for h in range(2):
                    if not first:
                        pe.wait_ge(s_lconv, 2 * (b - 1) + h + 1)
                    for j in range(LONG):
                        lo = DH + h * T - (LONG - 1) + j
                        mm = nc.tensor.matmul(p_fir[:, h, :], diag[:, j, :], vs[:, lo:lo + T],
                                              start=(j == 0), stop=(j == LONG - 1))
                    mm.then_inc(s_fir, 1)

            loop(pe, B, body)

        @block.scalar
        def _(act):
            def body(b):
                first = is_first(b)
                for i in range(6):
                    p, h = i // 2, i % 2
                    act.wait_ge(s_z, 12 * b + i + 1)
                    if not first and i == 0:
                        act.wait_ge(s_qn, b)
                        act.wait_ge(s_kn, b)
                        act.wait_ge(s_kdiag, H * b)
                    if not first and i == 4:
                        act.wait_ge(s_vb, b)
                        act.wait_ge(s_fir, 2 * b)
                        act.wait_ge(s_vout, 16 * b)
                    dst = (qs[:, h * T:(h + 1) * T], ks[:, h * T:(h + 1) * T], vs[:, DH + h * T:DH + (h + 1) * T])[p]
                    nc.scalar.activation(dst, p_z[:, h, :], ACT.Silu).then_inc(s_zread, 1)
                for h in range(2):
                    act.wait_ge(s_z, 12 * b + 7 + h)
                    if not first and h == 0:
                        act.wait_ge(s_kb, b)
                    nc.scalar.activation(beta[:, h * T:(h + 1) * T], p_z[:, h, :], ACT.Sigmoid).then_inc(s_zread, 1)
                act.wait_ge(s_zread, 12 * b + 4)
                nc.scalar.activation(rq[:, :], qs[:, :], ACT.Square).then_inc(s_sq, 1)
                nc.scalar.activation(rk[:, :], ks[:, :], ACT.Square).then_inc(s_sq, 1)
                for i in range(8, 12):
                    act.wait_ge(s_z, 12 * b + i + 1)
                    dst = (rq if i < 10 else rk)[:, (i % 2) * T:(i % 2 + 1) * T]
                    if i % 2 == 0:
                        act.wait_ge(s_z, 12 * b + i + 2)
                    nc.scalar.activation(dst, p_z[:, i % 2, :], ACT.Ln, bias=tiny[:, 0:1]).then_inc(s_zread, 1)
                act.wait_ge(s_zread, 12 * b + 12)
                nc.scalar.activation(rq[:, :], rq[:, :], ACT.Exp, scale=-0.5).then_inc(s_rs, 1)
                nc.scalar.activation(rk[:, :], rk[:, :], ACT.Exp, scale=-0.5).then_inc(s_rs, 1)
                for h in range(2):
                    act.wait_ge(s_fir, 2 * b + h + 1)
                    if not first and h == 0:
                        act.wait_ge(s_lout, 16 * b)
                    nc.scalar.copy(lconv[:, h * T:(h + 1) * T], p_fir[:, h, :]).then_inc(s_lconv, 1)

            loop(act, B, body)

        @block.gpsimd
        def _(pool):
            nc.gpsimd.memset(kdiag[:, :, :, :], 0.0).then_inc(s_ready, 1)
            nc.gpsimd.memset(vs[:, 0:DH], 0.0).then_inc(s_ready, 1)
            nc.gpsimd.memset(V[:, :].rearrange("p (b c) -> p b c", c=ROW)[:, :, 0:PAD], 0.0).then_inc(s_ready, 1)
            pool.wait_ge(s_w, 112)
            for j in range(LONG):
                nc.gpsimd.tensor_scalar(diag[:, j, :], ident[:, :], ltaps[:, j:j + 1], None, ALU.mult).then_inc(s_ready, 1)
            pool.wait_ge(s_ready, 1)

            def body(b):
                pool.wait_ge(s_rs, 2 * (b + 1))
                if not is_first(b):
                    pool.wait_ge(s_att, 4 * b)
                for h in range(H):
                    r = slice(h * DH, (h + 1) * DH)
                    split = lambda t: t[r, :].rearrange("p (n i) -> p n i", i=CS)
                    nc.gpsimd.tensor_tensor(kdiag[r, :, h, :], split(ks), split(rk), ALU.mult).then_inc(s_kdiag, 1)

            loop(pool, B, body)

        @block.vector
        def _(dve):
            nc.vector.memset(tiny[:, :], 1e-12)
            dve.wait_ge(s_w, 112)
            for p in range(3):
                dve.wait_ge(s_raw, 32 * (p + 1))
                for j in range(CONV):
                    nc.vector.tensor_tensor(wconv[:, p, j, :], wproj[:, :], taps[:, j, :], ALU.mult).then_inc(s_tap, 1)
            slot = lambda at: rec[:, :, at:at + DH]
            chunked = lambda t: t.rearrange("p (n i) -> p n i", i=CS)

            def front(b):
                first = is_first(b)
                dve.wait_ge(s_rs, 2 * (b + 1))
                if not first:
                    dve.wait_ge(s_recout, 16 * b)
                    dve.wait_ge(s_att, 4 * b)
                    dve.wait_ge(s_kt, b)
                nc.vector.tensor_tensor(kn[:, :], ks[:, :], rk[:, :], ALU.mult).then_inc(s_kn, 1)
                nc.vector.tensor_tensor(slot(Q), chunked(qs[:, :]), chunked(rq[:, :]), ALU.mult).then_inc(s_qn, 1)
                dve.wait_ge(s_kn, b + 1)
                dve.wait_ge(s_zread, 12 * b + 8)
                nc.vector.tensor_tensor(slot(KB), chunked(kn[:, :]), chunked(beta[:, :]), ALU.mult).then_inc(s_kb, 1)
                nc.vector.tensor_tensor(slot(VB), chunked(vs[:, DH:]), chunked(beta[:, :]), ALU.mult).then_inc(s_vb, 1)
                nc.vector.transpose(slot(K), chunked(kn[:, :])).then_inc(s_kt, 1)
                for g in range(4):
                    c = slice(8 * g, 8 * g + 8)
                    pa = p_att[:, g, :].rearrange("p (n c) -> p n c", c=64)
                    dve.wait_ge(s_att, 4 * b + g + 1)
                    if g == 0 and not first:
                        dve.wait_ge(s_uout, 64 * b)
                    nc.vector.tensor_tensor(upper[:, c, :], pa[:, :, 0:CS],
                                            keep_lt[:, :].unsqueeze(1).broadcast_to([D, 8, CS]), ALU.mult).then_inc(s_masked, 1)
                    nc.vector.tensor_tensor(rec[:, c, ATT:ATT + CS], pa[:, :, CS:2 * CS],
                                            keep_le[:, :].unsqueeze(1).broadcast_to([D, 8, CS]), ALU.mult).then_inc(s_masked, 1)

            def solve(b):
                dve.wait_ge(s_uin, 16 * (b + 1))
                if not is_first(b):
                    dve.wait_ge(s_rout, 64 * b)
                for step, j in enumerate(range(CS - 2, -1, -1)):
                    m = CS - 1 - j
                    p = prod[:, 0:m * m].rearrange("p (i l) -> p i l", l=m)
                    if step:
                        dve.wait_ge(s_solve, SOLVE * b + 2 * step)
                    nc.vector.tensor_tensor(p, umat[:, j, j + 1:CS].unsqueeze(1).broadcast_to([D, m, m]),
                                            rmat[:, j + 1:CS, j + 1:CS].rearrange("p l i -> p i l"),
                                            ALU.mult).then_inc(s_solve, 1)
                    dve.wait_ge(s_solve, SOLVE * b + 2 * step + 1)
                    nc.vector.tensor_reduce(rmat[:, j, j + 1:CS], p, AX.X, ALU.add, negate=True).then_inc(s_solve, 1)

            front(0)
            with dve.Fori(1, B) as b:
                solve(b - 1)
                front(b)
            solve(B - 1)


def delta_scan(nc, O, w, scratch):
    recs = scratch["records"]
    with ExitStack() as ctx:
        sb, ps, sem = alloc(nc, ctx)
        inp = sb("scan_in", [D, 2, B, REC])
        sdiag, rdiag, udiag = (sb(n, [D, B, H, DH]) for n in ("sdiag", "rdiag", "udiag"))
        strans, resid, qpart = sb("strans", [D, B, DH]), sb("resid", [D, B, CS]), sb("qpart", [D, B, CS])
        osum = sb("osum", [D, 2, B, CS])
        p_s = [ps(f"p_s{g}", [D, HALF_B, 2 * CS]) for g in range(2)]
        p_u = [ps(f"p_u{g}", [D, HALF_B, CS]) for g in range(2)]
        p_k = [ps(f"p_k{g}", [D, HALF_B, 2 * CS]) for g in range(2)]
        s_zero, s_in, s_out = sem("d_zero"), [sem("d_in0"), sem("d_in1")], [sem("d_out0"), sem("d_out1")]
        s_ms, s_resid, s_rdiag, s_mu, s_udiag, s_mk, s_state, s_sdiag, s_qpart, s_osum = (
            [sem(f"d_{n}{g}") for g in range(2)]
            for n in ("ms", "resid", "rdiag", "mu", "udiag", "mk", "state", "sdiag", "qpart", "osum"))
        block = ctx.enter_context(nc.Block())
        STEPS = NC_ // 2
        seqs = [slice(HALF_B * g, HALF_B * (g + 1)) for g in range(2)]

        def pairs(eng, body):
            body(0)
            with eng.Fori(1, STEPS) as i:
                body(i)

        @block.sync
        def _(sp):
            def body(i):
                for e in range(2):
                    n = 2 * i + e
                    if not is_first(i):
                        for g in range(2):
                            sp.wait_ge(s_mk[g], n - 1)
                            sp.wait_ge(s_resid[g], n - 1)
                    sp.dma_start(inp[:, e, :, :], recs[bass.ds(n, 1), :, :].rearrange("n p (b c) -> (n p) b c", c=REC)
                                 ).then_inc(s_in[e], 16)

            pairs(sp, body)

        @block.gpsimd
        def _(pool):
            for t in (sdiag, rdiag, udiag):
                nc.gpsimd.memset(t[:, :, :, :], 0.0).then_inc(s_zero, 1)
            nc.gpsimd.memset(strans[:, :, :], 0.0).then_inc(s_zero, 1)

            def body(i):
                for e in range(2):
                    n = 2 * i + e
                    for g in range(2):
                        pool.wait_ge(s_osum[g], n + 1)
                    pool.dma_start(O[:, bass.ds(n * CS * B, CS * B)],
                                   osum[:, e, :, :].rearrange("p b c -> p (b c)")).then_inc(s_out[e], 16)

            pairs(pool, body)
            for e in range(2):
                pool.wait_ge(s_out[e], 16 * STEPS)

        @block.tensor
        def _(pe):
            pe.wait_ge(s_zero, 4)

            def body(i):
                for e in range(2):
                    n = 2 * i + e
                    start = is_first(i) and e == 0
                    pe.wait_ge(s_in[e], 16 * (i + 1))
                    for g in range(2):
                        if not start:
                            pe.wait_ge(s_sdiag[g], n * H)
                            pe.wait_ge(s_qpart[g], n)
                        for b in range(HALF_B):
                            bb = HALF_B * g + b
                            mm = nc.tensor.matmul(p_s[g][:, b, :], sdiag[:, bb, :, :], inp[:, e, bb, KB:KB + 2 * DH],
                                                  start=True, stop=True)
                        mm.then_inc(s_ms[g], 1)
                    for g in range(2):
                        pe.wait_ge(s_rdiag[g], (n + 1) * H)
                        if not start:
                            pe.wait_ge(s_udiag[g], n * H)
                        for b in range(HALF_B):
                            bb = HALF_B * g + b
                            mm = nc.tensor.matmul(p_u[g][:, b, :], rdiag[:, bb, :, :], inp[:, e, bb, INV:INV + CS],
                                                  start=True, stop=True)
                        mm.then_inc(s_mu[g], 1)
                    for g in range(2):
                        pe.wait_ge(s_udiag[g], (n + 1) * H)
                        if not start:
                            pe.wait_ge(s_state[g], n)
                            pe.wait_ge(s_osum[g], n)
                        for b in range(HALF_B):
                            bb = HALF_B * g + b
                            mm = nc.tensor.matmul(p_k[g][:, b, :], udiag[:, bb, :, :], inp[:, e, bb, K:K + 2 * DH],
                                                  start=True, stop=True)
                        mm.then_inc(s_mk[g], 1)

            pairs(pe, body)

        @block.scalar
        def _(act):
            def body(i):
                for e in range(2):
                    n = 2 * i + e
                    start = is_first(i) and e == 0
                    for g in range(2):
                        act.wait_ge(s_resid[g], n + 1)
                        if not start:
                            act.wait_ge(s_osum[g], n)
                        nc.scalar.copy(qpart[:, seqs[g], :], p_s[g][:, :, CS:2 * CS]).then_inc(s_qpart[g], 1)

            pairs(act, body)

        @block.vector
        def _(dve):
            dve.wait_ge(s_zero, 4)

            def to_diagonal(dst, src, done, g):
                for h in range(H):
                    r = slice(h * DH, (h + 1) * DH)
                    nc.vector.transpose(dst[r, seqs[g], h, :], src(r)).then_inc(done[g], 1)

            def body(i):
                for e in range(2):
                    n = 2 * i + e
                    start = is_first(i) and e == 0
                    dve.wait_ge(s_in[e], 16 * (i + 1))
                    for g in range(2):
                        dve.wait_ge(s_ms[g], n + 1)
                        if not start:
                            dve.wait_ge(s_mu[g], n)
                        nc.vector.tensor_tensor(resid[:, seqs[g], :], inp[:, e, seqs[g], VB:VB + CS],
                                                p_s[g][:, :, 0:CS], ALU.subtract).then_inc(s_resid[g], 1)
                        dve.wait_ge(s_resid[g], n + 1)
                        to_diagonal(rdiag, lambda r: resid[r, seqs[g], :], s_rdiag, g)
                    for g in range(2):
                        dve.wait_ge(s_mu[g], n + 1)
                        if not start:
                            dve.wait_ge(s_mk[g], n)
                        to_diagonal(udiag, lambda r: p_u[g][r, :, :], s_udiag, g)
                    for g in range(2):
                        dve.wait_ge(s_mk[g], n + 1)
                        nc.vector.tensor_tensor(strans[:, seqs[g], :], strans[:, seqs[g], :], p_k[g][:, :, 0:DH],
                                                ALU.add).then_inc(s_state[g], 1)
                        dve.wait_ge(s_state[g], n + 1)
                        dve.wait_ge(s_ms[g], n + 1)
                        to_diagonal(sdiag, lambda r: strans[r, seqs[g], :], s_sdiag, g)
                        dve.wait_ge(s_qpart[g], n + 1)
                        if not is_first(i):
                            dve.wait_ge(s_out[e], 16 * i)
                        nc.vector.tensor_tensor(osum[:, e, seqs[g], :], qpart[:, seqs[g], :], p_k[g][:, :, CS:2 * CS],
                                                ALU.add).then_inc(s_osum[g], 1)

            pairs(dve, body)


def gate_mix(nc, X, V, L, O, w):
    with ExitStack() as ctx:
        sb, ps, sem = alloc(nc, ctx)
        w1 = sb("fg1", [128, BRANCHES, GH])
        w2 = sb("fg2", [128, GM, BRANCHES])
        b1, b2 = sb("fg1b", [128, GH // 128]), sb("fg2b", [128, BRANCHES])
        temp = sb("temp", [128, 4])
        headmean, wo, onorm = sb("headmean", [D, D]), sb("wo", [D, D]), sb("onorm", [D, 1])
        ident, staps, sdiag = sb("ident_g", [D, D]), sb("staps", [D, SHORT]), sb("sdiag_g", [D, SHORT, D])
        eps = sb("eps_g", [D, 1])
        otile, short = sb("otile", [D, 2, T]), sb("short", [D, 2, T])
        hid = sb("hid_g", [128, 2, GM, T])
        NS = T // 128
        lg = sb("lg", [128, 2, 4, NS * BRANCHES])
        small = sb("small", [128, 2, 4, NS])
        flo = sb("flo", [128, 2, NS])
        mix, part = sb("mix", [D, 2, T]), sb("part", [D, 2, BRANCHES, T])
        sq, rst = sb("sq_g", [D, 2, T]), sb("rst_g", [D, 2, T])
        p_a = ps("p_a", [D, 2, T])
        p_h = ps("p_h", [D, 2, T])
        p_w = ps("p_w", [D, 4, T])
        s_w, s_set, s_o = sem("g_weights"), sem("g_set"), [sem("g_o0"), sem("g_o1")]
        s_a, s_aread, s_h, s_hid, s_lg, s_soft, s_exp, s_pw, s_part, s_mix, s_sq, s_rst, s_norm, s_out = (
            sem("g_" + n) for n in ("a", "aread", "h", "hid", "lg", "soft", "exp", "pw", "part", "mix", "sq", "rst",
                                    "norm", "out"))
        block = ctx.enter_context(nc.Block())
        SOFT = 12

        @block.sync
        def _(sp):
            loads = ((w1[:, :, :], w["fg1"].rearrange("p (k n) -> p k n", k=BRANCHES)),
                     (w2[:, :, :], w["fg2"].rearrange("p (k n) -> p k n", n=BRANCHES)),
                     (b1[:, :], w["fg_b1"][:, :]), (b2[:, :], w["fg_b2"][:, :]), (temp[:, 0:1], w["logit_temp"][:, :]),
                     (headmean[:, :], w["headmean"][:, :]), (wo[:, :], w["o_proj"][:, :]), (onorm[:, :], w["o_norm"][:, :]),
                     (ident[:, :], w["ident"][:, :]), (staps[:, :], w["fir_short"][:, :]))
            for dst, src in loads:
                sp.dma_start(dst, src).then_inc(s_w, 16)
            osrc = O[:, :].rearrange("p (n b c) -> p b n c", b=B, c=CS)

            def body(b):
                for h in range(HALVES):
                    if not is_first(b):
                        sp.wait_ge(s_part, BRANCHES * (2 * b + h - 1))
                        sp.wait_ge(s_h, GM * (2 * b + h - 1))
                    src = O[:, :].rearrange("p (n c) -> p n c", c=B * CS)[:, h * (T // CS):(h + 1) * (T // CS), bass.ds(b * CS, CS)]
                    sp.dma_start(otile[:, h, :].rearrange("p (n c) -> p n c", c=CS), src).then_inc(s_o[h], 16)

            loop(sp, B, body)

        @block.tensor
        def _(pe):
            pe.wait_ge(s_w, 160)
            pe.wait_ge(s_set, 7)

            def gate(b, h):
                t = 2 * b + h
                if not is_first(b) or h:
                    pe.wait_ge(s_aread, 3 * t)
                for j in range(SHORT):
                    mm = nc.tensor.matmul(p_a[:, 0, :], sdiag[:, j, :], seq_cols(V, b, h * T - (SHORT - 1) + j, T),
                                          start=(j == 0), stop=(j == SHORT - 1))
                mm.then_inc(s_a, 1)
                pe.wait_ge(s_o[h], 16 * (b + 1))
                pe.wait_ge(s_aread, 3 * t + 1)
                if not is_first(b) or h:
                    pe.wait_ge(s_exp, t)
                srcs = (seq_cols(X, b, h * T, T), L[:, bass.ds(b * S + h * T, T)], otile[:, h, :], short[:, h, :])
                order = (0, 2, 3, 1)
                for m in range(GM):
                    for k in range(BRANCHES):
                        mm = nc.tensor.matmul(p_h[:, m, :], w1[:, order[k], m * 128:(m + 1) * 128], srcs[k],
                                              start=(k == 0), stop=(k == BRANCHES - 1))
                    mm.then_inc(s_h, 1)
                for s in range(NS):
                    pe.wait_ge(s_hid, GM * (t + 1))
                    for k in range(GM):
                        mm = nc.tensor.matmul(p_a[:, 1, s * BRANCHES:(s + 1) * BRANCHES],
                                              hid[:, h, k, s * 128:(s + 1) * 128], w2[:, k, :],
                                              start=(k == 0), stop=(k == GM - 1))
                mm.then_inc(s_lg, 1)

            def mix_(b, h):
                t = 2 * b + h
                pe.wait_ge(s_soft, SOFT * (t + 1))
                if not is_first(b) or h:
                    pe.wait_ge(s_part, BRANCHES * t)
                for g in range(BRANCHES):
                    for s in range(NS):
                        c = s * BRANCHES + g
                        mm = nc.tensor.matmul(p_w[:, g, s * 128:(s + 1) * 128],
                                              lg[:, h, 3, c:c + 1].broadcast_to([128, 128]), ident[:, :],
                                              start=True, stop=True)
                    mm.then_inc(s_pw, 1)
                pe.wait_ge(s_sq, t + 1)
                nc.tensor.matmul(p_a[:, 0, :], headmean[:, :], sq[:, h, :], start=True, stop=True).then_inc(s_a, 1)
                pe.wait_ge(s_norm, t + 1)
                pe.wait_ge(s_aread, 3 * t + 2)
                nc.tensor.matmul(p_a[:, 0, :], wo[:, :], mix[:, h, :], start=True, stop=True).then_inc(s_a, 1)

            def body(b):
                for h in range(HALVES):
                    gate(b, h)
                    mix_(b, h)

            loop(pe, B, body)

        @block.scalar
        def _(act):
            act.wait_ge(s_w, 160)
            act.wait_ge(s_set, 7)
            nc.scalar.activation(temp[:, 1:2], temp[:, 0:1], ACT.Abs).then_inc(s_set, 1)
            act.wait_ge(s_set, 8)
            nc.scalar.activation(temp[:, 1:2], temp[:, 1:2], ACT.Exp, scale=-1.0).then_inc(s_set, 1)
            act.wait_ge(s_set, 9)
            nc.scalar.activation(temp[:, 2:3], temp[:, 1:2], ACT.Ln, bias=1.0).then_inc(s_set, 1)
            act.wait_ge(s_set, 13)

            def body(b):
                for h in range(HALVES):
                    t = 2 * b + h
                    act.wait_ge(s_a, 3 * t + 1)
                    if not is_first(b):
                        act.wait_ge(s_part, BRANCHES * (t - 1))
                    nc.scalar.copy(short[:, h, :], p_a[:, 0, :]).then_inc(s_aread, 1)
                    for m in range(GM):
                        act.wait_ge(s_h, GM * t + m + 1)
                        nc.scalar.activation(hid[:, h, m, :], p_h[:, m, :], ACT.Gelu, bias=b1[:, m:m + 1]).then_inc(s_hid, 1)
                    act.wait_ge(s_soft, SOFT * t + 3)
                    nc.scalar.activation(lg[:, h, 1, :], lg[:, h, 0, :], ACT.Exp, scale=temp[:, 3:4]).then_inc(s_exp, 1)
                    act.wait_ge(s_mix, 3 * (t + 1))
                    nc.scalar.activation(sq[:, h, :], mix[:, h, :], ACT.Square).then_inc(s_sq, 1)
                    act.wait_ge(s_a, 3 * t + 2)
                    nc.scalar.activation(rst[:, h, :], p_a[:, 0, :], ACT.Ln, bias=eps[:, 0:1]).then_inc(s_aread, 1)
                    act.wait_ge(s_aread, 3 * t + 2)
                    nc.scalar.activation(rst[:, h, :], rst[:, h, :], ACT.Exp, scale=-0.5).then_inc(s_rst, 1)

            loop(act, B, body)

        @block.gpsimd
        def _(pool):
            def body(b):
                for h in range(HALVES):
                    t = 2 * b + h
                    pool.wait_ge(s_part, BRANCHES * t + 2)
                    if not is_first(b):
                        pool.wait_ge(s_a, 3 * (t - 1))
                    nc.gpsimd.tensor_tensor(mix[:, h, :], part[:, h, 0, :], part[:, h, 1, :], ALU.add).then_inc(s_mix, 1)
                    pool.wait_ge(s_part, BRANCHES * (t + 1))
                    nc.gpsimd.tensor_tensor(part[:, h, 2, :], part[:, h, 2, :], part[:, h, 3, :], ALU.add).then_inc(s_mix, 1)
                    pool.wait_ge(s_mix, 3 * t + 2)
                    nc.gpsimd.tensor_tensor(mix[:, h, :], mix[:, h, :], part[:, h, 2, :], ALU.add).then_inc(s_mix, 1)

            loop(pool, B, body)

        @block.vector
        def _(dve):
            nc.vector.memset(eps[:, :], EPS).then_inc(s_set, 1)
            dve.wait_ge(s_w, 160)
            for j in range(SHORT):
                nc.vector.tensor_scalar(sdiag[:, j, :], ident[:, :], staps[:, j:j + 1], None, ALU.mult).then_inc(s_set, 1)
            for k in range(1, BRANCHES):
                nc.vector.tensor_scalar(w1[:, k, :], w1[:, k, :], 1.0 / H, None, ALU.mult).then_inc(s_set, 1)
            dve.wait_ge(s_set, 10)
            nc.vector.tensor_scalar(temp[:, 1:2], temp[:, 0:1], 0.0, None, ALU.max).then_inc(s_set, 1)
            dve.wait_ge(s_set, 11)
            nc.vector.scalar_tensor_tensor(out=temp[:, 2:3], in0=temp[:, 1:2], scalar=1e-4, in1=temp[:, 2:3],
                                           op0=ALU.add, op1=ALU.add).then_inc(s_set, 1)
            dve.wait_ge(s_set, 12)
            nc.vector.reciprocal(temp[:, 3:4], temp[:, 2:3]).then_inc(s_set, 1)

            def body(b):
                for h in range(HALVES):
                    t = 2 * b + h
                    view = lambda k: lg[:, h, k, :].rearrange("p (s g) -> p s g", g=BRANCHES)
                    over = lambda x: x.unsqueeze(2).broadcast_to([128, NS, BRANCHES])
                    step = [0]

                    def chain(ins):
                        step[0] += 1
                        ins.then_inc(s_soft, 1)
                        dve.wait_ge(s_soft, SOFT * t + step[0])

                    dve.wait_ge(s_lg, t + 1)
                    logits = p_a[:, 1, 0:NS * BRANCHES].rearrange("p (s g) -> p s g", g=BRANCHES)
                    chain(nc.vector.tensor_tensor(view(0), logits, b2[:, :].unsqueeze(1).broadcast_to([128, NS, BRANCHES]), ALU.add))
                    chain(nc.vector.tensor_reduce(small[:, h, 0, :], view(0), AX.X, ALU.max))
                    chain(nc.vector.tensor_tensor(view(0), view(0), over(small[:, h, 0, :]), ALU.subtract))
                    dve.wait_ge(s_exp, t + 1)
                    chain(nc.vector.tensor_reduce(small[:, h, 1, :], view(1), AX.X, ALU.add))
                    chain(nc.vector.reciprocal(small[:, h, 2, :], small[:, h, 1, :]))
                    chain(nc.vector.tensor_tensor(view(2), view(1), over(small[:, h, 2, :]), ALU.mult))
                    chain(nc.vector.tensor_scalar(flo[:, h, :], view(2)[:, :, 3], 0.05, None, ALU.mult))
                    for g in range(2):
                        chain(nc.vector.tensor_tensor(view(2)[:, :, g], view(2)[:, :, g], flo[:, h, :], ALU.max))
                    chain(nc.vector.tensor_reduce(small[:, h, 1, :], view(2), AX.X, ALU.add))
                    chain(nc.vector.reciprocal(small[:, h, 3, :], small[:, h, 1, :]))
                    if not is_first(b):
                        dve.wait_ge(s_pw, BRANCHES * (t - 1))
                    chain(nc.vector.tensor_tensor(view(3), view(2), over(small[:, h, 3, :]), ALU.mult))
                    srcs = (short[:, h, :], L[:, bass.ds(b * S + h * T, T)], otile[:, h, :], seq_cols(V, b, h * T, T))
                    for g in range(BRANCHES):
                        dve.wait_ge(s_pw, BRANCHES * t + g + 1)
                        if g == 0 and not is_first(b):
                            dve.wait_ge(s_mix, 3 * (t - 1))
                        nc.vector.tensor_tensor(part[:, h, g, :], p_w[:, g, :], srcs[g], ALU.mult).then_inc(s_part, 1)
                    dve.wait_ge(s_rst, t + 1)
                    nc.vector.scalar_tensor_tensor(out=mix[:, h, :], in0=mix[:, h, :], scalar=onorm[:, 0:1],
                                                   in1=rst[:, h, :], op0=ALU.mult, op1=ALU.mult).then_inc(s_norm, 1)
                    x = seq_cols(X, b, h * T, T)
                    dve.wait_ge(s_a, 3 * (t + 1))
                    nc.vector.tensor_tensor(x, x, p_a[:, 0, :], ALU.add).then_inc(s_aread, 1)

            loop(dve, B, body)


NE = 32
FI = 256
FK = FI // 128
NT = B * S // 128
TPB = S // 128
SLOTS = NT + NE


def shared_and_logits(nc, X, XT, Y, LG, w, scratch):
    with ExitStack() as ctx:
        sb, ps, sem = alloc(nc, ctx)
        gate_w = sb("gate_w", [D, NE])
        wg, wu, wd = sb("swg", [D, FI]), sb("swu", [D, FI]), sb("swd", [128, FK, D])
        ident = sb("ident_m", [D, D])
        zeros = sb("zeros", [128, 8 * D])
        xs = sb("xs", [D, S])
        sg, hs = sb("sg", [128, 2, FK, T]), sb("hs", [128, 2, FK, T])
        p_l = ps("p_l", [128, TPB, NE])
        p_t = ps("p_t", [128, TPB, D])
        p_g, p_u = ps("p_g", [128, FK, T]), ps("p_u2", [128, FK, T])
        p_d = ps("p_d", [128, T // 128, D])
        s_w, s_zero, s_clear = sem("m_weights"), sem("m_zero"), sem("m_clear")
        s_xs, s_l, s_t, s_lg, s_xt, s_g, s_u, s_sg, s_hs, s_d, s_y = (
            sem("m_" + n) for n in ("xs", "l", "t", "lg", "xt", "g", "u", "sg", "hs", "d", "y"))
        block = ctx.enter_context(nc.Block())

        @block.sync
        def _(sp):
            loads = ((gate_w[:, :], w["gate_w"][:, :]), (wg[:, :], w["sg"][:, :]), (wu[:, :], w["su"][:, :]),
                     (wd[:, :, :], w["sd"].rearrange("(k p) n -> p k n", p=128)), (ident[:, :], w["ident"][:, :]))
            for dst, src in loads:
                sp.dma_start(dst, src).then_inc(s_w, 16)
            sp.wait_ge(s_zero, 1)
            for i in range(SLOTS // 8):
                dst = scratch["slots"][i * 1024:(i + 1) * 1024, :].rearrange("(p r) d -> p (r d)", p=128)
                sp.dma_start(dst, zeros[:, :]).then_inc(s_clear, 16)
            sp.wait_ge(s_clear, 16 * (SLOTS // 8))

        @block.gpsimd
        def _(pool):
            nc.gpsimd.memset(zeros[:, :], 0.0).then_inc(s_zero, 1)

        @block.tensor
        def _(pe):
            pe.wait_ge(s_w, 80)

            def body(b):
                first = is_first(b)
                pe.wait_ge(s_xs, b + 1)
                if not first:
                    pe.wait_ge(s_lg, b)
                    pe.wait_ge(s_xt, b)
                for s in range(TPB):
                    mm = nc.tensor.matmul(p_l[:, s, :], xs[:, s * 128:(s + 1) * 128], gate_w[:, :], start=True, stop=True)
                mm.then_inc(s_l, 1)
                for s in range(TPB):
                    mm = nc.tensor.transpose(p_t[:, s, :], xs[:, s * 128:(s + 1) * 128], ident[:, :])
                mm.then_inc(s_t, 1)
                for h in range(2):
                    for k in range(FK):
                        i = FK * (2 * b + h) + k
                        if not first or h:
                            pe.wait_ge(s_sg, i - 1)
                            pe.wait_ge(s_hs, i - 1)
                        x = xs[:, h * T:(h + 1) * T]
                        nc.tensor.matmul(p_g[:, k, :], wg[:, k * 128:(k + 1) * 128], x, start=True, stop=True).then_inc(s_g, 1)
                        nc.tensor.matmul(p_u[:, k, :], wu[:, k * 128:(k + 1) * 128], x, start=True, stop=True).then_inc(s_u, 1)
                for h in range(2):
                    t = 2 * b + h
                    pe.wait_ge(s_hs, FK * (t + 1))
                    if not first or h:
                        pe.wait_ge(s_y, t)
                    for s in range(T // 128):
                        for k in range(FK):
                            mm = nc.tensor.matmul(p_d[:, s, :], hs[:, h, k, s * 128:(s + 1) * 128], wd[:, k, :],
                                                  start=(k == 0), stop=(k == FK - 1))
                    mm.then_inc(s_d, 1)

            loop(pe, B, body)

        @block.scalar
        def _(act):
            def body(b):
                for h in range(2):
                    for k in range(FK):
                        i = FK * (2 * b + h) + k
                        act.wait_ge(s_g, i + 1)
                        if not is_first(b):
                            act.wait_ge(s_hs, i - 3)
                        nc.scalar.activation(sg[:, h, k, :], p_g[:, k, :], ACT.Silu).then_inc(s_sg, 1)

            loop(act, B, body)

        @block.vector
        def _(dve):
            def body(b):
                first = is_first(b)
                if not first:
                    dve.wait_ge(s_t, b)
                    dve.wait_ge(s_g, 4 * b)
                    dve.wait_ge(s_u, 4 * b)
                nc.vector.tensor_scalar(xs[:, :], seq_cols(X, b, 0, S), 1.0, None, ALU.mult).then_inc(s_xs, 1)
                dve.wait_ge(s_l, b + 1)
                nc.vector.tensor_scalar(LG[:, bass.ds(b * TPB, TPB), :], p_l[:, :, :], 1.0, None, ALU.mult).then_inc(s_lg, 1)
                dve.wait_ge(s_t, b + 1)
                nc.vector.tensor_scalar(XT[:, bass.ds(b * TPB, TPB), :], p_t[:, :, :], 1.0, None, ALU.mult).then_inc(s_xt, 1)
                for h in range(2):
                    for k in range(FK):
                        i = FK * (2 * b + h) + k
                        dve.wait_ge(s_sg, i + 1)
                        dve.wait_ge(s_u, i + 1)
                        if not first:
                            dve.wait_ge(s_d, 2 * b + h - 1)
                        nc.vector.tensor_tensor(hs[:, h, k, :], sg[:, h, k, :], p_u[:, k, :], ALU.mult).then_inc(s_hs, 1)
                dve.wait_ge(s_xt, b + 1)
                for h in range(2):
                    dve.wait_ge(s_d, 2 * b + h + 1)
                    at = bass.ds(b * TPB + h * (T // 128), T // 128)
                    nc.vector.tensor_tensor(Y[:, at, :], XT[:, at, :], p_d[:, :, :], ALU.add).then_inc(s_y, 1)

            loop(dve, B, body)


def route(nc, XT, LG, POS, w, scratch, TE):
    with ExitStack() as ctx:
        sb, ps, sem = alloc(nc, ctx)
        N = NT * NE
        down = sb("down", [128, NE])
        before, ones = sb("before", [128, 128], BF16), sb("ones_b", [128, 128], BF16)
        restart = sb("restart", [128, NE, NT])
        top, score = sb("top", [128, NT]), sb("score", [128, NT])
        cand, oneh = sb("cand", [128, NT, NE]), sb("oneh", [128, NT, NE])
        onehb = sb("onehb", [128, NT, NE], BF16)
        best = sb("best", [128, NT])
        count, prefix = sb("count", [128, NE, NT]), sb("prefix", [128, NE, NT])
        tot, toti = sb("tot", [128, NE]), sb("toti", [128, NE], I32)
        padded, ends, begins, onef = (sb(n, [128, NE]) for n in ("padded", "ends", "begins", "onef"))
        posf = sb("posf", [128, NT])
        starts, cmp, tef = sb("starts", [1, SLOTS]), sb("cmp", [1, SLOTS, NE]), sb("tef", [1, SLOTS])
        p_r, p_c = ps("p_r", [128, NT, NE]), ps("p_c2", [128, NT, NE])
        s_w, s_one, s_r, s_c, s_score, s_d, s_scaled, s_sent = (
            sem("r_" + n) for n in ("weights", "onehot", "rank", "count", "score", "dve", "scaled", "sent"))
        block = ctx.enter_context(nc.Block())
        bc = lambda x: x.unsqueeze(2).broadcast_to([128, NT, NE])
        rows = lambda x: x.unsqueeze(1).broadcast_to([128, NT, NE])
        TOP, SLOT = 1, 100

        @block.sync
        def _(sp):
            loads = ((down[:, :], w["down"][:, :]), (before[:, :].bitcast(U16), w["before"][:, :]), (ones[:, :].bitcast(U16), w["ones"][:, :]),
                     (restart[:, :, :], w["restart"].rearrange("p (e t) -> p e t", t=NT)), (starts[:, :], w["starts"][:, :]))
            for dst, src in loads:
                sp.dma_start(dst, src).then_inc(s_w, 16)

        @block.tensor
        def _(pe):
            pe.wait_ge(s_one, 1)
            flat = lambda t: t[:, :, :].rearrange("p t e -> p (t e)")
            for q in range(N // T):
                c = slice(q * T, (q + 1) * T)
                mm = nc.tensor.matmul(flat(p_c)[:, c], ones[:, :], flat(onehb)[:, c], start=True, stop=True)
            mm.then_inc(s_c, 1)
            for q in range(N // T):
                c = slice(q * T, (q + 1) * T)
                mm = nc.tensor.matmul(flat(p_r)[:, c], before[:, :], flat(onehb)[:, c], start=True, stop=True)
            mm.then_inc(s_r, 1)

        @block.scalar
        def _(act):
            act.wait_ge(s_d, 1)
            nc.scalar.activation(score[:, :], top[:, :], ACT.Sigmoid).then_inc(s_score, 1)

        @block.vector
        def _(dve):
            count_ = [0]

            def chain(ins):
                count_[0] += 1
                ins.then_inc(s_d, 1)
                dve.wait_ge(s_d, count_[0])

            dve.wait_ge(s_w, 80)
            chain(nc.vector.tensor_reduce(top[:, :], LG[:, :, :], AX.X, ALU.max))
            chain(nc.vector.tensor_tensor(cand[:, :, :], LG[:, :, :], bc(top[:, :]), ALU.is_equal))
            chain(nc.vector.tensor_tensor(cand[:, :, :], cand[:, :, :], rows(down[:, :]), ALU.mult))
            chain(nc.vector.tensor_reduce(best[:, :], cand[:, :, :], AX.X, ALU.max))
            chain(nc.vector.tensor_tensor(oneh[:, :, :], bc(best[:, :]), rows(down[:, :]), ALU.is_equal))
            nc.vector.tensor_copy(onehb[:, :, :], oneh[:, :, :]).then_inc(s_one, 1)
            chain(nc.vector.memset(onef[:, :], 1.0))
            dve.wait_ge(s_c, 1)
            chain(nc.vector.tensor_copy(count[:, :, :], p_c[:, :, :].rearrange("p t e -> p e t")))
            flat = lambda t: t[:, :, :].rearrange("p e t -> p (e t)")
            chain(nc.vector.tensor_tensor_scan(flat(prefix), flat(restart), flat(count), 0.0, ALU.mult, ALU.add))
            chain(nc.vector.tensor_scalar(tot[:, :], prefix[:, :, NT - 1], 127.0, None, ALU.add))
            chain(nc.vector.tensor_copy(toti[:, :], tot[:, :]))
            chain(nc.vector.tensor_scalar(toti[:, :], toti[:, :], 7, 7, ALU.arith_shift_right, ALU.logical_shift_left))
            chain(nc.vector.tensor_copy(padded[:, :], toti[:, :]))
            chain(nc.vector.tensor_tensor_scan(ends[:, :], onef[:, :], padded[:, :], 0.0, ALU.mult, ALU.add))
            chain(nc.vector.tensor_tensor(begins[:, :], ends[:, :], padded[:, :], ALU.subtract))
            chain(nc.vector.tensor_tensor(prefix[:, :, :], prefix[:, :, :], count[:, :, :], ALU.subtract))
            chain(nc.vector.tensor_tensor(prefix[:, :, :], prefix[:, :, :],
                                          begins[:, :].unsqueeze(2).broadcast_to([128, NE, NT]), ALU.add))
            dve.wait_ge(s_r, 1)
            chain(nc.vector.tensor_tensor(cand[:, :, :], p_r[:, :, :], prefix[:, :, :].rearrange("p e t -> p t e"), ALU.add))
            chain(nc.vector.tensor_tensor(cand[:, :, :], cand[:, :, :], oneh[:, :, :], ALU.mult))
            chain(nc.vector.tensor_reduce(posf[:, :], cand[:, :, :], AX.X, ALU.add))
            chain(nc.vector.tensor_copy(POS[:, :], posf[:, :]))
            chain(nc.vector.tensor_tensor(cmp[:, :, :], ends[0:1, :].unsqueeze(1).broadcast_to([1, SLOTS, NE]),
                                          starts[:, :].unsqueeze(2).broadcast_to([1, SLOTS, NE]), ALU.is_le))
            chain(nc.vector.tensor_reduce(tef[:, :], cmp[:, :, :], AX.X, ALU.add))
            chain(nc.vector.tensor_scalar(tef[:, :], tef[:, :], float(NE - 1), None, ALU.min))
            chain(nc.vector.tensor_copy(TE[:, :], tef[:, :]))
            dve.wait_ge(s_score, 1)
            for q in range(4):
                c = slice(q * NT // 4, (q + 1) * NT // 4)
                nc.vector.tensor_tensor(XT[:, c, :], XT[:, c, :],
                                        score[:, c].unsqueeze(2).broadcast_to([128, NT // 4, D]), ALU.mult).then_inc(s_scaled, 1)

        @block.gpsimd
        def _(pool):
            for t in range(NT):
                if t % (NT // 4) == 0:
                    pool.wait_ge(s_scaled, t // (NT // 4) + 1)
                pool.indirect_dma_start(out=scratch["slots"][:, :],
                                        out_offset=bass.IndirectOffsetOnAxis(ap=POS[:, t:t + 1], axis=0),
                                        in_=XT[:, t, :], in_offset=None).then_inc(s_sent, 16)
            pool.wait_ge(s_sent, 16 * NT)


def experts(nc, w, scratch, TE):
    with ExitStack() as ctx:
        sb, ps, sem = alloc(nc, ctx)
        WE = 2 * FI + FK * D
        wts = sb("wts", [128, 2, WE])
        xin, xt = sb("xin", [128, 2, D]), sb("xt_e", [D, 2, 128])
        sg, hs, ys = sb("sg_e", [128, 2, FK, 128]), sb("hs_e", [128, 2, FK, 128]), sb("ys", [128, 2, D])
        ident = sb("ident_e", [D, D])
        p_t = [ps(f"p_te{i}", [128, T]) for i in range(2)]
        p_gu = [ps(f"p_gu{i}", [128, 2 * FK, 128]) for i in range(2)]
        p_y = [ps(f"p_ye{i}", [128, T]) for i in range(2)]
        s_id = sem("e_ident")
        s_w, s_x, s_out = ([sem(f"e_{n}{i}") for i in range(2)] for n in ("w", "x", "out"))
        s_t, s_xt, s_gu, s_sg, s_hs, s_y, s_ys = (sem("e_" + n) for n in ("t", "xt", "gu", "sg", "hs", "y", "ys"))
        block = ctx.enter_context(nc.Block())

        def pairs(eng, body):
            body(0)
            with eng.Fori(1, SLOTS // 2) as i:
                body(i)

        @block.sync
        def _(sp):
            sp.dma_start(ident[:, :], w["ident"][:, :]).then_inc(s_id, 16)

            def body(i):
                for e in range(2):
                    m = 2 * i + e
                    number = sp.value_load(TE[0:1, m:m + 1] if isinstance(m, int) else TE[0:1, bass.ds(m, 1)],
                                           min_val=0, max_val=NE - 1)
                    if not is_first(i):
                        sp.wait_ge(s_y, m - 1)
                    sp.dma_start(wts[:, e, :], w["experts"][bass.ds(number, 1), :, :].rearrange("e p c -> (e p) c")
                                 ).then_inc(s_w[e], 16)

            pairs(sp, body)

        @block.gpsimd
        def _(pool):
            def body(i):
                for e in range(2):
                    m = 2 * i + e
                    if not is_first(i):
                        pool.wait_ge(s_t, m - 1)
                    pool.dma_start(xin[:, e, :], scratch["slots"][bass.ds(m * 128, 128), :]).then_inc(s_x[e], 16)

            pairs(pool, body)

        @block.tensor
        def _(pe):
            pe.wait_ge(s_id, 16)

            def turn(m, i, e, start):
                pe.wait_ge(s_x[e], 16 * (i + 1))
                if not start:
                    pe.wait_ge(s_xt, m - 1)
                nc.tensor.transpose(p_t[e][:, 0:128], xin[:, e, :], ident[:, :]).then_inc(s_t, 1)

            def body(i):
                for e in range(2):
                    turn(2 * i + e, i, e, is_first(i))
                for e in range(2):
                    m = 2 * i + e
                    pe.wait_ge(s_xt, m + 1)
                    pe.wait_ge(s_w[e], 16 * (i + 1))
                    if not is_first(i):
                        pe.wait_ge(s_sg, m - 1)
                        pe.wait_ge(s_hs, m - 1)
                    for k in range(2 * FK):
                        mm = nc.tensor.matmul(p_gu[e][:, k, :], wts[:, e, k * 128:(k + 1) * 128], xt[:, e, :],
                                              start=True, stop=True)
                    mm.then_inc(s_gu, 1)
                for e in range(2):
                    m = 2 * i + e
                    pe.wait_ge(s_hs, m + 1)
                    if not is_first(i):
                        pe.wait_ge(s_ys, m - 1)
                    for k in range(FK):
                        mm = nc.tensor.matmul(p_y[e][:, 0:D], hs[:, e, k, :],
                                              wts[:, e, 2 * FI + k * D:2 * FI + (k + 1) * D],
                                              start=(k == 0), stop=(k == FK - 1))
                    mm.then_inc(s_y, 1)

            pairs(pe, body)

        @block.scalar
        def _(act):
            def body(i):
                for e in range(2):
                    m = 2 * i + e
                    act.wait_ge(s_gu, m + 1)
                    if not is_first(i):
                        act.wait_ge(s_hs, m - 1)
                    nc.scalar.activation(sg[:, e, :, :], p_gu[e][:, 0:FK, :], ACT.Silu).then_inc(s_sg, 1)
                for e in range(2):
                    m = 2 * i + e
                    act.wait_ge(s_ys, m + 1)
                    act.dma_start(scratch["results"][bass.ds(m * 128, 128), :], ys[:, e, :]).then_inc(s_out[e], 16)

            pairs(act, body)
            for e in range(2):
                act.wait_ge(s_out[e], 16 * (SLOTS // 2))

        @block.vector
        def _(dve):
            def body(i):
                for e in range(2):
                    m = 2 * i + e
                    dve.wait_ge(s_t, m + 1)
                    if not is_first(i):
                        dve.wait_ge(s_gu, m - 1)
                    nc.vector.tensor_copy(xt[:, e, :], p_t[e][:, 0:128]).then_inc(s_xt, 1)
                for e in range(2):
                    m = 2 * i + e
                    dve.wait_ge(s_sg, m + 1)
                    if not is_first(i):
                        dve.wait_ge(s_y, m - 1)
                    nc.vector.tensor_tensor(hs[:, e, :, :], sg[:, e, :, :], p_gu[e][:, FK:2 * FK, :],
                                            ALU.mult).then_inc(s_hs, 1)
                for e in range(2):
                    m = 2 * i + e
                    dve.wait_ge(s_y, m + 1)
                    if not is_first(i):
                        dve.wait_ge(s_out[e], 16 * i)
                    nc.vector.tensor_copy(ys[:, e, :], p_y[e][:, 0:D]).then_inc(s_ys, 1)

            pairs(dve, body)


def combine(nc, Y, POS, out, scratch):
    with ExitStack() as ctx:
        sb, _, sem = alloc(nc, ctx)
        G = sb("G", [128, NT, D])
        eps = sb("eps_o", [128, 1])
        sums, var, rstd = sb("sums", [128, 2, TPB]), sb("var", [128, 2, TPB]), sb("rstd_o", [128, 2, TPB])
        cen, sq = sb("cen", [128, 2, TPB, D]), sb("sq_o", [128, 2, TPB, D])
        s_g, s_eps, s_add, s_sum, s_cen, s_sq, s_var, s_ln, s_rstd, s_done = (
            sem("z_" + n) for n in ("gathered", "eps", "add", "sum", "cen", "sq", "var", "ln", "rstd", "done"))
        s_out = [sem("z_out0"), sem("z_out1")]
        block = ctx.enter_context(nc.Block())
        dst = out.rearrange("(b t p) d -> b p t d", t=TPB, p=128)
        over = lambda x: x.unsqueeze(2).broadcast_to([128, TPB, D])

        @block.gpsimd
        def _(pool):
            for t in range(NT):
                pool.indirect_dma_start(out=G[:, t, :], out_offset=None, in_=scratch["results"][:, :],
                                        in_offset=bass.IndirectOffsetOnAxis(ap=POS[:, t:t + 1], axis=0)).then_inc(s_g, 16)
                if t % TPB == TPB - 1:
                    pool.wait_ge(s_g, 16 * (t + 1))

        @block.sync
        def _(sp):
            for b in range(B):
                sp.wait_ge(s_done, b + 1)
                sp.dma_start(dst[b], cen[:, b % 2, :, :]).then_inc(s_out[b % 2], 16)
            for e in range(2):
                sp.wait_ge(s_out[e], 16 * B // 2)

        @block.scalar
        def _(act):
            act.wait_ge(s_eps, 1)
            for b in range(B):
                e = b % 2
                act.wait_ge(s_cen, b + 1)
                if b >= 2:
                    act.wait_ge(s_var, b - 1)
                nc.scalar.activation(sq[:, e, :, :], cen[:, e, :, :], ACT.Square).then_inc(s_sq, 1)
                act.wait_ge(s_var, b + 1)
                nc.scalar.activation(var[:, e, :], var[:, e, :], ACT.Ln, bias=eps[:, 0:1], scale=1.0 / D).then_inc(s_ln, 1)
                act.wait_ge(s_ln, b + 1)
                if b >= 2:
                    act.wait_ge(s_done, b - 1)
                nc.scalar.activation(rstd[:, e, :], var[:, e, :], ACT.Exp, scale=-0.5).then_inc(s_rstd, 1)

        @block.vector
        def _(dve):
            nc.vector.memset(eps[:, :], EPS).then_inc(s_eps, 1)

            def centre(b):
                e = b % 2
                c = slice(b * TPB, (b + 1) * TPB)
                dve.wait_ge(s_g, 16 * TPB * (b + 1))
                nc.vector.tensor_tensor(G[:, c, :], G[:, c, :], Y[:, c, :], ALU.add).then_inc(s_add, 1)
                dve.wait_ge(s_add, b + 1)
                nc.vector.tensor_reduce(sums[:, e, :], G[:, c, :], AX.X, ALU.add).then_inc(s_sum, 1)
                dve.wait_ge(s_sum, 2 * b + 1)
                nc.vector.tensor_scalar(sums[:, e, :], sums[:, e, :], 1.0 / D, None, ALU.mult).then_inc(s_sum, 1)
                dve.wait_ge(s_sum, 2 * b + 2)
                if b >= 2:
                    dve.wait_ge(s_out[e], 16 * (b // 2))
                nc.vector.tensor_tensor(cen[:, e, :, :], G[:, c, :], over(sums[:, e, :]), ALU.subtract).then_inc(s_cen, 1)

            def scale(b):
                e = b % 2
                dve.wait_ge(s_sq, b + 1)
                nc.vector.tensor_reduce(var[:, e, :], sq[:, e, :, :], AX.X, ALU.add).then_inc(s_var, 1)
                dve.wait_ge(s_rstd, b + 1)
                nc.vector.tensor_tensor(cen[:, e, :, :], cen[:, e, :, :], over(rstd[:, e, :]), ALU.mult).then_inc(s_done, 1)

            for b in range(B):
                centre(b)
                if b:
                    scale(b - 1)
            scale(B - 1)


def clear_semaphores(nc):
    nc.all_engine_barrier()
    nc.gpsimd.sem_clear(range(min(nc.free_semaphores), max(nc.free_semaphores) + 1))
    nc.all_engine_barrier()


def build(nc, w, out, stages):
    with ExitStack() as ctx:
        X = ctx.enter_context(nc.sbuf_tensor("X", [D, B * ROW], F32))
        with ExitStack() as c1:
            sb, _, _ = alloc(nc, c1)
            dt, dtx, parts = sb("dt", [D, B * S]), sb("dtx", [D, B * S]), sb("parts", [96, B * S], BF16)
            scan_inputs(nc, X, dt, dtx, parts, w)
            selective_scan(nc, X, dt, dtx, parts, w)
        layer_norm(nc, X, w, "n1")
        if stages >= 2:
            ternary_ffn(nc, X, w)
            layer_norm(nc, X, w, "n2")
        if stages >= 3:
            scratch = {
                "upper": nc.dram_tensor("upper_scratch", (H, NC_, CS, CS), F32, kind="Internal").ap(),
                "records": nc.dram_tensor("record_scratch", (NC_, D, B * REC), F32, kind="Internal").ap(),
            }
            with ExitStack() as c3:
                sb, _, _ = alloc(nc, c3)
                V, L = sb("V", [D, B * ROW]), sb("L", [D, B * S])
                delta_inputs(nc, X, V, L, w, scratch)
                with ExitStack() as c4:
                    O = c4.enter_context(nc.sbuf_tensor("O", [D, B * S], F32))
                    delta_scan(nc, O, w, scratch)
                    gate_mix(nc, X, V, L, O, w)
            layer_norm(nc, X, w, "n3")
        clear_semaphores(nc)
        scratch["slots"] = nc.dram_tensor("slot_scratch", (SLOTS * 128, D), F32, kind="Internal").ap()
        scratch["results"] = nc.dram_tensor("result_scratch", (SLOTS * 128, D), F32, kind="Internal").ap()
        with ExitStack() as c5:
            sb, _, _ = alloc(nc, c5)
            Y = sb("Y", [128, NT, D])
            POS, TE = sb("POS", [128, NT], U32), sb("TE", [1, SLOTS], I32)
            with ExitStack() as c6:
                sb, _, _ = alloc(nc, c6)
                XT, LG = sb("XT", [128, NT, D]), sb("LG", [128, NT, NE])
                shared_and_logits(nc, X, XT, Y, LG, w, scratch)
                route(nc, XT, LG, POS, w, scratch, TE)
            experts(nc, w, scratch, TE)
            combine(nc, Y, POS, out, scratch)


STAGES = 3


def bf16_ones(where):
    return np.where(where, 0x3F80, 0).astype(np.uint16)


def lay_out(inputs):
    g = {k: np.ascontiguousarray(v) for k, v in inputs.items()}
    col = lambda v: np.ascontiguousarray(v.reshape(-1, 128).T)
    T_ = lambda v: np.ascontiguousarray(v.T)
    a = {}
    a["x"] = T_(g["L0_attn_x"].reshape(B * S, D))
    wx = g["L0_attn_W_xproj"]
    a["bc"] = np.ascontiguousarray(np.concatenate([wx[:, :32]] * 3, axis=1))
    a["low"] = np.ascontiguousarray(wx[:, 32:])
    a["dt"] = g["L0_attn_W_dt"]
    a["b_dt"] = col(g["L0_attn_b_dt"])
    a["A_log"] = T_(g["L0_attn_A_log"])
    for n in ("w1", "w2", "h1", "h2", "w3"):
        a[n] = T_(g[f"L0_ffn_{n}_w"])
    a["ffn_scales"] = np.ascontiguousarray(np.concatenate([col(g[f"L0_ffn_{n}_s"]) for n in ("w1", "w2", "h1", "h2", "w3")], axis=1))
    rep = lambda v, n=128: np.ascontiguousarray(np.broadcast_to(v.reshape(1, -1), (n, v.size)))
    for n in "qkv":
        a[n + "_proj"] = T_(g[f"L1_attn_{n}_proj_w"])
        a[n + "_conv"] = rep(g[f"L1_attn_{n}_conv_w"].T)
    a["b_proj"] = np.ascontiguousarray(np.repeat(g["L1_attn_b_proj_w"].T, DH, axis=1))
    a["fir_long"] = np.ascontiguousarray(g["L1_attn_fir_long_w"].reshape(D, LONG))
    a["fir_short"] = np.ascontiguousarray(g["L1_attn_fir_short_w"].reshape(D, SHORT))
    fg = g["L1_attn_fg_w1"].T
    a["fg1"] = np.ascontiguousarray(np.concatenate([fg[:D]] + [np.tile(fg[D + DH * i:D + DH * (i + 1)], (H, 1)) for i in range(3)], axis=1))
    a["fg2"] = np.ascontiguousarray(g["L1_attn_fg_w2"].T.reshape(GM, 128, BRANCHES).transpose(1, 0, 2).reshape(128, -1))
    a["fg_b1"] = col(g["L1_attn_fg_b1"])
    a["fg_b2"] = rep(g["L1_attn_fg_b2"])
    a["logit_temp"] = rep(g["L1_attn_logit_temp"])
    a["o_proj"] = T_(g["L1_attn_o_proj_w"])
    a["o_norm"] = np.ascontiguousarray(np.tile(g["L1_attn_o_norm_w"], H).reshape(D, 1))
    a["gate_w"] = g["L1_ffn_gate_w"]
    a["sg"], a["su"], a["sd"] = (g[f"L1_ffn_shared_{n}_w"] for n in ("gate", "up", "down"))
    rd = g["L1_ffn_routed_down_w"].reshape(NE, FK, 128, D).transpose(0, 2, 1, 3).reshape(NE, 128, FK * D)
    a["experts"] = np.ascontiguousarray(np.concatenate([g["L1_ffn_routed_gate_w"], g["L1_ffn_routed_up_w"], rd], axis=2))
    i128 = np.arange(128)
    a["down"] = np.ascontiguousarray(np.broadcast_to((NE - np.arange(NE)).astype(np.float32), (128, NE)))
    a["before"] = bf16_ones(i128[:, None] < i128[None, :])
    a["ones"] = bf16_ones(np.ones((128, 128), bool))
    a["restart"] = np.ascontiguousarray(np.broadcast_to((np.arange(NE * NT) % NT != 0).astype(np.float32), (128, NE * NT)))
    a["starts"] = (128.0 * np.arange(SLOTS)).astype(np.float32).reshape(1, SLOTS)
    i32 = np.arange(32)
    a["keep_lt"] = np.tile((i32[:, None] < i32[None, :]).astype(np.float32), (H, 1))
    a["keep_le"] = np.tile((i32[:, None] <= i32[None, :]).astype(np.float32), (H, 1))
    a["headsum"] = np.kron(np.eye(H, dtype=np.float32), np.ones((DH, DH), np.float32))
    a["headmean"] = np.kron(np.eye(H, dtype=np.float32), np.full((DH, DH), 1.0 / DH, np.float32))
    a["eye32"] = np.ascontiguousarray(np.broadcast_to(np.eye(32, dtype=np.float32).reshape(1, -1), (128, 1024)))

    r = np.arange(96)
    a["select"] = np.ascontiguousarray(np.broadcast_to(bf16_ones((r[:, None] % 32 == np.arange(32)[None, :])[:, :, None]), (96, 32, 128)))
    a["ident"] = np.eye(128, dtype=np.float32)
    a["mean_w"] = np.full((128, 128), 1.0 / D, np.float32)
    return a


def kernel(**inputs):
    import concourse.bacc as bacc
    from concourse.bass_utils import run_bass_kernel_spmd

    a = lay_out(inputs)
    nc = bacc.Bacc("TRN2", target_bir_lowering=False, num_devices=1)
    w = {k: nc.dram_tensor("in_" + k, v.shape, mybir.dt.from_np(v.dtype), kind="ExternalInput").ap() for k, v in a.items()}
    out = nc.dram_tensor("out_x", (B * S, D), F32, kind="ExternalOutput").ap()
    build(nc, w, out, STAGES)
    r = run_bass_kernel_spmd(nc, [{"in_" + k: v for k, v in a.items()}], core_ids=[0])
    return r.results[0]["out_x"].reshape(B, S, D)
```

```python
from contextlib import ExitStack

import numpy as np

import concourse.bass as bass
from concourse import mybir

F32 = mybir.dt.float32
BF16 = mybir.dt.bfloat16
I32 = mybir.dt.int32
U32 = mybir.dt.uint32
U16 = mybir.dt.uint16
ALU = mybir.AluOpType
ACT = mybir.ActivationFunctionType
AX = mybir.AxisListType

D = 128
B = 8
S = 1024
T = 512
TILES = B * S // T
HALVES = S // T
PAD = 4
ROW = PAD + S
LAG = 3
READS = 4
NSTATE = 16
DTR = 64
HID = 512
KT = HID // 128
EPS = 1e-5
LN_EXP = "natural_log_exp_and_others"


def alloc(nc, ctx):
    def sb(name, shape, dt=F32):
        return ctx.enter_context(nc.sbuf_tensor(name, shape, dt))

    def ps(name, shape, dt=F32):
        return ctx.enter_context(nc.psum_tensor(name, shape, dt))

    def sem(name):
        return ctx.enter_context(nc.semaphore(name))

    return sb, ps, sem


def loop(eng, n, body):
    body(0)
    with eng.Fori(1, n) as i:
        body(i)


def is_first(i):
    return isinstance(i, int) and i == 0


def tile_cols(X, t):
    if isinstance(t, int):
        b, h = t // HALVES, t % HALVES
        return X[:, b * ROW + PAD + h * T:b * ROW + PAD + (h + 1) * T]
    raise TypeError


def seq_cols(X, b, lo, n):
    return X[:, bass.ds(b * ROW + (PAD + lo), n)]


def scan_inputs(nc, X, dt, dtx, parts, w):
    with ExitStack() as ctx:
        sb, ps, sem = alloc(nc, ctx)
        wbc, wr, wdt = sb("wbc", [D, 96]), sb("wr", [D, DTR]), sb("wdt", [DTR, D])
        bdt = sb("bdt", [D, 1])
        low = sb("low", [DTR, T])
        rest, rest2, mid = sb("rest", [96, T]), sb("rest2", [96, T]), sb("mid", [96, T], BF16)
        absz, expz, lnz, posz = (sb(n, [D, T]) for n in ("absz", "expz", "lnz", "posz"))
        p_bc, p_low, p_z = ps("p_bc", [96, T]), ps("p_low", [DTR, T]), ps("p_z", [D, T])
        s_w, s_x, s_pad = sem("a_weights"), sem("a_x"), sem("a_pad")
        s_proj, s_low, s_z = sem("a_proj"), sem("a_low"), sem("a_z")
        s_hi, s_rest, s_mid, s_rest2, s_parts = sem("a_hi"), sem("a_rest"), sem("a_mid"), sem("a_rest2"), sem("a_parts")
        s_abs, s_exp, s_ln, s_pos, s_dt, s_dtx = (sem(n) for n in ("a_abs", "a_exp", "a_ln", "a_pos", "a_dt", "a_dtx"))
        block = ctx.enter_context(nc.Block())

        @block.sync
        def _(sp):
            for dst, src in ((wbc, w["bc"]), (wr, w["low"]), (wdt, w["dt"]), (bdt, w["b_dt"])):
                sp.dma_start(dst[:, :], src[:, :]).then_inc(s_w, 16)
            sp.dma_start(X[:, :].rearrange("p (b c) -> p b c", c=ROW)[:, :, PAD:ROW],
                         w["x"].rearrange("p (b c) -> p b c", c=S)).then_inc(s_x, 16)

        @block.gpsimd
        def _(pool):
            nc.gpsimd.memset(X[:, :].rearrange("p (b c) -> p b c", c=ROW)[:, :, 0:PAD], 0.0).then_inc(s_pad, 1)

        @block.tensor
        def _(pe):
            pe.wait_ge(s_w, 64)
            pe.wait_ge(s_x, 16)

            def body(b):
                for h in range(HALVES):
                    t = b * HALVES + h
                    x = seq_cols(X, b, h * T, T)
                    first = is_first(b) and h == 0
                    if not first:
                        pe.wait_ge(s_hi, t)
                        pe.wait_ge(s_rest, t)
                        pe.wait_ge(s_low, t)
                    nc.tensor.matmul(p_bc[:, :], wbc[:, :], x, start=True, stop=True)
                    nc.tensor.matmul(p_low[:, :], wr[:, :], x, start=True, stop=True).then_inc(s_proj, 1)
                    pe.wait_ge(s_low, t + 1)
                    if not first:
                        pe.wait_ge(s_abs, t)
                        pe.wait_ge(s_pos, t)
                    nc.tensor.matmul(p_z[:, :], wdt[:, :], low[:, :], start=True, stop=True).then_inc(s_z, 1)

            loop(pe, B, body)

        @block.scalar
        def _(act):
            nc.scalar.preload_act_table_set(LN_EXP)
            act.wait_ge(s_w, 64)

            def body(b):
                for h in range(HALVES):
                    t = b * HALVES + h
                    first = is_first(b) and h == 0
                    cols = bass.ds(b * S + h * T, T)
                    act.wait_ge(s_proj, t + 1)
                    nc.scalar.copy(low[:, :], p_low[:, :]).then_inc(s_low, 1)
                    act.nop()
                    nc.scalar.copy(parts[:, cols], p_bc[:, :]).then_inc(s_hi, 1)
                    act.wait_ge(s_rest, t + 1)
                    if not first:
                        act.wait_ge(s_rest2, t)
                    nc.scalar.copy(mid[:, :], rest[:, :]).then_inc(s_mid, 1)
                    act.wait_ge(s_mid, t + 1)
                    act.nop()
                    nc.scalar.copy(parts[32:64, cols], mid[32:64, :]).then_inc(s_parts, 1)
                    act.wait_ge(s_rest2, t + 1)
                    act.nop()
                    nc.scalar.copy(parts[64:96, cols], rest2[64:96, :]).then_inc(s_parts, 1)
                    act.wait_ge(s_z, t + 1)
                    nc.scalar.activation(absz[:, :], p_z[:, :], ACT.Abs, bias=bdt[:, 0:1]).then_inc(s_abs, 1)
                    act.wait_ge(s_abs, t + 1)
                    nc.scalar.activation(expz[:, :], absz[:, :], ACT.Exp, scale=-1.0).then_inc(s_exp, 1)
                    act.wait_ge(s_exp, t + 1)
                    if not first:
                        act.wait_ge(s_dt, t)
                    nc.scalar.activation(lnz[:, :], expz[:, :], ACT.Ln, bias=1.0).then_inc(s_ln, 1)

            loop(act, B, body)

        @block.vector
        def _(dve):
            dve.wait_ge(s_w, 64)
            dve.wait_ge(s_x, 16)

            def body(b):
                for h in range(HALVES):
                    t = b * HALVES + h
                    first = is_first(b) and h == 0
                    cols = bass.ds(b * S + h * T, T)
                    dve.wait_ge(s_hi, t + 1)
                    if not first:
                        dve.wait_ge(s_parts, 2 * t)
                    nc.vector.tensor_tensor(rest[:, :], p_bc[:, :], parts[:, cols], ALU.subtract).then_inc(s_rest, 1)
                    dve.wait_ge(s_mid, t + 1)
                    nc.vector.tensor_tensor(rest2[:, :], rest[:, :], mid[:, :], ALU.subtract).then_inc(s_rest2, 1)
                    dve.wait_ge(s_abs, t + 1)
                    nc.vector.tensor_scalar(posz[:, :], p_z[:, :], bdt[:, 0:1], 0.0, ALU.add, ALU.max).then_inc(s_pos, 1)
                    dve.wait_ge(s_pos, t + 1)
                    dve.wait_ge(s_ln, t + 1)
                    nc.vector.tensor_tensor(dt[:, cols], posz[:, :], lnz[:, :], ALU.add).then_inc(s_dt, 1)
                    dve.wait_ge(s_dt, t + 1)
                    nc.vector.tensor_tensor(dtx[:, cols], dt[:, cols], seq_cols(X, b, h * T, T),
                                            ALU.mult).then_inc(s_dtx, 1)

            loop(dve, B, body)


def selective_scan(nc, X, dt, dtx, parts, w):
    with ExitStack() as ctx:
        sb, ps, sem = alloc(nc, ctx)
        select = sb("select", [96, 2 * NSTATE, D], BF16)
        ident = sb("ident_a", [D, D])
        alog, negA = sb("alog", [D, NSTATE]), sb("negA", [D, NSTATE])
        dtseq = sb("dtseq", [D, S])
        decay = sb("decay", [D, 2, S])
        inject = sb("inject", [D, 2, S])
        state = sb("state", [D, 2, S])
        crow = sb("crow", [D, 2, S])
        read = sb("read", [D, READS, S])
        p_b, p_c, p_y = ps("p_b", [D, 2, HALVES, T]), ps("p_c", [D, HALVES, T]), ps("p_y", [D, HALVES, T])
        s_w, s_ea, s_a, s_dtcopy = sem("b_weights"), sem("b_expA"), sem("b_negA"), sem("b_dtcopy")
        s_bready, s_inject, s_decay, s_state = (sem(n) for n in ("b_bready", "b_inject", "b_decay", "b_state"))
        s_cready, s_crow, s_read, s_summed = (sem(n) for n in ("b_cready", "b_crow", "b_read", "b_summed"))
        s_yused = sem("b_yused")
        block = ctx.enter_context(nc.Block())

        @block.sync
        def _(sp):
            sp.dma_start(select[:, :, :].bitcast(U16), w["select"][:, :, :]).then_inc(s_w, 16)
            sp.dma_start(ident[:, :], w["ident"][:, :]).then_inc(s_w, 16)
            sp.dma_start(alog[:, :], w["A_log"][:, :]).then_inc(s_w, 16)

        @block.tensor
        def _(pe):
            pe.wait_ge(s_w, 48)

            def sum_states(b, n):
                pe.wait_ge(s_read, b * NSTATE + n + 1)
                if n == 0 and not is_first(b):
                    pe.wait_ge(s_yused, HALVES * b)
                for h in range(HALVES):
                    mm = nc.tensor.matmul(p_y[:, h, :], ident[:, :], read[:, n % READS, h * T:(h + 1) * T],
                                          start=(n == 0), stop=(n == NSTATE - 1))
                mm.then_inc(s_summed, 1)

            def body(b):
                for n in range(NSTATE):
                    k = b * NSTATE + n
                    first = is_first(b) and n == 0
                    for h in range(HALVES):
                        rhs = parts[:, bass.ds(b * S + h * T, T)]
                        if not is_first(b) or n >= 2:
                            pe.wait_ge(s_inject, HALVES * (k - 2) + h + 1)
                        nc.tensor.matmul(p_b[:, n % 2, h, :], select[:, n, :], rhs, start=True, stop=True).then_inc(s_bready, 1)
                    for h in range(HALVES):
                        rhs = parts[:, bass.ds(b * S + h * T, T)]
                        if not first:
                            pe.wait_ge(s_crow, HALVES * (k - 1) + h + 1)
                        nc.tensor.matmul(p_c[:, h, :], select[:, NSTATE + n, :], rhs,
                                         start=True, stop=True).then_inc(s_cready, 1)
                    if n >= LAG:
                        sum_states(b, n - LAG)
                    elif not is_first(b):
                        sum_states(b - 1, NSTATE - LAG + n)

            loop(pe, B, body)
            for n in range(NSTATE - LAG, NSTATE):
                sum_states(B - 1, n)

        @block.scalar
        def _(act):
            act.wait_ge(s_w, 48)
            nc.scalar.activation(alog[:, :], alog[:, :], ACT.Exp).then_inc(s_ea, 1)
            act.wait_ge(s_a, 1)

            def body(b):
                if not is_first(b):
                    act.wait_ge(s_decay, NSTATE * b)
                nc.scalar.copy(dtseq[:, :], dt[:, bass.ds(b * S, S)]).then_inc(s_dtcopy, 1)
                for n in range(NSTATE):
                    k = b * NSTATE + n
                    warm = not is_first(b) or n >= 2
                    if warm:
                        act.wait_ge(s_state, k - 1)
                    if n == 0:
                        act.wait_ge(s_dtcopy, b + 1)
                    nc.scalar.activation(decay[:, n % 2, :], dtseq[:, :], ACT.Exp,
                                         scale=negA[:, n:n + 1]).then_inc(s_decay, 1)
                    if warm:
                        act.wait_ge(s_read, k - 1)
                    for h in range(HALVES):
                        act.wait_ge(s_cready, HALVES * k + h + 1)
                        nc.scalar.copy(crow[:, n % 2, h * T:(h + 1) * T], p_c[:, h, :]).then_inc(s_crow, 1)

            loop(act, B, body)

        @block.gpsimd
        def _(pool):
            def body(b):
                for n in range(NSTATE):
                    k = b * NSTATE + n
                    pool.wait_ge(s_state, k + 1)
                    pool.wait_ge(s_crow, HALVES * (k + 1))
                    if not is_first(b) or n >= READS:
                        pool.wait_ge(s_summed, k - READS + 1)
                    nc.gpsimd.tensor_tensor(read[:, n % READS, :], state[:, n % 2, :], crow[:, n % 2, :],
                                            ALU.mult).then_inc(s_read, 1)

            loop(pool, B, body)

        @block.vector
        def _(dve):
            dve.wait_ge(s_ea, 1)
            nc.vector.tensor_scalar(negA[:, :], alog[:, :], -1.0, None, ALU.mult).then_inc(s_a, 1)

            def body(b):
                def make_inject(n):
                    k = b * NSTATE + n
                    if not is_first(b) or n >= 2:
                        dve.wait_ge(s_state, k - 1)
                    for h in range(HALVES):
                        dve.wait_ge(s_bready, HALVES * k + h + 1)
                        nc.vector.tensor_tensor(inject[:, n % 2, h * T:(h + 1) * T], p_b[:, n % 2, h, :],
                                                dtx[:, bass.ds(b * S + h * T, T)], ALU.mult).then_inc(s_inject, 1)

                make_inject(0)
                for n in range(NSTATE):
                    k = b * NSTATE + n
                    if n + 1 < NSTATE:
                        make_inject(n + 1)
                    dve.wait_ge(s_inject, HALVES * (k + 1))
                    dve.wait_ge(s_decay, k + 1)
                    if not is_first(b) or n >= 2:
                        dve.wait_ge(s_read, k - 1)
                    nc.vector.tensor_tensor_scan(state[:, n % 2, :], decay[:, n % 2, :], inject[:, n % 2, :], 0.0,
                                                 ALU.mult, ALU.add).then_inc(s_state, 1)
                    if n == LAG - 1 and not is_first(b):
                        add_sums(b - 1)

            def add_sums(b):
                dve.wait_ge(s_summed, NSTATE * (b + 1))
                for h in range(HALVES):
                    x = seq_cols(X, b, h * T, T)
                    nc.vector.tensor_tensor(x, p_y[:, h, :], x, ALU.add).then_inc(s_yused, 1)

            loop(dve, B, body)
            add_sums(B - 1)


def layer_norm(nc, X, w, tag):
    with ExitStack() as ctx:
        sb, ps, sem = alloc(nc, ctx)
        mean_w = sb(tag + "mean_w", [D, D])
        eps = sb(tag + "eps", [D, 1])
        centred, square = sb(tag + "centred", [D, 2, T]), sb(tag + "square", [D, 2, T])
        logv, rstd = sb(tag + "logv", [D, 2, T]), sb(tag + "rstd", [D, 2, T])
        p_mean, p_var = ps(tag + "p_mean", [D, 2, T]), ps(tag + "p_var", [D, 2, T])
        s_w, s_eps = sem(tag + "weights"), sem(tag + "eps_set")
        s_mean, s_centred, s_square, s_var, s_log, s_rstd, s_out = (
            sem(tag + n) for n in ("mean", "centred", "square", "var", "log", "rstd", "out"))
        block = ctx.enter_context(nc.Block())

        @block.sync
        def _(sp):
            sp.dma_start(mean_w[:, :], w["mean_w"][:, :]).then_inc(s_w, 16)

        @block.tensor
        def _(pe):
            pe.wait_ge(s_w, 16)

            def mean(b, h):
                t = b * HALVES + h
                if not is_first(b):
                    pe.wait_ge(s_centred, t - 1)
                nc.tensor.matmul(p_mean[:, h, :], mean_w[:, :], seq_cols(X, b, h * T, T),
                                 start=True, stop=True).then_inc(s_mean, 1)

            def var(b, h):
                t = b * HALVES + h
                pe.wait_ge(s_square, t + 1)
                if not is_first(b):
                    pe.wait_ge(s_log, t - 1)
                nc.tensor.matmul(p_var[:, h, :], mean_w[:, :], square[:, h, :],
                                 start=True, stop=True).then_inc(s_var, 1)

            def body(b):
                mean(b, 0)
                mean(b, 1)
                var(b, 0)
                var(b, 1)

            loop(pe, B, body)

        @block.scalar
        def _(act):
            nc.scalar.preload_act_table_set(LN_EXP)
            act.wait_ge(s_eps, 1)

            def body(b):
                for h in range(HALVES):
                    t = b * HALVES + h
                    act.wait_ge(s_centred, t + 1)
                    if not is_first(b):
                        act.wait_ge(s_var, t - 1)
                    nc.scalar.activation(square[:, h, :], centred[:, h, :], ACT.Square).then_inc(s_square, 1)
                for h in range(HALVES):
                    t = b * HALVES + h
                    act.wait_ge(s_var, t + 1)
                    nc.scalar.activation(logv[:, h, :], p_var[:, h, :], ACT.Ln, bias=eps[:, 0:1]).then_inc(s_log, 1)
                    act.wait_ge(s_log, t + 1)
                    if not is_first(b):
                        act.wait_ge(s_out, t - 1)
                    nc.scalar.activation(rstd[:, h, :], logv[:, h, :], ACT.Exp, scale=-0.5).then_inc(s_rstd, 1)

            loop(act, B, body)

        @block.vector
        def _(dve):
            nc.vector.memset(eps[:, :], EPS).then_inc(s_eps, 1)

            def body(b):
                for h in range(HALVES):
                    t = b * HALVES + h
                    dve.wait_ge(s_mean, t + 1)
                    if not is_first(b):
                        dve.wait_ge(s_square, t - 1)
                        dve.wait_ge(s_out, t - 1)
                    nc.vector.tensor_tensor(centred[:, h, :], seq_cols(X, b, h * T, T), p_mean[:, h, :],
                                            ALU.subtract).then_inc(s_centred, 1)
                for h in range(HALVES):
                    t = b * HALVES + h
                    dve.wait_ge(s_rstd, t + 1)
                    dve.wait_ge(s_centred, t + 1)
                    nc.vector.tensor_tensor(seq_cols(X, b, h * T, T), centred[:, h, :], rstd[:, h, :],
                                            ALU.mult).then_inc(s_out, 1)

            loop(dve, B, body)


def ternary_ffn(nc, X, w):
    with ExitStack() as ctx:
        sb, ps, sem = alloc(nc, ctx)
        w1, w2 = sb("w1", [D, HID]), sb("w2", [D, HID])
        h1, h2, w3 = sb("h1", [128, KT, HID]), sb("h2", [128, KT, HID]), sb("w3", [128, KT, D])
        scales = sb("scales", [128, 4 * KT + 1])
        gate = sb("gate", [128, 2, KT, T])
        act0 = sb("act0", [128, 2, KT, T])
        p_hid = ps("p_hid", [128, 4, T])
        p_out = ps("p_out", [128, 2, T])
        s_w = sem("f_weights")
        s_g, s_u, s_gate, s_prod = sem("f_g"), sem("f_u"), sem("f_gate"), sem("f_prod")
        s_mm1, s_mm2, s_act1, s_act2, s_mm3, s_out = (sem("f_" + n) for n in ("mm1", "mm2", "act1", "act2", "mm3", "out"))
        block = ctx.enter_context(nc.Block())

        @block.sync
        def _(sp):
            sp.dma_start(w1[:, :], w["w1"][:, :]).then_inc(s_w, 16)
            sp.dma_start(w2[:, :], w["w2"][:, :]).then_inc(s_w, 16)
            sp.dma_start(h1[:, :, :], w["h1"].rearrange("(k p) n -> p k n", p=128)).then_inc(s_w, 16)
            sp.dma_start(h2[:, :, :], w["h2"].rearrange("(k p) n -> p k n", p=128)).then_inc(s_w, 16)
            sp.dma_start(w3[:, :, :], w["w3"].rearrange("(k p) n -> p k n", p=128)).then_inc(s_w, 16)
            sp.dma_start(scales[:, :], w["ffn_scales"][:, :]).then_inc(s_w, 16)

        N = 2 * KT

        @block.tensor
        def _(pe):
            pe.wait_ge(s_w, 96)

            def body(b):
                base = b * N
                for h in range(2):
                    x = seq_cols(X, b, h * T, T)
                    for m in range(KT):
                        i = h * KT + m
                        bank = 2 * (i % 2)
                        if i >= 2:
                            pe.wait_ge(s_gate, base + i - 1)
                            pe.wait_ge(s_prod, base + i - 1)
                        elif not is_first(b):
                            pe.wait_ge(s_act2, base)
                        nc.tensor.matmul(p_hid[:, bank, :], w1[:, m * 128:(m + 1) * 128], x,
                                         start=True, stop=True).then_inc(s_g, 1)
                        nc.tensor.matmul(p_hid[:, bank + 1, :], w2[:, m * 128:(m + 1) * 128], x,
                                         start=True, stop=True).then_inc(s_u, 1)
                for layer, (wt, src, s_src, s_mm, s_free) in enumerate((
                        (h1, act0, s_prod, s_mm1, s_act1), (h2, gate, s_act1, s_mm2, s_act2))):
                    for h in range(2):
                        pe.wait_ge(s_src, base + KT * (h + 1))
                        for m in range(KT):
                            i = h * KT + m
                            if i >= 4:
                                pe.wait_ge(s_free, base + i - 3)
                            elif layer == 0:
                                pe.wait_ge(s_gate, base + N)
                                pe.wait_ge(s_prod, base + N)
                            else:
                                pe.wait_ge(s_act1, base + N - 3 + i)
                            for k in range(KT):
                                mm = nc.tensor.matmul(p_hid[:, i % 4, :], wt[:, k, m * 128:(m + 1) * 128],
                                                      src[:, h, k, :], start=(k == 0), stop=(k == KT - 1))
                            mm.then_inc(s_mm, 1)
                for h in range(2):
                    pe.wait_ge(s_act2, base + KT * (h + 1))
                    if not is_first(b):
                        pe.wait_ge(s_out, 2 * b)
                    for k in range(KT):
                        mm = nc.tensor.matmul(p_out[:, h, :], w3[:, k, :], act0[:, h, k, :],
                                              start=(k == 0), stop=(k == KT - 1))
                    mm.then_inc(s_mm3, 1)

            loop(pe, B, body)

        @block.scalar
        def _(act):
            act.wait_ge(s_w, 96)

            def body(b):
                base = b * N
                for i in range(N):
                    h, m = i // KT, i % KT
                    act.wait_ge(s_g, base + i + 1)
                    if i == 0 and not is_first(b):
                        act.wait_ge(s_mm2, base)
                    nc.scalar.activation(gate[:, h, m, :], p_hid[:, 2 * (i % 2), :], ACT.Silu,
                                         scale=scales[:, m:m + 1]).then_inc(s_gate, 1)
                for i in range(N):
                    h, m = i // KT, i % KT
                    act.wait_ge(s_mm1, base + i + 1)
                    if i == 0:
                        act.wait_ge(s_prod, base + N)
                    nc.scalar.activation(gate[:, h, m, :], p_hid[:, i % 4, :], ACT.Gelu,
                                         scale=scales[:, 2 * KT + m:2 * KT + m + 1]).then_inc(s_act1, 1)
                for i in range(N):
                    h, m = i // KT, i % KT
                    act.wait_ge(s_mm2, base + i + 1)
                    if m == 0:
                        act.wait_ge(s_mm1, base + KT * (h + 1))
                    nc.scalar.activation(act0[:, h, m, :], p_hid[:, i % 4, :], ACT.Gelu,
                                         scale=scales[:, 3 * KT + m:3 * KT + m + 1]).then_inc(s_act2, 1)

            loop(act, B, body)

        @block.vector
        def _(dve):
            dve.wait_ge(s_w, 96)

            def body(b):
                base = b * N
                for i in range(N):
                    h, m = i // KT, i % KT
                    dve.wait_ge(s_u, base + i + 1)
                    dve.wait_ge(s_gate, base + i + 1)
                    if i == 0 and not is_first(b):
                        dve.wait_ge(s_mm3, 2 * b)
                    nc.vector.scalar_tensor_tensor(out=act0[:, h, m, :], in0=p_hid[:, 2 * (i % 2) + 1, :],
                                                   scalar=scales[:, KT + m:KT + m + 1], in1=gate[:, h, m, :],
                                                   op0=ALU.mult, op1=ALU.mult).then_inc(s_prod, 1)
                for h in range(2):
                    x = seq_cols(X, b, h * T, T)
                    dve.wait_ge(s_mm3, 2 * b + h + 1)
                    nc.vector.scalar_tensor_tensor(out=x, in0=p_out[:, h, :], scalar=scales[:, 4 * KT:4 * KT + 1],
                                                   in1=x, op0=ALU.mult, op1=ALU.add).then_inc(s_out, 1)

            loop(dve, B, body)


H = 4
DH = 32
CS = 32
NC_ = S // CS
CONV = 4
SHORT, LONG = 3, 31
PE_TAPS = 16
BRANCHES = 4
GH = 128
KB, Q, K, ATT, VB, INV = (DH * i for i in range(6))
REC = 6 * DH
HALF_B = 4


def started(b):
    return not isinstance(b, int) or b > 0


def pipeline(eng, step, late=None):
    for b in range(2):
        step(b, b, 0)
    with eng.Fori(1, B // 2) as i:
        for e in range(2):
            step(2 * i + e, e, i)
    if late:
        late(B - 1)


def delta_inputs(nc, X, V, L, w, scratch):
    chunks, recs = scratch["upper"], scratch["records"]
    with ExitStack() as ctx:
        sb, ps, sem = alloc(nc, ctx)
        wconv = sb("wconv", [D, 3, CONV, D])
        wproj = sb("wproj", [D, D])
        taps = sb("taps", [D, CONV, D])
        wbeta, headsum = sb("wbeta", [D, D]), sb("headsum", [D, D])
        ident, ltaps = sb("ident_c", [D, D]), sb("ltaps", [D, LONG])
        diag = sb("diag", [D, PE_TAPS, D])
        keep_lt, keep_le = sb("keep_lt", [D, CS]), sb("keep_le", [D, CS])
        tiny = sb("tiny", [D, 1])
        qs, ks, kn = sb("qs", [D, S]), sb("ks", [D, S]), sb("kn", [D, S])
        vs = sb("vs", [D, 2, DH + S])
        beta, rq, rk = sb("beta", [D, S]), sb("rq", [D, S]), sb("rk", [D, S])
        kdiag = sb("kdiag", [D, NC_, H, CS])
        rec = sb("rec", [D, NC_, INV])
        upper = sb("upper", [D, NC_, CS])
        umat, rmat = sb("umat", [D, CS, CS]), sb("rmat", [D, CS, CS])
        prod = sb("prod", [D, (CS - 1) * (CS - 1)])
        acc = sb("acc", [D, 2, S])
        p_z = ps("p_zc", [D, 2, T])
        p_att = ps("p_att", [D, 4, T])
        p_fir = ps("p_fir", [D, 2, T])
        s_w, s_raw, s_tap, s_ready = sem("c_weights"), sem("c_raw"), sem("c_tap"), sem("c_ready")
        s_z, s_zread, s_sq, s_rs = sem("c_z"), sem("c_zread"), sem("c_sq"), sem("c_rs")
        s_qn, s_kn, s_kb, s_vb, s_kt, s_kdiag = (sem("c_" + n) for n in ("qn", "kn", "kb", "vb", "kt", "kdiag"))
        s_att, s_masked, s_fir, s_joined, s_acc, s_long = (
            sem("c_" + n) for n in ("att", "masked", "fir", "joined", "acc", "long"))
        s_uout, s_uin, s_solve, s_rout, s_recout = (
            sem("c_" + n) for n in ("uout", "uin", "solve", "rout", "recout"))
        s_vout = [sem("c_vout0"), sem("c_vout1")]
        block = ctx.enter_context(nc.Block())
        SOLVE = 2 * (CS - 1)
        DVE_TAPS = LONG - PE_TAPS

        @block.sync
        def _(sp):
            loads = ((wbeta, w["b_proj"]), (headsum, w["headsum"]), (ident, w["ident"]), (ltaps, w["fir_long"]),
                     (keep_lt, w["keep_lt"]), (keep_le, w["keep_le"]))
            for dst, src in loads:
                sp.dma_start(dst[:, :], src[:, :]).then_inc(s_w, 16)
            sp.dma_start(rmat[:, :, :], w["eye32"].rearrange("p (j i) -> p j i", i=CS)).then_inc(s_w, 16)
            for p, n in enumerate("qkv"):
                if p:
                    sp.wait_ge(s_tap, CONV * p)
                sp.dma_start(wproj[:, :], w[n + "_proj"][:, :]).then_inc(s_raw, 16)
                sp.dma_start(taps[:, :, :], w[n + "_conv"].rearrange("p (j n) -> p j n", j=CONV)).then_inc(s_raw, 16)

            def inverse_out(b):
                sp.wait_ge(s_solve, SOLVE * (b + 1))
                for h in range(H):
                    dst = recs[:, h * CS:(h + 1) * CS, bass.ds(b * REC + INV, CS)]
                    sp.dma_start(dst, rmat[h * NC_:(h + 1) * NC_, :, :]).then_inc(s_rout, 16)

            def step(b, e, i):
                sp.wait_ge(s_zread, 12 * b + 6)
                sp.dma_start(V[:, bass.ds(b * ROW + PAD, S)], vs[:, e, DH:]).then_inc(s_vout[e], 16)
                if started(b):
                    inverse_out(b - 1)
                sp.wait_ge(s_masked, 8 * (b + 1))
                for h in range(H):
                    sp.dma_start(chunks[h].rearrange("n j i -> j n i"),
                                 upper[h * CS:(h + 1) * CS, :, :]).then_inc(s_uout, 16)
                sp.wait_ge(s_vb, b + 1)
                sp.wait_ge(s_kt, b + 1)
                dst = recs[:, :, bass.ds(b * REC, INV)].rearrange("n p c -> p n c")
                sp.dma_start(dst, rec[:, :, :]).then_inc(s_recout, 16)
                sp.wait_ge(s_uout, 64 * (b + 1))
                sp.dma_start(umat[:, :, :], chunks.rearrange("h n j i -> (h n) j i")).then_inc(s_uin, 16)

            pipeline(sp, step, inverse_out)
            for s, n in ((s_rout, 64 * B), (s_vout[0], 8 * B), (s_vout[1], 8 * B), (s_recout, 16 * B)):
                sp.wait_ge(s, n)

        @block.tensor
        def _(pe):
            pe.wait_ge(s_w, 112)
            pe.wait_ge(s_ready, 3 + PE_TAPS)
            pe.wait_ge(s_tap, 3 * CONV)

            def fir(b, e, h):
                if started(b):
                    pe.wait_ge(s_joined, 2 * (b - 1) + h + 1)
                for j in range(PE_TAPS):
                    lo = DH + h * T - (LONG - 1) + j
                    mm = nc.tensor.matmul(p_fir[:, h, :], diag[:, j, :], vs[:, e, lo:lo + T],
                                          start=(j == 0), stop=(j == PE_TAPS - 1))
                mm.then_inc(s_fir, 1)

            def step(b, e, i):
                first = is_first(b)

                def bank_free(i):
                    if i >= 2 or not first:
                        pe.wait_ge(s_zread, 12 * b + i - 1)

                for i in range(6):
                    bank_free(i)
                    p, h = i // 2, i % 2
                    for j in range(CONV):
                        mm = nc.tensor.matmul(p_z[:, i % 2, :], wconv[:, p, j, :],
                                              seq_cols(X, b, h * T - (CONV - 1) + j, T),
                                              start=(j == 0), stop=(j == CONV - 1))
                    mm.then_inc(s_z, 1)
                for h in range(2):
                    bank_free(6 + h)
                    nc.tensor.matmul(p_z[:, h, :], wbeta[:, :], seq_cols(X, b, h * T, T),
                                     start=True, stop=True).then_inc(s_z, 1)
                if not first:
                    fir(b - 1, 1 - e, 0)
                for i in range(8, 12):
                    bank_free(i)
                    pe.wait_ge(s_sq, 2 * b + (i - 8) // 2 + 1)
                    src = rq if i < 10 else rk
                    nc.tensor.matmul(p_z[:, i % 2, :], headsum[:, :], src[:, (i % 2) * T:(i % 2 + 1) * T],
                                     start=True, stop=True).then_inc(s_z, 1)
                if not first:
                    fir(b - 1, 1 - e, 1)
                pe.wait_ge(s_kdiag, H * (b + 1))
                pe.wait_ge(s_kb, b + 1)
                pe.wait_ge(s_qn, b + 1)
                for g in range(4):
                    if not first:
                        pe.wait_ge(s_masked, 8 * b)
                    for c in range(8):
                        n = 8 * g + c
                        mm = nc.tensor.matmul(p_att[:, g, c * 64:(c + 1) * 64], kdiag[:, n, :, :],
                                              rec[:, n, KB:KB + 2 * DH], start=True, stop=True)
                    mm.then_inc(s_att, 1)

            def late(b):
                for h in range(2):
                    fir(b, b % 2, h)

            pipeline(pe, step, late)

        @block.scalar
        def _(act):
            def step(b, e, turn):
                first = is_first(b)
                for i in range(6):
                    p, h = i // 2, i % 2
                    act.wait_ge(s_z, 12 * b + i + 1)
                    if not first and i == 0:
                        act.wait_ge(s_qn, b)
                        act.wait_ge(s_kn, b)
                        act.wait_ge(s_kdiag, H * b)
                    if i == 4 and not (isinstance(b, int) and b < 2):
                        act.wait_ge(s_vb, b - 1)
                        act.wait_ge(s_fir, 2 * (b - 1))
                        act.wait_ge(s_acc, DVE_TAPS * (b - 1))
                        act.wait_ge(s_vout[e], 16 * turn)
                    dst = (qs[:, h * T:(h + 1) * T], ks[:, h * T:(h + 1) * T], vs[:, e, DH + h * T:DH + (h + 1) * T])[p]
                    nc.scalar.activation(dst, p_z[:, h, :], ACT.Silu).then_inc(s_zread, 1)
                for h in range(2):
                    act.wait_ge(s_z, 12 * b + 7 + h)
                    if not first and h == 0:
                        act.wait_ge(s_kb, b)
                        act.wait_ge(s_vb, b)
                    nc.scalar.activation(beta[:, h * T:(h + 1) * T], p_z[:, h, :], ACT.Sigmoid).then_inc(s_zread, 1)
                act.wait_ge(s_zread, 12 * b + 4)
                nc.scalar.activation(rq[:, :], qs[:, :], ACT.Square).then_inc(s_sq, 1)
                nc.scalar.activation(rk[:, :], ks[:, :], ACT.Square).then_inc(s_sq, 1)
                nc.scalar.preload_act_table_set(LN_EXP)
                for i in range(8, 12):
                    act.wait_ge(s_z, 12 * b + i + 1)
                    dst = (rq if i < 10 else rk)[:, (i % 2) * T:(i % 2 + 1) * T]
                    if i % 2 == 0:
                        act.wait_ge(s_z, 12 * b + i + 2)
                    nc.scalar.activation(dst, p_z[:, i % 2, :], ACT.Ln, bias=tiny[:, 0:1]).then_inc(s_zread, 1)
                act.wait_ge(s_zread, 12 * b + 12)
                nc.scalar.activation(rq[:, :], rq[:, :], ACT.Exp, scale=-0.5).then_inc(s_rs, 1)
                nc.scalar.activation(rk[:, :], rk[:, :], ACT.Exp, scale=-0.5).then_inc(s_rs, 1)

            pipeline(act, step)

        @block.gpsimd
        def _(pool):
            nc.gpsimd.memset(kdiag[:, :, :, :], 0.0).then_inc(s_ready, 1)
            nc.gpsimd.memset(vs[:, :, 0:DH], 0.0).then_inc(s_ready, 1)
            nc.gpsimd.memset(V[:, :].rearrange("p (b c) -> p b c", c=ROW)[:, :, 0:PAD], 0.0).then_inc(s_ready, 1)
            pool.wait_ge(s_w, 112)
            for j in range(PE_TAPS):
                nc.gpsimd.tensor_scalar(diag[:, j, :], ident[:, :], ltaps[:, j:j + 1], None, ALU.mult).then_inc(s_ready, 1)
            pool.wait_ge(s_ready, 1)

            def long_out(b):
                pool.wait_ge(s_acc, DVE_TAPS * (b + 1))
                pool.wait_ge(s_joined, 2 * (b + 1))
                nc.gpsimd.tensor_tensor(L[:, bass.ds(b * S, S)], acc[:, 0, :], acc[:, 1, :], ALU.add).then_inc(s_long, 1)

            def step(b, e, i):
                pool.wait_ge(s_rs, 2 * (b + 1))
                if not is_first(b):
                    pool.wait_ge(s_att, 4 * b)
                if not (isinstance(b, int) and b < 2):
                    pool.wait_ge(s_long, b - 1)
                for h in range(H):
                    r = slice(h * DH, (h + 1) * DH)
                    split = lambda t: t[r, :].rearrange("p (n i) -> p n i", i=CS)
                    nc.gpsimd.tensor_tensor(kdiag[r, :, h, :], split(ks), split(rk), ALU.mult).then_inc(s_kdiag, 1)
                if not is_first(b):
                    pool.wait_ge(s_kdiag, H * (b + 1))
                    long_out(b - 1)

            pipeline(pool, step, long_out)

        @block.vector
        def _(dve):
            nc.vector.memset(tiny[:, :], 1e-12)
            dve.wait_ge(s_w, 112)
            for p in range(3):
                dve.wait_ge(s_raw, 32 * (p + 1))
                for j in range(CONV):
                    nc.vector.tensor_tensor(wconv[:, p, j, :], wproj[:, :], taps[:, j, :], ALU.mult).then_inc(s_tap, 1)
            slot = lambda at: rec[:, :, at:at + DH]
            chunked = lambda t: t.rearrange("p (n i) -> p n i", i=CS)

            def scaled(b, e):
                first = is_first(b)
                dve.wait_ge(s_rs, 2 * (b + 1))
                if not first:
                    dve.wait_ge(s_recout, 16 * b)
                    dve.wait_ge(s_att, 4 * b)
                    dve.wait_ge(s_kt, b)
                nc.vector.tensor_tensor(kn[:, :], ks[:, :], rk[:, :], ALU.mult).then_inc(s_kn, 1)
                nc.vector.tensor_tensor(slot(Q), chunked(qs[:, :]), chunked(rq[:, :]), ALU.mult).then_inc(s_qn, 1)
                dve.wait_ge(s_kn, b + 1)
                dve.wait_ge(s_zread, 12 * b + 8)
                nc.vector.tensor_tensor(slot(KB), chunked(kn[:, :]), chunked(beta[:, :]), ALU.mult).then_inc(s_kb, 1)
                nc.vector.tensor_tensor(slot(VB), chunked(vs[:, e, DH:]), chunked(beta[:, :]), ALU.mult).then_inc(s_vb, 1)
                nc.vector.transpose(slot(K), chunked(kn[:, :])).then_inc(s_kt, 1)

            def masks(b):
                for g in range(4):
                    c = slice(8 * g, 8 * g + 8)
                    pa = p_att[:, g, :].rearrange("p (n c) -> p n c", c=64)
                    dve.wait_ge(s_att, 4 * b + g + 1)
                    if g == 0 and started(b):
                        dve.wait_ge(s_uout, 64 * b)
                    nc.vector.tensor_tensor(upper[:, c, :], pa[:, :, 0:CS],
                                            keep_lt[:, :].unsqueeze(1).broadcast_to([D, 8, CS]), ALU.mult).then_inc(s_masked, 1)
                    nc.vector.tensor_tensor(rec[:, c, ATT:ATT + CS], pa[:, :, CS:2 * CS],
                                            keep_le[:, :].unsqueeze(1).broadcast_to([D, 8, CS]), ALU.mult).then_inc(s_masked, 1)

            def fir(b, e):
                for k in range(DVE_TAPS):
                    j = PE_TAPS + k
                    lo = DH - (LONG - 1) + j
                    v = vs[:, e, lo:lo + S]
                    if k >= 2:
                        dve.wait_ge(s_acc, DVE_TAPS * b + k - 1)
                        nc.vector.scalar_tensor_tensor(out=acc[:, k % 2, :], in0=v, scalar=ltaps[:, j:j + 1],
                                                       in1=acc[:, k % 2, :], op0=ALU.mult, op1=ALU.add).then_inc(s_acc, 1)
                    else:
                        if k == 0 and started(b):
                            dve.wait_ge(s_long, b)
                        nc.vector.tensor_scalar(acc[:, k % 2, :], v, ltaps[:, j:j + 1], None, ALU.mult).then_inc(s_acc, 1)

            def solve(b):
                dve.wait_ge(s_uin, 16 * (b + 1))
                if started(b):
                    dve.wait_ge(s_rout, 64 * b)
                for n, j in enumerate(range(CS - 2, -1, -1)):
                    m = CS - 1 - j
                    p = prod[:, 0:m * m].rearrange("p (i l) -> p i l", l=m)
                    if n:
                        dve.wait_ge(s_solve, SOLVE * b + 2 * n)
                    nc.vector.tensor_tensor(p, umat[:, j, j + 1:CS].unsqueeze(1).broadcast_to([D, m, m]),
                                            rmat[:, j + 1:CS, j + 1:CS].rearrange("p l i -> p i l"),
                                            ALU.mult).then_inc(s_solve, 1)
                    dve.wait_ge(s_solve, SOLVE * b + 2 * n + 1)
                    nc.vector.tensor_reduce(rmat[:, j, j + 1:CS], p, AX.X, ALU.add, negate=True).then_inc(s_solve, 1)

            def join(b):
                for h in range(2):
                    c = slice(h * T, (h + 1) * T)
                    dve.wait_ge(s_acc, DVE_TAPS * (b + 1))
                    dve.wait_ge(s_fir, 2 * b + h + 1)
                    nc.vector.tensor_tensor(acc[:, 0, c], acc[:, 0, c], p_fir[:, h, :], ALU.add).then_inc(s_joined, 1)

            def step(b, e, i):
                if not is_first(b):
                    fir(b - 1, 1 - e)
                scaled(b, e)
                if not is_first(b):
                    solve(b - 1)
                    join(b - 1)
                masks(b)

            def late(b):
                fir(b, b % 2)
                solve(b)
                join(b)

            pipeline(dve, step, late)


def delta_scan(nc, O, w, scratch):
    recs = scratch["records"]
    with ExitStack() as ctx:
        sb, ps, sem = alloc(nc, ctx)
        inp = sb("scan_in", [D, 2, B, REC])
        sdiag, rdiag, udiag = (sb(n, [D, B, H, DH]) for n in ("sdiag", "rdiag", "udiag"))
        strans, resid, qpart = sb("strans", [D, B, DH]), sb("resid", [D, B, CS]), sb("qpart", [D, B, CS])
        osum = sb("osum", [D, 2, B, CS])
        p_s = [ps(f"p_s{g}", [D, HALF_B, 2 * CS]) for g in range(2)]
        p_u = [ps(f"p_u{g}", [D, HALF_B, CS]) for g in range(2)]
        p_k = [ps(f"p_k{g}", [D, HALF_B, 2 * CS]) for g in range(2)]
        s_zero, s_in, s_out = sem("d_zero"), [sem("d_in0"), sem("d_in1")], [sem("d_out0"), sem("d_out1")]
        s_ms, s_resid, s_rdiag, s_mu, s_udiag, s_mk, s_state, s_sdiag, s_qpart, s_osum = (
            [sem(f"d_{n}{g}") for g in range(2)]
            for n in ("ms", "resid", "rdiag", "mu", "udiag", "mk", "state", "sdiag", "qpart", "osum"))
        block = ctx.enter_context(nc.Block())
        STEPS = NC_ // 2
        seqs = [slice(HALF_B * g, HALF_B * (g + 1)) for g in range(2)]

        def pairs(eng, body):
            body(0)
            with eng.Fori(1, STEPS) as i:
                body(i)

        @block.sync
        def _(sp):
            def body(i):
                for e in range(2):
                    n = 2 * i + e
                    if not is_first(i):
                        for g in range(2):
                            sp.wait_ge(s_mk[g], n - 1)
                            sp.wait_ge(s_resid[g], n - 1)
                    sp.dma_start(inp[:, e, :, :], recs[bass.ds(n, 1), :, :].rearrange("n p (b c) -> (n p) b c", c=REC)
                                 ).then_inc(s_in[e], 16)

            pairs(sp, body)

        @block.gpsimd
        def _(pool):
            for t in (sdiag, rdiag, udiag):
                nc.gpsimd.memset(t[:, :, :, :], 0.0).then_inc(s_zero, 1)
            nc.gpsimd.memset(strans[:, :, :], 0.0).then_inc(s_zero, 1)

            def body(i):
                for e in range(2):
                    n = 2 * i + e
                    for g in range(2):
                        pool.wait_ge(s_osum[g], n + 1)
                    pool.dma_start(O[:, bass.ds(n * CS * B, CS * B)],
                                   osum[:, e, :, :].rearrange("p b c -> p (b c)")).then_inc(s_out[e], 16)

            pairs(pool, body)
            for e in range(2):
                pool.wait_ge(s_out[e], 16 * STEPS)

        @block.tensor
        def _(pe):
            pe.wait_ge(s_zero, 4)

            def body(i):
                for e in range(2):
                    n = 2 * i + e
                    start = is_first(i) and e == 0
                    pe.wait_ge(s_in[e], 16 * (i + 1))
                    for g in range(2):
                        if not start:
                            pe.wait_ge(s_sdiag[g], n * H)
                            pe.wait_ge(s_qpart[g], n)
                        for b in range(HALF_B):
                            bb = HALF_B * g + b
                            mm = nc.tensor.matmul(p_s[g][:, b, :], sdiag[:, bb, :, :], inp[:, e, bb, KB:KB + 2 * DH],
                                                  start=True, stop=True)
                        mm.then_inc(s_ms[g], 1)
                    for g in range(2):
                        pe.wait_ge(s_rdiag[g], (n + 1) * H)
                        if not start:
                            pe.wait_ge(s_udiag[g], n * H)
                        for b in range(HALF_B):
                            bb = HALF_B * g + b
                            mm = nc.tensor.matmul(p_u[g][:, b, :], rdiag[:, bb, :, :], inp[:, e, bb, INV:INV + CS],
                                                  start=True, stop=True)
                        mm.then_inc(s_mu[g], 1)
                    for g in range(2):
                        pe.wait_ge(s_udiag[g], (n + 1) * H)
                        if not start:
                            pe.wait_ge(s_state[g], n)
                            pe.wait_ge(s_osum[g], n)
                        for b in range(HALF_B):
                            bb = HALF_B * g + b
                            mm = nc.tensor.matmul(p_k[g][:, b, :], udiag[:, bb, :, :], inp[:, e, bb, K:K + 2 * DH],
                                                  start=True, stop=True)
                        mm.then_inc(s_mk[g], 1)

            pairs(pe, body)

        @block.scalar
        def _(act):
            def body(i):
                for e in range(2):
                    n = 2 * i + e
                    start = is_first(i) and e == 0
                    for g in range(2):
                        act.wait_ge(s_resid[g], n + 1)
                        if not start:
                            act.wait_ge(s_osum[g], n)
                        nc.scalar.copy(qpart[:, seqs[g], :], p_s[g][:, :, CS:2 * CS]).then_inc(s_qpart[g], 1)

            pairs(act, body)

        @block.vector
        def _(dve):
            dve.wait_ge(s_zero, 4)

            def to_diagonal(dst, src, done, g):
                for h in range(H):
                    r = slice(h * DH, (h + 1) * DH)
                    nc.vector.transpose(dst[r, seqs[g], h, :], src(r)).then_inc(done[g], 1)

            def body(i):
                for e in range(2):
                    n = 2 * i + e
                    start = is_first(i) and e == 0
                    dve.wait_ge(s_in[e], 16 * (i + 1))
                    for g in range(2):
                        dve.wait_ge(s_ms[g], n + 1)
                        if not start:
                            dve.wait_ge(s_mu[g], n)
                        nc.vector.tensor_tensor(resid[:, seqs[g], :], inp[:, e, seqs[g], VB:VB + CS],
                                                p_s[g][:, :, 0:CS], ALU.subtract).then_inc(s_resid[g], 1)
                        dve.wait_ge(s_resid[g], n + 1)
                        to_diagonal(rdiag, lambda r: resid[r, seqs[g], :], s_rdiag, g)
                    for g in range(2):
                        dve.wait_ge(s_mu[g], n + 1)
                        if not start:
                            dve.wait_ge(s_mk[g], n)
                        to_diagonal(udiag, lambda r: p_u[g][r, :, :], s_udiag, g)
                    for g in range(2):
                        dve.wait_ge(s_mk[g], n + 1)
                        nc.vector.tensor_tensor(strans[:, seqs[g], :], strans[:, seqs[g], :], p_k[g][:, :, 0:DH],
                                                ALU.add).then_inc(s_state[g], 1)
                        dve.wait_ge(s_state[g], n + 1)
                        dve.wait_ge(s_ms[g], n + 1)
                        to_diagonal(sdiag, lambda r: strans[r, seqs[g], :], s_sdiag, g)
                        dve.wait_ge(s_qpart[g], n + 1)
                        if not is_first(i):
                            dve.wait_ge(s_out[e], 16 * i)
                        nc.vector.tensor_tensor(osum[:, e, seqs[g], :], qpart[:, seqs[g], :], p_k[g][:, :, CS:2 * CS],
                                                ALU.add).then_inc(s_osum[g], 1)

            pairs(dve, body)


def gate_mix(nc, X, V, L, O, w):
    with ExitStack() as ctx:
        sb, ps, sem = alloc(nc, ctx)
        w1 = sb("fg1", [128, BRANCHES, GH])
        w2 = sb("fg2", [128, BRANCHES])
        b1, b2 = sb("fg1b", [128, 1]), sb("fg2b", [128, BRANCHES])
        temp = sb("temp", [128, 4])
        headmean, wo, onorm = sb("headmean", [D, D]), sb("wo", [D, D]), sb("onorm", [D, 1])
        ident, staps, sdiag = sb("ident_g", [D, D]), sb("staps", [D, SHORT]), sb("sdiag_g", [D, SHORT, D])
        eps = sb("eps_g", [D, 1])
        otile, short = sb("otile", [D, 2, S]), sb("short", [D, 2, S])
        hid = sb("hid_g", [128, S])
        NS = S // 128
        lg = sb("lg", [128, 4, NS * BRANCHES])
        small = sb("small", [128, 4, NS])
        flo = sb("flo", [128, NS])
        mix, part = sb("mix", [D, 2, T]), sb("part", [D, 2, BRANCHES, T])
        sq, rst = sb("sq_g", [D, 2, T]), sb("rst_g", [D, 2, T])
        p_a = ps("p_a", [D, 2, T])
        p_h = ps("p_h", [D, 2, T])
        p_w = ps("p_w", [D, BRANCHES, T])
        s_w, s_set, s_o = sem("g_weights"), sem("g_set"), [sem("g_o0"), sem("g_o1")]
        s_smm, s_short, s_h, s_hid, s_lg, s_soft, s_exp, s_pw, s_part, s_mix, s_sq, s_mean, s_log, s_rst, s_norm, s_proj, s_out = (
            sem("g_" + n) for n in ("smm", "short", "h", "hid", "lg", "soft", "exp", "pw", "part", "mix", "sq", "mean",
                                    "log", "rst", "norm", "proj", "out"))
        block = ctx.enter_context(nc.Block())
        SOFT = 12
        W = 2 * BRANCHES
        half = [slice(h * T, (h + 1) * T) for h in range(HALVES)]

        def from_third(b):
            return not isinstance(b, int) or b > 1

        @block.sync
        def _(sp):
            loads = ((w1[:, :, :], w["fg1"].rearrange("p (k n) -> p k n", k=BRANCHES)), (w2[:, :], w["fg2"][:, :]),
                     (b1[:, :], w["fg_b1"][:, :]), (b2[:, :], w["fg_b2"][:, :]), (temp[:, 0:1], w["logit_temp"][:, :]),
                     (headmean[:, :], w["headmean"][:, :]), (wo[:, :], w["o_proj"][:, :]), (onorm[:, :], w["o_norm"][:, :]),
                     (ident[:, :], w["ident"][:, :]), (staps[:, :], w["fir_short"][:, :]))
            for dst, src in loads:
                sp.dma_start(dst, src).then_inc(s_w, 16)

            def step(b, e, i):
                if from_third(b):
                    sp.wait_ge(s_part, W * (b - 1))
                src = O[:, :].rearrange("p (n c) -> p n c", c=B * CS)[:, :, bass.ds(b * CS, CS)]
                sp.dma_start(otile[:, e, :].rearrange("p (n c) -> p n c", c=CS), src).then_inc(s_o[e], 16)

            pipeline(sp, step)

        @block.tensor
        def _(pe):
            pe.wait_ge(s_w, 160)
            pe.wait_ge(s_set, 7)

            def spread(b, h):
                pe.wait_ge(s_soft, SOFT * (b + 1))
                if started(b) or h:
                    pe.wait_ge(s_part, W * b + BRANCHES * h)
                for g in range(BRANCHES):
                    for s in range(T // 128):
                        c = (h * (T // 128) + s) * BRANCHES + g
                        mm = nc.tensor.matmul(p_w[:, g, s * 128:(s + 1) * 128],
                                              lg[:, 3, c:c + 1].broadcast_to([128, 128]), ident[:, :],
                                              start=True, stop=True)
                    mm.then_inc(s_pw, 1)

            def short_fir(b, h):
                if from_third(b):
                    pe.wait_ge(s_out, 2 * (b - 2) + h + 1)
                elif started(b):
                    pe.wait_ge(s_short, 2 * (b - 1) + h + 1)
                for j in range(SHORT):
                    mm = nc.tensor.matmul(p_a[:, h, :], sdiag[:, j, :], seq_cols(V, b, h * T - (SHORT - 1) + j, T),
                                          start=(j == 0), stop=(j == SHORT - 1))
                mm.then_inc(s_smm, 1)

            def hidden(b, e, i, h):
                if h == 0:
                    pe.wait_ge(s_o[e], 16 * (i + 1))
                    if started(b):
                        pe.wait_ge(s_soft, SOFT * (b - 1) + 1)
                elif started(b):
                    pe.wait_ge(s_hid, 2 * b)
                pe.wait_ge(s_short, 2 * b + h + 1)
                srcs = (seq_cols(X, b, h * T, T), short[:, e, half[h]], L[:, bass.ds(b * S + h * T, T)], otile[:, e, half[h]])
                for k in range(BRANCHES):
                    mm = nc.tensor.matmul(p_h[:, h, :], w1[:, k, :], srcs[k], start=(k == 0), stop=(k == BRANCHES - 1))
                mm.then_inc(s_h, 1)

            def logits(b):
                pe.wait_ge(s_hid, 2 * (b + 1))
                for s in range(NS):
                    mm = nc.tensor.matmul(p_h[:, 0, s * BRANCHES:(s + 1) * BRANCHES], hid[:, s * 128:(s + 1) * 128],
                                          w2[:, :], start=True, stop=True)
                mm.then_inc(s_lg, 1)

            def mean(b, h):
                pe.wait_ge(s_sq, 2 * b + h + 1)
                if isinstance(b, int) and b == B - 1:
                    pe.wait_ge(s_out, 2 * (b - 1) + h + 1)
                else:
                    pe.wait_ge(s_short, 2 * (b + 1) + h + 1)
                nc.tensor.matmul(p_a[:, h, :], headmean[:, :], sq[:, h, :], start=True, stop=True).then_inc(s_mean, 1)

            def project(b, h):
                pe.wait_ge(s_log, 2 * b + h + 1)
                pe.wait_ge(s_norm, 2 * b + h + 1)
                nc.tensor.matmul(p_a[:, h, :], wo[:, :], mix[:, h, :], start=True, stop=True).then_inc(s_proj, 1)

            def step(b, e, i):
                late = not is_first(b)
                if late:
                    spread(b - 1, 0)
                short_fir(b, 0)
                short_fir(b, 1)
                if late:
                    spread(b - 1, 1)
                hidden(b, e, i, 0)
                hidden(b, e, i, 1)
                if late:
                    mean(b - 1, 0)
                logits(b)
                if late:
                    mean(b - 1, 1)
                    project(b - 1, 0)
                    project(b - 1, 1)

            def late(b):
                for part_ in (spread, mean, project):
                    part_(b, 0)
                    part_(b, 1)

            pipeline(pe, step, late)

        @block.scalar
        def _(act):
            nc.scalar.preload_act_table_set(LN_EXP)
            act.wait_ge(s_w, 160)
            act.wait_ge(s_set, 7)
            nc.scalar.activation(temp[:, 1:2], temp[:, 0:1], ACT.Abs).then_inc(s_set, 1)
            act.wait_ge(s_set, 8)
            nc.scalar.activation(temp[:, 1:2], temp[:, 1:2], ACT.Exp, scale=-1.0).then_inc(s_set, 1)
            act.wait_ge(s_set, 9)
            nc.scalar.activation(temp[:, 2:3], temp[:, 1:2], ACT.Ln, bias=1.0).then_inc(s_set, 1)
            act.wait_ge(s_set, 13)

            def square(b, h):
                act.wait_ge(s_mix, 6 * b + 3 * (h + 1))
                if started(b):
                    act.wait_ge(s_mean, 2 * (b - 1) + h + 1)
                nc.scalar.activation(sq[:, h, :], mix[:, h, :], ACT.Square).then_inc(s_sq, 1)

            def factor(b, h):
                act.wait_ge(s_mean, 2 * b + h + 1)
                if started(b):
                    act.wait_ge(s_norm, 2 * (b - 1) + h + 1)
                nc.scalar.activation(rst[:, h, :], p_a[:, h, :], ACT.Ln, bias=eps[:, 0:1]).then_inc(s_log, 1)
                act.wait_ge(s_log, 2 * b + h + 1)
                nc.scalar.activation(rst[:, h, :], rst[:, h, :], ACT.Exp, scale=-0.5).then_inc(s_rst, 1)

            def step(b, e, i):
                late = not is_first(b)
                for h in range(HALVES):
                    act.wait_ge(s_smm, 2 * b + h + 1)
                    if from_third(b):
                        act.wait_ge(s_part, W * (b - 1))
                        act.wait_ge(s_h, 2 * (b - 1))
                    nc.scalar.copy(short[:, e, half[h]], p_a[:, h, :]).then_inc(s_short, 1)
                if late:
                    square(b - 1, 0)
                for h in range(HALVES):
                    act.wait_ge(s_h, 2 * b + h + 1)
                    if late:
                        act.wait_ge(s_lg, b)
                    nc.scalar.activation(hid[:, half[h]], p_h[:, h, :], ACT.Gelu, bias=b1[:, 0:1]).then_inc(s_hid, 1)
                nc.scalar.preload_act_table_set(LN_EXP)
                if late:
                    square(b - 1, 1)
                    factor(b - 1, 0)
                act.wait_ge(s_soft, SOFT * b + 3)
                nc.scalar.activation(lg[:, 1, :], lg[:, 0, :], ACT.Exp, scale=temp[:, 3:4]).then_inc(s_exp, 1)
                if late:
                    factor(b - 1, 1)

            def late(b):
                for h in range(HALVES):
                    square(b, h)
                for h in range(HALVES):
                    factor(b, h)

            pipeline(act, step, late)

        @block.gpsimd
        def _(pool):
            def late(b):
                for h in range(HALVES):
                    pool.wait_ge(s_part, W * b + BRANCHES * h + 2)
                    if started(b):
                        pool.wait_ge(s_proj, 2 * (b - 1) + h + 1)
                    nc.gpsimd.tensor_tensor(mix[:, h, :], part[:, h, 0, :], part[:, h, 1, :], ALU.add).then_inc(s_mix, 1)
                    pool.wait_ge(s_part, W * b + BRANCHES * (h + 1))
                    nc.gpsimd.tensor_tensor(part[:, h, 2, :], part[:, h, 2, :], part[:, h, 3, :], ALU.add).then_inc(s_mix, 1)
                    pool.wait_ge(s_mix, 6 * b + 3 * h + 2)
                    nc.gpsimd.tensor_tensor(mix[:, h, :], mix[:, h, :], part[:, h, 2, :], ALU.add).then_inc(s_mix, 1)

            def step(b, e, i):
                if not is_first(b):
                    late(b - 1)

            pipeline(pool, step, late)

        @block.vector
        def _(dve):
            nc.vector.memset(eps[:, :], EPS).then_inc(s_set, 1)
            dve.wait_ge(s_w, 160)
            for j in range(SHORT):
                nc.vector.tensor_scalar(sdiag[:, j, :], ident[:, :], staps[:, j:j + 1], None, ALU.mult).then_inc(s_set, 1)
            for k in range(1, BRANCHES):
                nc.vector.tensor_scalar(w1[:, k, :], w1[:, k, :], 1.0 / H, None, ALU.mult).then_inc(s_set, 1)
            dve.wait_ge(s_set, 10)
            nc.vector.tensor_scalar(temp[:, 1:2], temp[:, 0:1], 0.0, None, ALU.max).then_inc(s_set, 1)
            dve.wait_ge(s_set, 11)
            nc.vector.scalar_tensor_tensor(out=temp[:, 2:3], in0=temp[:, 1:2], scalar=1e-4, in1=temp[:, 2:3],
                                           op0=ALU.add, op1=ALU.add).then_inc(s_set, 1)
            dve.wait_ge(s_set, 12)
            nc.vector.reciprocal(temp[:, 3:4], temp[:, 2:3]).then_inc(s_set, 1)
            view = lambda k: lg[:, k, :].rearrange("p (s g) -> p s g", g=BRANCHES)
            over = lambda x: x.unsqueeze(2).broadcast_to([128, NS, BRANCHES])
            step_ = [0]

            def chain(b, ins):
                step_[0] += 1
                ins.then_inc(s_soft, 1)
                dve.wait_ge(s_soft, SOFT * b + step_[0])

            def softmax_start(b):
                step_[0] = 0
                dve.wait_ge(s_lg, b + 1)
                logits = p_h[:, 0, 0:NS * BRANCHES].rearrange("p (s g) -> p s g", g=BRANCHES)
                chain(b, nc.vector.tensor_tensor(view(0), logits, b2[:, :].unsqueeze(1).broadcast_to([128, NS, BRANCHES]), ALU.add))
                chain(b, nc.vector.tensor_reduce(small[:, 0, :], view(0), AX.X, ALU.max))
                chain(b, nc.vector.tensor_tensor(view(0), view(0), over(small[:, 0, :]), ALU.subtract))

            def softmax_end(b):
                dve.wait_ge(s_exp, b + 1)
                chain(b, nc.vector.tensor_reduce(small[:, 1, :], view(1), AX.X, ALU.add))
                chain(b, nc.vector.reciprocal(small[:, 2, :], small[:, 1, :]))
                chain(b, nc.vector.tensor_tensor(view(2), view(1), over(small[:, 2, :]), ALU.mult))
                chain(b, nc.vector.tensor_scalar(flo[:, :], view(2)[:, :, 3], 0.05, None, ALU.mult))
                for g in range(2):
                    chain(b, nc.vector.tensor_tensor(view(2)[:, :, g], view(2)[:, :, g], flo[:, :], ALU.max))
                chain(b, nc.vector.tensor_reduce(small[:, 1, :], view(2), AX.X, ALU.add))
                chain(b, nc.vector.reciprocal(small[:, 3, :], small[:, 1, :]))
                if started(b):
                    dve.wait_ge(s_pw, W * b)
                chain(b, nc.vector.tensor_tensor(view(3), view(2), over(small[:, 3, :]), ALU.mult))

            def parts(b, e, h):
                srcs = (short[:, e, half[h]], L[:, bass.ds(b * S + h * T, T)], otile[:, e, half[h]], seq_cols(V, b, h * T, T))
                for g in range(BRANCHES):
                    dve.wait_ge(s_pw, W * b + BRANCHES * h + g + 1)
                    if g == 0 and started(b):
                        dve.wait_ge(s_mix, 6 * (b - 1) + 3 * (h + 1))
                    nc.vector.tensor_tensor(part[:, h, g, :], p_w[:, g, :], srcs[g], ALU.mult).then_inc(s_part, 1)

            def norm(b, h):
                dve.wait_ge(s_rst, 2 * b + h + 1)
                nc.vector.scalar_tensor_tensor(out=mix[:, h, :], in0=mix[:, h, :], scalar=onorm[:, 0:1],
                                               in1=rst[:, h, :], op0=ALU.mult, op1=ALU.mult).then_inc(s_norm, 1)

            def add(b, h):
                x = seq_cols(X, b, h * T, T)
                dve.wait_ge(s_proj, 2 * b + h + 1)
                nc.vector.tensor_tensor(x, x, p_a[:, h, :], ALU.add).then_inc(s_out, 1)

            def step(b, e, i):
                late = not is_first(b)
                if late:
                    parts(b - 1, 1 - e, 0)
                    parts(b - 1, 1 - e, 1)
                softmax_start(b)
                if late:
                    norm(b - 1, 0)
                softmax_end(b)
                if late:
                    norm(b - 1, 1)
                    add(b - 1, 0)
                    add(b - 1, 1)

            def late(b):
                e = b % 2
                parts(b, e, 0)
                parts(b, e, 1)
                for part_ in (norm, add):
                    part_(b, 0)
                    part_(b, 1)

            pipeline(dve, step, late)


NE = 32
FI = 256
FK = FI // 128
NT = B * S // 128
TPB = S // 128
SLOTS = NT + NE


def shared_and_logits(nc, X, XT, Y, LG, w, scratch):
    with ExitStack() as ctx:
        sb, ps, sem = alloc(nc, ctx)
        gate_w = sb("gate_w", [D, NE])
        wg, wu, wd = sb("swg", [D, FI]), sb("swu", [D, FI]), sb("swd", [128, FK, D])
        ident = sb("ident_m", [D, D])
        zeros = sb("zeros", [128, 8 * D])
        xs = sb("xs", [D, S])
        sg, hs = sb("sg", [128, 2, FK, T]), sb("hs", [128, 2, FK, T])
        p_l = ps("p_l", [128, TPB, NE])
        p_t = ps("p_t", [128, TPB, D])
        p_g, p_u = ps("p_g", [128, FK, T]), ps("p_u2", [128, FK, T])
        p_d = ps("p_d", [128, T // 128, D])
        s_w, s_zero, s_clear = sem("m_weights"), sem("m_zero"), sem("m_clear")
        s_xs, s_l, s_t, s_lg, s_xt, s_g, s_u, s_sg, s_hs, s_d, s_y = (
            sem("m_" + n) for n in ("xs", "l", "t", "lg", "xt", "g", "u", "sg", "hs", "d", "y"))
        block = ctx.enter_context(nc.Block())

        @block.sync
        def _(sp):
            loads = ((gate_w[:, :], w["gate_w"][:, :]), (wg[:, :], w["sg"][:, :]), (wu[:, :], w["su"][:, :]),
                     (wd[:, :, :], w["sd"].rearrange("(k p) n -> p k n", p=128)), (ident[:, :], w["ident"][:, :]))
            for dst, src in loads:
                sp.dma_start(dst, src).then_inc(s_w, 16)
            sp.wait_ge(s_zero, 1)
            for i in range(SLOTS // 8):
                dst = scratch["slots"][i * 1024:(i + 1) * 1024, :].rearrange("(p r) d -> p (r d)", p=128)
                sp.dma_start(dst, zeros[:, :]).then_inc(s_clear, 16)
            sp.wait_ge(s_clear, 16 * (SLOTS // 8))

        @block.gpsimd
        def _(pool):
            nc.gpsimd.memset(zeros[:, :], 0.0).then_inc(s_zero, 1)

        @block.tensor
        def _(pe):
            pe.wait_ge(s_w, 80)

            def body(b):
                first = is_first(b)
                pe.wait_ge(s_xs, b + 1)
                if not first:
                    pe.wait_ge(s_lg, b)
                    pe.wait_ge(s_xt, b)
                for s in range(TPB):
                    mm = nc.tensor.matmul(p_l[:, s, :], xs[:, s * 128:(s + 1) * 128], gate_w[:, :], start=True, stop=True)
                mm.then_inc(s_l, 1)
                for s in range(TPB):
                    mm = nc.tensor.transpose(p_t[:, s, :], xs[:, s * 128:(s + 1) * 128], ident[:, :])
                mm.then_inc(s_t, 1)
                for h in range(2):
                    for k in range(FK):
                        i = FK * (2 * b + h) + k
                        if not first or h:
                            pe.wait_ge(s_sg, i - 1)
                            pe.wait_ge(s_hs, i - 1)
                        x = xs[:, h * T:(h + 1) * T]
                        nc.tensor.matmul(p_g[:, k, :], wg[:, k * 128:(k + 1) * 128], x, start=True, stop=True).then_inc(s_g, 1)
                        nc.tensor.matmul(p_u[:, k, :], wu[:, k * 128:(k + 1) * 128], x, start=True, stop=True).then_inc(s_u, 1)
                for h in range(2):
                    t = 2 * b + h
                    pe.wait_ge(s_hs, FK * (t + 1))
                    if not first or h:
                        pe.wait_ge(s_y, t)
                    for s in range(T // 128):
                        for k in range(FK):
                            mm = nc.tensor.matmul(p_d[:, s, :], hs[:, h, k, s * 128:(s + 1) * 128], wd[:, k, :],
                                                  start=(k == 0), stop=(k == FK - 1))
                    mm.then_inc(s_d, 1)

            loop(pe, B, body)

        @block.scalar
        def _(act):
            def body(b):
                for h in range(2):
                    for k in range(FK):
                        i = FK * (2 * b + h) + k
                        act.wait_ge(s_g, i + 1)
                        if not is_first(b):
                            act.wait_ge(s_hs, i - 3)
                        nc.scalar.activation(sg[:, h, k, :], p_g[:, k, :], ACT.Silu).then_inc(s_sg, 1)

            loop(act, B, body)

        @block.vector
        def _(dve):
            def body(b):
                first = is_first(b)
                if not first:
                    dve.wait_ge(s_t, b)
                    dve.wait_ge(s_g, 4 * b)
                    dve.wait_ge(s_u, 4 * b)
                nc.vector.tensor_scalar(xs[:, :], seq_cols(X, b, 0, S), 1.0, None, ALU.mult).then_inc(s_xs, 1)
                dve.wait_ge(s_l, b + 1)
                nc.vector.tensor_scalar(LG[:, bass.ds(b * TPB, TPB), :], p_l[:, :, :], 1.0, None, ALU.mult).then_inc(s_lg, 1)
                dve.wait_ge(s_t, b + 1)
                nc.vector.tensor_scalar(XT[:, bass.ds(b * TPB, TPB), :], p_t[:, :, :], 1.0, None, ALU.mult).then_inc(s_xt, 1)
                for h in range(2):
                    for k in range(FK):
                        i = FK * (2 * b + h) + k
                        dve.wait_ge(s_sg, i + 1)
                        dve.wait_ge(s_u, i + 1)
                        if not first:
                            dve.wait_ge(s_d, 2 * b + h - 1)
                        nc.vector.tensor_tensor(hs[:, h, k, :], sg[:, h, k, :], p_u[:, k, :], ALU.mult).then_inc(s_hs, 1)
                dve.wait_ge(s_xt, b + 1)
                for h in range(2):
                    dve.wait_ge(s_d, 2 * b + h + 1)
                    at = bass.ds(b * TPB + h * (T // 128), T // 128)
                    nc.vector.tensor_tensor(Y[:, at, :], XT[:, at, :], p_d[:, :, :], ALU.add).then_inc(s_y, 1)

            loop(dve, B, body)


def route(nc, XT, LG, POS, w, scratch, TE):
    with ExitStack() as ctx:
        sb, ps, sem = alloc(nc, ctx)
        N = NT * NE
        down = sb("down", [128, NE])
        before, ones = sb("before", [128, 128], BF16), sb("ones_b", [128, 128], BF16)
        restart = sb("restart", [128, NE, NT])
        top, score = sb("top", [128, NT]), sb("score", [128, NT])
        cand, oneh = sb("cand", [128, NT, NE]), sb("oneh", [128, NT, NE])
        onehb = sb("onehb", [128, NT, NE], BF16)
        best = sb("best", [128, NT])
        count, prefix = sb("count", [128, NE, NT]), sb("prefix", [128, NE, NT])
        tot, toti = sb("tot", [128, NE]), sb("toti", [128, NE], I32)
        padded, ends, begins, onef = (sb(n, [128, NE]) for n in ("padded", "ends", "begins", "onef"))
        posf = sb("posf", [128, NT])
        starts, cmp, tef = sb("starts", [1, SLOTS]), sb("cmp", [1, SLOTS, NE]), sb("tef", [1, SLOTS])
        p_r, p_c = ps("p_r", [128, NT, NE]), ps("p_c2", [128, NT, NE])
        s_w, s_one, s_r, s_c, s_score, s_d, s_scaled, s_sent = (
            sem("r_" + n) for n in ("weights", "onehot", "rank", "count", "score", "dve", "scaled", "sent"))
        block = ctx.enter_context(nc.Block())
        bc = lambda x: x.unsqueeze(2).broadcast_to([128, NT, NE])
        rows = lambda x: x.unsqueeze(1).broadcast_to([128, NT, NE])
        TOP, SLOT = 1, 100

        @block.sync
        def _(sp):
            loads = ((down[:, :], w["down"][:, :]), (before[:, :].bitcast(U16), w["before"][:, :]), (ones[:, :].bitcast(U16), w["ones"][:, :]),
                     (restart[:, :, :], w["restart"].rearrange("p (e t) -> p e t", t=NT)), (starts[:, :], w["starts"][:, :]))
            for dst, src in loads:
                sp.dma_start(dst, src).then_inc(s_w, 16)

        @block.tensor
        def _(pe):
            pe.wait_ge(s_one, 1)
            flat = lambda t: t[:, :, :].rearrange("p t e -> p (t e)")
            for q in range(N // T):
                c = slice(q * T, (q + 1) * T)
                mm = nc.tensor.matmul(flat(p_c)[:, c], ones[:, :], flat(onehb)[:, c], start=True, stop=True)
            mm.then_inc(s_c, 1)
            for q in range(N // T):
                c = slice(q * T, (q + 1) * T)
                mm = nc.tensor.matmul(flat(p_r)[:, c], before[:, :], flat(onehb)[:, c], start=True, stop=True)
            mm.then_inc(s_r, 1)

        @block.scalar
        def _(act):
            act.wait_ge(s_d, 1)
            nc.scalar.activation(score[:, :], top[:, :], ACT.Sigmoid).then_inc(s_score, 1)

        @block.vector
        def _(dve):
            count_ = [0]

            def chain(ins):
                count_[0] += 1
                ins.then_inc(s_d, 1)
                dve.wait_ge(s_d, count_[0])

            dve.wait_ge(s_w, 80)
            chain(nc.vector.tensor_reduce(top[:, :], LG[:, :, :], AX.X, ALU.max))
            chain(nc.vector.tensor_tensor(cand[:, :, :], LG[:, :, :], bc(top[:, :]), ALU.is_equal))
            chain(nc.vector.tensor_tensor(cand[:, :, :], cand[:, :, :], rows(down[:, :]), ALU.mult))
            chain(nc.vector.tensor_reduce(best[:, :], cand[:, :, :], AX.X, ALU.max))
            chain(nc.vector.tensor_tensor(oneh[:, :, :], bc(best[:, :]), rows(down[:, :]), ALU.is_equal))
            nc.vector.tensor_copy(onehb[:, :, :], oneh[:, :, :]).then_inc(s_one, 1)
            chain(nc.vector.memset(onef[:, :], 1.0))
            dve.wait_ge(s_c, 1)
            chain(nc.vector.tensor_copy(count[:, :, :], p_c[:, :, :].rearrange("p t e -> p e t")))
            flat = lambda t: t[:, :, :].rearrange("p e t -> p (e t)")
            chain(nc.vector.tensor_tensor_scan(flat(prefix), flat(restart), flat(count), 0.0, ALU.mult, ALU.add))
            chain(nc.vector.tensor_scalar(tot[:, :], prefix[:, :, NT - 1], 127.0, None, ALU.add))
            chain(nc.vector.tensor_copy(toti[:, :], tot[:, :]))
            chain(nc.vector.tensor_scalar(toti[:, :], toti[:, :], 7, 7, ALU.arith_shift_right, ALU.logical_shift_left))
            chain(nc.vector.tensor_copy(padded[:, :], toti[:, :]))
            chain(nc.vector.tensor_tensor_scan(ends[:, :], onef[:, :], padded[:, :], 0.0, ALU.mult, ALU.add))
            chain(nc.vector.tensor_tensor(begins[:, :], ends[:, :], padded[:, :], ALU.subtract))
            chain(nc.vector.tensor_tensor(prefix[:, :, :], prefix[:, :, :], count[:, :, :], ALU.subtract))
            chain(nc.vector.tensor_tensor(prefix[:, :, :], prefix[:, :, :],
                                          begins[:, :].unsqueeze(2).broadcast_to([128, NE, NT]), ALU.add))
            dve.wait_ge(s_r, 1)
            chain(nc.vector.tensor_tensor(cand[:, :, :], p_r[:, :, :], prefix[:, :, :].rearrange("p e t -> p t e"), ALU.add))
            chain(nc.vector.tensor_tensor(cand[:, :, :], cand[:, :, :], oneh[:, :, :], ALU.mult))
            chain(nc.vector.tensor_reduce(posf[:, :], cand[:, :, :], AX.X, ALU.add))
            chain(nc.vector.tensor_copy(POS[:, :], posf[:, :]))
            chain(nc.vector.tensor_tensor(cmp[:, :, :], ends[0:1, :].unsqueeze(1).broadcast_to([1, SLOTS, NE]),
                                          starts[:, :].unsqueeze(2).broadcast_to([1, SLOTS, NE]), ALU.is_le))
            chain(nc.vector.tensor_reduce(tef[:, :], cmp[:, :, :], AX.X, ALU.add))
            chain(nc.vector.tensor_scalar(tef[:, :], tef[:, :], float(NE - 1), None, ALU.min))
            chain(nc.vector.tensor_copy(TE[:, :], tef[:, :]))
            dve.wait_ge(s_score, 1)
            for q in range(4):
                c = slice(q * NT // 4, (q + 1) * NT // 4)
                nc.vector.tensor_tensor(XT[:, c, :], XT[:, c, :],
                                        score[:, c].unsqueeze(2).broadcast_to([128, NT // 4, D]), ALU.mult).then_inc(s_scaled, 1)

        @block.gpsimd
        def _(pool):
            for t in range(NT):
                if t % (NT // 4) == 0:
                    pool.wait_ge(s_scaled, t // (NT // 4) + 1)
                pool.indirect_dma_start(out=scratch["slots"][:, :],
                                        out_offset=bass.IndirectOffsetOnAxis(ap=POS[:, t:t + 1], axis=0),
                                        in_=XT[:, t, :], in_offset=None).then_inc(s_sent, 16)
            pool.wait_ge(s_sent, 16 * NT)


def experts(nc, w, scratch, TE):
    with ExitStack() as ctx:
        sb, ps, sem = alloc(nc, ctx)
        WE = 2 * FI + FK * D
        wts = sb("wts", [128, 2, WE])
        xin, xt = sb("xin", [128, 2, D]), sb("xt_e", [D, 2, 128])
        sg, hs, ys = sb("sg_e", [128, 2, FK, 128]), sb("hs_e", [128, 2, FK, 128]), sb("ys", [128, 2, D])
        ident = sb("ident_e", [D, D])
        p_t = [ps(f"p_te{i}", [128, T]) for i in range(2)]
        p_gu = [ps(f"p_gu{i}", [128, 2 * FK, 128]) for i in range(2)]
        p_y = [ps(f"p_ye{i}", [128, T]) for i in range(2)]
        s_id = sem("e_ident")
        s_w, s_x, s_out = ([sem(f"e_{n}{i}") for i in range(2)] for n in ("w", "x", "out"))
        s_t, s_xt, s_gu, s_sg, s_hs, s_y, s_ys = (sem("e_" + n) for n in ("t", "xt", "gu", "sg", "hs", "y", "ys"))
        block = ctx.enter_context(nc.Block())

        def pairs(eng, body):
            body(0)
            with eng.Fori(1, SLOTS // 2) as i:
                body(i)

        @block.sync
        def _(sp):
            sp.dma_start(ident[:, :], w["ident"][:, :]).then_inc(s_id, 16)

            def body(i):
                for e in range(2):
                    m = 2 * i + e
                    number = sp.value_load(TE[0:1, m:m + 1] if isinstance(m, int) else TE[0:1, bass.ds(m, 1)],
                                           min_val=0, max_val=NE - 1)
                    if not is_first(i):
                        sp.wait_ge(s_y, m - 1)
                    sp.dma_start(wts[:, e, :], w["experts"][bass.ds(number, 1), :, :].rearrange("e p c -> (e p) c")
                                 ).then_inc(s_w[e], 16)

            pairs(sp, body)

        @block.gpsimd
        def _(pool):
            def body(i):
                for e in range(2):
                    m = 2 * i + e
                    if not is_first(i):
                        pool.wait_ge(s_t, m - 1)
                    pool.dma_start(xin[:, e, :], scratch["slots"][bass.ds(m * 128, 128), :]).then_inc(s_x[e], 16)

            pairs(pool, body)

        @block.tensor
        def _(pe):
            pe.wait_ge(s_id, 16)

            def turn(m, i, e, start):
                pe.wait_ge(s_x[e], 16 * (i + 1))
                if not start:
                    pe.wait_ge(s_xt, m - 1)
                nc.tensor.transpose(p_t[e][:, 0:128], xin[:, e, :], ident[:, :]).then_inc(s_t, 1)

            def body(i):
                for e in range(2):
                    turn(2 * i + e, i, e, is_first(i))
                for e in range(2):
                    m = 2 * i + e
                    pe.wait_ge(s_xt, m + 1)
                    pe.wait_ge(s_w[e], 16 * (i + 1))
                    if not is_first(i):
                        pe.wait_ge(s_sg, m - 1)
                        pe.wait_ge(s_hs, m - 1)
                    for k in range(2 * FK):
                        mm = nc.tensor.matmul(p_gu[e][:, k, :], wts[:, e, k * 128:(k + 1) * 128], xt[:, e, :],
                                              start=True, stop=True)
                    mm.then_inc(s_gu, 1)
                for e in range(2):
                    m = 2 * i + e
                    pe.wait_ge(s_hs, m + 1)
                    if not is_first(i):
                        pe.wait_ge(s_ys, m - 1)
                    for k in range(FK):
                        mm = nc.tensor.matmul(p_y[e][:, 0:D], hs[:, e, k, :],
                                              wts[:, e, 2 * FI + k * D:2 * FI + (k + 1) * D],
                                              start=(k == 0), stop=(k == FK - 1))
                    mm.then_inc(s_y, 1)

            pairs(pe, body)

        @block.scalar
        def _(act):
            def body(i):
                for e in range(2):
                    m = 2 * i + e
                    act.wait_ge(s_gu, m + 1)
                    if not is_first(i):
                        act.wait_ge(s_hs, m - 1)
                    nc.scalar.activation(sg[:, e, :, :], p_gu[e][:, 0:FK, :], ACT.Silu).then_inc(s_sg, 1)
                for e in range(2):
                    m = 2 * i + e
                    act.wait_ge(s_ys, m + 1)
                    act.dma_start(scratch["results"][bass.ds(m * 128, 128), :], ys[:, e, :]).then_inc(s_out[e], 16)

            pairs(act, body)
            for e in range(2):
                act.wait_ge(s_out[e], 16 * (SLOTS // 2))

        @block.vector
        def _(dve):
            def body(i):
                for e in range(2):
                    m = 2 * i + e
                    dve.wait_ge(s_t, m + 1)
                    if not is_first(i):
                        dve.wait_ge(s_gu, m - 1)
                    nc.vector.tensor_copy(xt[:, e, :], p_t[e][:, 0:128]).then_inc(s_xt, 1)
                for e in range(2):
                    m = 2 * i + e
                    dve.wait_ge(s_sg, m + 1)
                    if not is_first(i):
                        dve.wait_ge(s_y, m - 1)
                    nc.vector.tensor_tensor(hs[:, e, :, :], sg[:, e, :, :], p_gu[e][:, FK:2 * FK, :],
                                            ALU.mult).then_inc(s_hs, 1)
                for e in range(2):
                    m = 2 * i + e
                    dve.wait_ge(s_y, m + 1)
                    if not is_first(i):
                        dve.wait_ge(s_out[e], 16 * i)
                    nc.vector.tensor_copy(ys[:, e, :], p_y[e][:, 0:D]).then_inc(s_ys, 1)

            pairs(dve, body)


def combine(nc, Y, POS, out, scratch):
    with ExitStack() as ctx:
        sb, _, sem = alloc(nc, ctx)
        G = sb("G", [128, NT, D])
        eps = sb("eps_o", [128, 1])
        sums, var, rstd = sb("sums", [128, 2, TPB]), sb("var", [128, 2, TPB]), sb("rstd_o", [128, 2, TPB])
        cen, sq = sb("cen", [128, 2, TPB, D]), sb("sq_o", [128, 2, TPB, D])
        s_g, s_eps, s_add, s_sum, s_cen, s_sq, s_var, s_ln, s_rstd, s_done = (
            sem("z_" + n) for n in ("gathered", "eps", "add", "sum", "cen", "sq", "var", "ln", "rstd", "done"))
        s_out = [sem("z_out0"), sem("z_out1")]
        block = ctx.enter_context(nc.Block())
        dst = out.rearrange("(b t p) d -> b p t d", t=TPB, p=128)
        over = lambda x: x.unsqueeze(2).broadcast_to([128, TPB, D])

        @block.gpsimd
        def _(pool):
            for t in range(NT):
                pool.indirect_dma_start(out=G[:, t, :], out_offset=None, in_=scratch["results"][:, :],
                                        in_offset=bass.IndirectOffsetOnAxis(ap=POS[:, t:t + 1], axis=0)).then_inc(s_g, 16)
                if t % TPB == TPB - 1:
                    pool.wait_ge(s_g, 16 * (t + 1))

        @block.sync
        def _(sp):
            for b in range(B):
                sp.wait_ge(s_done, b + 1)
                sp.dma_start(dst[b], cen[:, b % 2, :, :]).then_inc(s_out[b % 2], 16)
            for e in range(2):
                sp.wait_ge(s_out[e], 16 * B // 2)

        @block.scalar
        def _(act):
            act.wait_ge(s_eps, 1)
            for b in range(B):
                e = b % 2
                act.wait_ge(s_cen, b + 1)
                if b >= 2:
                    act.wait_ge(s_var, b - 1)
                nc.scalar.activation(sq[:, e, :, :], cen[:, e, :, :], ACT.Square).then_inc(s_sq, 1)
                act.wait_ge(s_var, b + 1)
                nc.scalar.activation(var[:, e, :], var[:, e, :], ACT.Ln, bias=eps[:, 0:1], scale=1.0 / D).then_inc(s_ln, 1)
                act.wait_ge(s_ln, b + 1)
                if b >= 2:
                    act.wait_ge(s_done, b - 1)
                nc.scalar.activation(rstd[:, e, :], var[:, e, :], ACT.Exp, scale=-0.5).then_inc(s_rstd, 1)

        @block.vector
        def _(dve):
            nc.vector.memset(eps[:, :], EPS).then_inc(s_eps, 1)

            def centre(b):
                e = b % 2
                c = slice(b * TPB, (b + 1) * TPB)
                dve.wait_ge(s_g, 16 * TPB * (b + 1))
                nc.vector.tensor_tensor(G[:, c, :], G[:, c, :], Y[:, c, :], ALU.add).then_inc(s_add, 1)
                dve.wait_ge(s_add, b + 1)
                nc.vector.tensor_reduce(sums[:, e, :], G[:, c, :], AX.X, ALU.add).then_inc(s_sum, 1)
                dve.wait_ge(s_sum, 2 * b + 1)
                nc.vector.tensor_scalar(sums[:, e, :], sums[:, e, :], 1.0 / D, None, ALU.mult).then_inc(s_sum, 1)
                dve.wait_ge(s_sum, 2 * b + 2)
                if b >= 2:
                    dve.wait_ge(s_out[e], 16 * (b // 2))
                nc.vector.tensor_tensor(cen[:, e, :, :], G[:, c, :], over(sums[:, e, :]), ALU.subtract).then_inc(s_cen, 1)

            def scale(b):
                e = b % 2
                dve.wait_ge(s_sq, b + 1)
                nc.vector.tensor_reduce(var[:, e, :], sq[:, e, :, :], AX.X, ALU.add).then_inc(s_var, 1)
                dve.wait_ge(s_rstd, b + 1)
                nc.vector.tensor_tensor(cen[:, e, :, :], cen[:, e, :, :], over(rstd[:, e, :]), ALU.mult).then_inc(s_done, 1)

            for b in range(B):
                centre(b)
                if b:
                    scale(b - 1)
            scale(B - 1)


def clear_semaphores(nc):
    nc.all_engine_barrier()
    nc.gpsimd.sem_clear(range(min(nc.free_semaphores), max(nc.free_semaphores) + 1))
    nc.all_engine_barrier()


def build(nc, w, out, stages):
    with ExitStack() as ctx:
        X = ctx.enter_context(nc.sbuf_tensor("X", [D, B * ROW], F32))
        with ExitStack() as c1:
            sb, _, _ = alloc(nc, c1)
            dt, dtx, parts = sb("dt", [D, B * S]), sb("dtx", [D, B * S]), sb("parts", [96, B * S], BF16)
            scan_inputs(nc, X, dt, dtx, parts, w)
            selective_scan(nc, X, dt, dtx, parts, w)
        layer_norm(nc, X, w, "n1")
        if stages >= 2:
            ternary_ffn(nc, X, w)
            layer_norm(nc, X, w, "n2")
        if stages >= 3:
            scratch = {
                "upper": nc.dram_tensor("upper_scratch", (H, NC_, CS, CS), F32, kind="Internal").ap(),
                "records": nc.dram_tensor("record_scratch", (NC_, D, B * REC), F32, kind="Internal").ap(),
            }
            with ExitStack() as c3:
                sb, _, _ = alloc(nc, c3)
                V, L = sb("V", [D, B * ROW]), sb("L", [D, B * S])
                delta_inputs(nc, X, V, L, w, scratch)
                with ExitStack() as c4:
                    O = c4.enter_context(nc.sbuf_tensor("O", [D, B * S], F32))
                    delta_scan(nc, O, w, scratch)
                    gate_mix(nc, X, V, L, O, w)
            layer_norm(nc, X, w, "n3")
        clear_semaphores(nc)
        scratch["slots"] = nc.dram_tensor("slot_scratch", (SLOTS * 128, D), F32, kind="Internal").ap()
        scratch["results"] = nc.dram_tensor("result_scratch", (SLOTS * 128, D), F32, kind="Internal").ap()
        with ExitStack() as c5:
            sb, _, _ = alloc(nc, c5)
            Y = sb("Y", [128, NT, D])
            POS, TE = sb("POS", [128, NT], U32), sb("TE", [1, SLOTS], I32)
            with ExitStack() as c6:
                sb, _, _ = alloc(nc, c6)
                XT, LG = sb("XT", [128, NT, D]), sb("LG", [128, NT, NE])
                shared_and_logits(nc, X, XT, Y, LG, w, scratch)
                route(nc, XT, LG, POS, w, scratch, TE)
            experts(nc, w, scratch, TE)
            combine(nc, Y, POS, out, scratch)


STAGES = 3


def bf16_ones(where):
    return np.where(where, 0x3F80, 0).astype(np.uint16)


def lay_out(inputs):
    g = {k: np.ascontiguousarray(v) for k, v in inputs.items()}
    col = lambda v: np.ascontiguousarray(v.reshape(-1, 128).T)
    T_ = lambda v: np.ascontiguousarray(v.T)
    a = {}
    a["x"] = T_(g["L0_attn_x"].reshape(B * S, D))
    wx = g["L0_attn_W_xproj"]
    a["bc"] = np.ascontiguousarray(np.concatenate([wx[:, :32]] * 3, axis=1))
    a["low"] = np.ascontiguousarray(wx[:, 32:])
    a["dt"] = g["L0_attn_W_dt"]
    a["b_dt"] = col(g["L0_attn_b_dt"])
    a["A_log"] = T_(g["L0_attn_A_log"])
    for n in ("w1", "w2", "h1", "h2", "w3"):
        a[n] = T_(g[f"L0_ffn_{n}_w"])
    a["ffn_scales"] = np.ascontiguousarray(np.concatenate([col(g[f"L0_ffn_{n}_s"]) for n in ("w1", "w2", "h1", "h2", "w3")], axis=1))
    rep = lambda v, n=128: np.ascontiguousarray(np.broadcast_to(v.reshape(1, -1), (n, v.size)))
    for n in "qkv":
        a[n + "_proj"] = T_(g[f"L1_attn_{n}_proj_w"])
        a[n + "_conv"] = rep(g[f"L1_attn_{n}_conv_w"].T)
    a["b_proj"] = np.ascontiguousarray(np.repeat(g["L1_attn_b_proj_w"].T, DH, axis=1))
    a["fir_long"] = np.ascontiguousarray(g["L1_attn_fir_long_w"].reshape(D, LONG))
    a["fir_short"] = np.ascontiguousarray(g["L1_attn_fir_short_w"].reshape(D, SHORT))
    fg = g["L1_attn_fg_w1"].T
    a["fg1"] = np.ascontiguousarray(np.concatenate([fg[:D]] + [np.tile(fg[D + DH * i:D + DH * (i + 1)], (H, 1)) for i in range(3)], axis=1))
    a["fg2"] = np.ascontiguousarray(g["L1_attn_fg_w2"].T)
    a["fg_b1"] = col(g["L1_attn_fg_b1"])
    a["fg_b2"] = rep(g["L1_attn_fg_b2"])
    a["logit_temp"] = rep(g["L1_attn_logit_temp"])
    a["o_proj"] = T_(g["L1_attn_o_proj_w"])
    a["o_norm"] = np.ascontiguousarray(np.tile(g["L1_attn_o_norm_w"], H).reshape(D, 1))
    a["gate_w"] = g["L1_ffn_gate_w"]
    a["sg"], a["su"], a["sd"] = (g[f"L1_ffn_shared_{n}_w"] for n in ("gate", "up", "down"))
    rd = g["L1_ffn_routed_down_w"].reshape(NE, FK, 128, D).transpose(0, 2, 1, 3).reshape(NE, 128, FK * D)
    a["experts"] = np.ascontiguousarray(np.concatenate([g["L1_ffn_routed_gate_w"], g["L1_ffn_routed_up_w"], rd], axis=2))
    i128 = np.arange(128)
    a["down"] = np.ascontiguousarray(np.broadcast_to((NE - np.arange(NE)).astype(np.float32), (128, NE)))
    a["before"] = bf16_ones(i128[:, None] < i128[None, :])
    a["ones"] = bf16_ones(np.ones((128, 128), bool))
    a["restart"] = np.ascontiguousarray(np.broadcast_to((np.arange(NE * NT) % NT != 0).astype(np.float32), (128, NE * NT)))
    a["starts"] = (128.0 * np.arange(SLOTS)).astype(np.float32).reshape(1, SLOTS)
    i32 = np.arange(32)
    a["keep_lt"] = np.tile((i32[:, None] < i32[None, :]).astype(np.float32), (H, 1))
    a["keep_le"] = np.tile((i32[:, None] <= i32[None, :]).astype(np.float32), (H, 1))
    a["headsum"] = np.kron(np.eye(H, dtype=np.float32), np.ones((DH, DH), np.float32))
    a["headmean"] = np.kron(np.eye(H, dtype=np.float32), np.full((DH, DH), 1.0 / DH, np.float32))
    a["eye32"] = np.ascontiguousarray(np.broadcast_to(np.eye(32, dtype=np.float32).reshape(1, -1), (128, 1024)))

    r = np.arange(96)
    a["select"] = np.ascontiguousarray(np.broadcast_to(bf16_ones((r[:, None] % 32 == np.arange(32)[None, :])[:, :, None]), (96, 32, 128)))
    a["ident"] = np.eye(128, dtype=np.float32)
    a["mean_w"] = np.full((128, 128), 1.0 / D, np.float32)
    return a


def kernel(**inputs):
    import concourse.bacc as bacc
    from concourse.bass_utils import run_bass_kernel_spmd

    a = lay_out(inputs)
    nc = bacc.Bacc("TRN2", target_bir_lowering=False, num_devices=1)
    w = {k: nc.dram_tensor("in_" + k, v.shape, mybir.dt.from_np(v.dtype), kind="ExternalInput").ap() for k, v in a.items()}
    out = nc.dram_tensor("out_x", (B * S, D), F32, kind="ExternalOutput").ap()
    build(nc, w, out, STAGES)
    r = run_bass_kernel_spmd(nc, [{"in_" + k: v for k, v in a.items()}], core_ids=[0])
    return r.results[0]["out_x"].reshape(B, S, D)
```

```python
from contextlib import ExitStack

import numpy as np

import concourse.bass as bass
from concourse import mybir

F32 = mybir.dt.float32
BF16 = mybir.dt.bfloat16
I32 = mybir.dt.int32
U32 = mybir.dt.uint32
U16 = mybir.dt.uint16
ALU = mybir.AluOpType
ACT = mybir.ActivationFunctionType
AX = mybir.AxisListType

D = 128
B = 8
S = 1024
T = 512
HALVES = S // T
PAD = 4
ROW = PAD + S
LAG = 3
READS = 4
NSTATE = 16
DTR = 64
HID = 512
KT = HID // 128
EPS = 1e-5
LN_EXP = "natural_log_exp_and_others"


def alloc(nc, ctx):
    def sb(name, shape, dt=F32):
        return ctx.enter_context(nc.sbuf_tensor(name, shape, dt))

    def ps(name, shape, dt=F32):
        return ctx.enter_context(nc.psum_tensor(name, shape, dt))

    def sem(name):
        return ctx.enter_context(nc.semaphore(name))

    return sb, ps, sem


def loop(eng, n, body):
    body(0)
    with eng.Fori(1, n) as i:
        body(i)


def is_first(i):
    return isinstance(i, int) and i == 0


def started(b):
    return not isinstance(b, int) or b > 0


def pipeline(eng, step, late=None):
    for b in range(2):
        step(b, b, 0)
    with eng.Fori(1, B // 2) as i:
        for e in range(2):
            step(2 * i + e, e, i)
    if late:
        late(B - 1)


def seq_cols(X, b, lo, n):
    return X[:, bass.ds(b * ROW + (PAD + lo), n)]


def scan_inputs(nc, X, dt, dtx, parts, w):
    with ExitStack() as ctx:
        sb, ps, sem = alloc(nc, ctx)
        wbc, wr, wdt = sb("wbc", [D, 96]), sb("wr", [D, DTR]), sb("wdt", [DTR, D])
        bdt = sb("bdt", [D, 1])
        low = sb("low", [DTR, 2, T])
        rest, mid = sb("rest", [96, 2, T]), sb("mid", [96, 2, T], BF16)
        absz, expz, lnz, posz = (sb(n, [D, 2, T]) for n in ("absz", "expz", "lnz", "posz"))
        p_bc, p_low, p_z = ps("p_bc", [96, 2, T]), ps("p_low", [DTR, 2, T]), ps("p_z", [D, 2, T])
        s_w, s_x, s_xrest, s_pad = sem("a_weights"), sem("a_x"), sem("a_xrest"), sem("a_pad")
        s_proj, s_low, s_z = sem("a_proj"), sem("a_low"), sem("a_z")
        s_hi, s_rest, s_mid, s_rest2, s_parts = sem("a_hi"), sem("a_rest"), sem("a_mid"), sem("a_rest2"), sem("a_parts")
        s_abs, s_exp, s_ln, s_pos, s_dt, s_dtx = (sem(n) for n in ("a_abs", "a_exp", "a_ln", "a_pos", "a_dt", "a_dtx"))
        block = ctx.enter_context(nc.Block())

        @block.sync
        def _(sp):
            for dst, src in ((wbc, w["bc"]), (wr, w["low"]), (wdt, w["dt"]), (bdt, w["b_dt"])):
                sp.dma_start(dst[:, :], src[:, :]).then_inc(s_w, 16)
            x, src = X[:, :].rearrange("p (b c) -> p b c", c=ROW), w["x"].rearrange("p (b c) -> p b c", c=S)
            sp.dma_start(x[:, 0, PAD:ROW], src[:, 0, :]).then_inc(s_x, 16)
            sp.dma_start(x[:, 1:B, PAD:ROW], src[:, 1:B, :]).then_inc(s_xrest, 16)

        @block.gpsimd
        def _(pool):
            nc.gpsimd.memset(X[:, :].rearrange("p (b c) -> p b c", c=ROW)[:, :, 0:PAD], 0.0).then_inc(s_pad, 1)
            pool.wait_ge(s_pad, 1)

            def body(b):
                cols = bass.ds(b * S, S)
                pool.wait_ge(s_mid, 2 * (b + 1))
                if not is_first(b):
                    pool.wait_ge(s_dtx, b)
                pool.nop()
                nc.gpsimd.tensor_copy(parts[32:64, cols], mid[32:64, :, :].rearrange("p h t -> p (h t)")).then_inc(s_parts, 1)
                pool.wait_ge(s_parts, b + 1)
                pool.wait_ge(s_dt, 2 * (b + 1))
                nc.gpsimd.tensor_tensor(dtx[:, cols], dt[:, cols], seq_cols(X, b, 0, S), ALU.mult).then_inc(s_dtx, 1)

            loop(pool, B, body)

        @block.tensor
        def _(pe):
            pe.wait_ge(s_w, 64)
            pe.wait_ge(s_x, 16)

            def body(b):
                for h in range(HALVES):
                    x = seq_cols(X, b, h * T, T)
                    if not is_first(b):
                        pe.wait_ge(s_rest, 2 * b + h - 1)
                        pe.wait_ge(s_low, 2 * b + h - 1)
                    nc.tensor.matmul(p_bc[:, h, :], wbc[:, :], x, start=True, stop=True)
                    nc.tensor.matmul(p_low[:, h, :], wr[:, :], x, start=True, stop=True).then_inc(s_proj, 1)
                for h in range(HALVES):
                    pe.wait_ge(s_low, 2 * b + h + 1)
                    if not is_first(b):
                        pe.wait_ge(s_pos, 2 * b + h - 1)
                    nc.tensor.matmul(p_z[:, h, :], wdt[:, :], low[:, h, :], start=True, stop=True).then_inc(s_z, 1)
                if is_first(b):
                    pe.wait_ge(s_xrest, 16)

            loop(pe, B, body)

        @block.scalar
        def _(act):
            nc.scalar.preload_act_table_set(LN_EXP)
            act.wait_ge(s_w, 64)

            def body(b):
                first = is_first(b)
                for h in range(HALVES):
                    act.wait_ge(s_proj, 2 * b + h + 1)
                    act.nop()
                    nc.scalar.copy(parts[:, bass.ds(b * S + h * T, T)], p_bc[:, h, :]).then_inc(s_hi, 1)
                for h in range(HALVES):
                    act.wait_ge(s_rest, 2 * b + h + 1)
                    if not first:
                        act.wait_ge(s_rest2, 2 * b + h - 1)
                        act.wait_ge(s_parts, b)
                    nc.scalar.copy(mid[:, h, :], rest[:, h, :]).then_inc(s_mid, 1)
                for h in range(HALVES):
                    act.wait_ge(s_z, 2 * b + h + 1)
                    nc.scalar.activation(absz[:, h, :], p_z[:, h, :], ACT.Abs, bias=bdt[:, 0:1]).then_inc(s_abs, 1)
                for h in range(HALVES):
                    act.wait_ge(s_abs, 2 * b + h + 1)
                    nc.scalar.activation(expz[:, h, :], absz[:, h, :], ACT.Exp, scale=-1.0).then_inc(s_exp, 1)
                for h in range(HALVES):
                    act.wait_ge(s_exp, 2 * b + h + 1)
                    if not first:
                        act.wait_ge(s_dt, 2 * b + h - 1)
                    nc.scalar.activation(lnz[:, h, :], expz[:, h, :], ACT.Ln, bias=1.0).then_inc(s_ln, 1)

            loop(act, B, body)

        @block.vector
        def _(dve):
            dve.wait_ge(s_w, 64)

            def body(b):
                first = is_first(b)
                for h in range(HALVES):
                    dve.wait_ge(s_proj, 2 * b + h + 1)
                    if not first:
                        dve.wait_ge(s_z, 2 * b + h - 1)
                    nc.vector.tensor_copy(low[:, h, :], p_low[:, h, :]).then_inc(s_low, 1)
                for h in range(HALVES):
                    dve.wait_ge(s_hi, 2 * b + h + 1)
                    if not first:
                        dve.wait_ge(s_mid, 2 * b + h - 1)
                    nc.vector.tensor_tensor(rest[:, h, :], p_bc[:, h, :], parts[:, bass.ds(b * S + h * T, T)],
                                            ALU.subtract).then_inc(s_rest, 1)
                for h in range(HALVES):
                    dve.wait_ge(s_mid, 2 * b + h + 1)
                    nc.vector.tensor_tensor(parts[64:96, bass.ds(b * S + h * T, T)], rest[64:96, h, :], mid[64:96, h, :],
                                            ALU.subtract).then_inc(s_rest2, 1)
                for h in range(HALVES):
                    dve.wait_ge(s_abs, 2 * b + h + 1)
                    nc.vector.tensor_scalar(posz[:, h, :], p_z[:, h, :], bdt[:, 0:1], 0.0, ALU.add, ALU.max).then_inc(s_pos, 1)
                for h in range(HALVES):
                    dve.wait_ge(s_pos, 2 * b + h + 1)
                    dve.wait_ge(s_ln, 2 * b + h + 1)
                    nc.vector.tensor_tensor(dt[:, bass.ds(b * S + h * T, T)], posz[:, h, :], lnz[:, h, :],
                                            ALU.add).then_inc(s_dt, 1)

            loop(dve, B, body)


def selective_scan(nc, X, dt, dtx, parts, w):
    with ExitStack() as ctx:
        sb, ps, sem = alloc(nc, ctx)
        select = sb("select", [96, 2 * NSTATE, D], BF16)
        ident = sb("ident_a", [D, D])
        alog, negA = sb("alog", [D, NSTATE]), sb("negA", [D, NSTATE])
        dtseq = sb("dtseq", [D, S])
        decay = sb("decay", [D, 2, S])
        inject = sb("inject", [D, 2, S])
        state = sb("state", [D, 2, S])
        crow = sb("crow", [D, 2, S])
        read = sb("read", [D, READS, S])
        p_b, p_c, p_y = ps("p_b", [D, 2, HALVES, T]), ps("p_c", [D, HALVES, T]), ps("p_y", [D, HALVES, T])
        s_w, s_ea, s_a, s_dtcopy = sem("b_weights"), sem("b_expA"), sem("b_negA"), sem("b_dtcopy")
        s_bready, s_inject, s_decay, s_state = (sem(n) for n in ("b_bready", "b_inject", "b_decay", "b_state"))
        s_cready, s_crow, s_read, s_summed = (sem(n) for n in ("b_cready", "b_crow", "b_read", "b_summed"))
        s_yused = sem("b_yused")
        block = ctx.enter_context(nc.Block())

        @block.sync
        def _(sp):
            sp.dma_start(select[:, :, :].bitcast(U16), w["select"][:, :, :]).then_inc(s_w, 16)
            sp.dma_start(ident[:, :], w["ident"][:, :]).then_inc(s_w, 16)
            sp.dma_start(alog[:, :], w["A_log"][:, :]).then_inc(s_w, 16)

        @block.tensor
        def _(pe):
            pe.wait_ge(s_w, 48)

            def sum_states(b, n):
                pe.wait_ge(s_read, b * NSTATE + n + 1)
                if n == 0 and not is_first(b):
                    pe.wait_ge(s_yused, HALVES * b)
                for h in range(HALVES):
                    mm = nc.tensor.matmul(p_y[:, h, :], ident[:, :], read[:, n % READS, h * T:(h + 1) * T],
                                          start=(n == 0), stop=(n == NSTATE - 1))
                mm.then_inc(s_summed, 1)

            def body(b):
                for n in range(NSTATE):
                    k = b * NSTATE + n
                    first = is_first(b) and n == 0
                    for h in range(HALVES):
                        rhs = parts[:, bass.ds(b * S + h * T, T)]
                        if not is_first(b) or n >= 2:
                            pe.wait_ge(s_inject, HALVES * (k - 2) + h + 1)
                        nc.tensor.matmul(p_b[:, n % 2, h, :], select[:, n, :], rhs, start=True, stop=True).then_inc(s_bready, 1)
                    for h in range(HALVES):
                        rhs = parts[:, bass.ds(b * S + h * T, T)]
                        if not first:
                            pe.wait_ge(s_crow, HALVES * (k - 1) + h + 1)
                        nc.tensor.matmul(p_c[:, h, :], select[:, NSTATE + n, :], rhs,
                                         start=True, stop=True).then_inc(s_cready, 1)
                    if n >= LAG:
                        sum_states(b, n - LAG)
                    elif not is_first(b):
                        sum_states(b - 1, NSTATE - LAG + n)

            loop(pe, B, body)
            for n in range(NSTATE - LAG, NSTATE):
                sum_states(B - 1, n)

        @block.scalar
        def _(act):
            act.wait_ge(s_w, 48)
            nc.scalar.activation(alog[:, :], alog[:, :], ACT.Exp).then_inc(s_ea, 1)
            act.wait_ge(s_a, 1)

            def body(b):
                if not is_first(b):
                    act.wait_ge(s_decay, NSTATE * b)
                nc.scalar.copy(dtseq[:, :], dt[:, bass.ds(b * S, S)]).then_inc(s_dtcopy, 1)
                for n in range(NSTATE):
                    k = b * NSTATE + n
                    warm = not is_first(b) or n >= 2
                    if warm:
                        act.wait_ge(s_state, k - 1)
                    if n == 0:
                        act.wait_ge(s_dtcopy, b + 1)
                    nc.scalar.activation(decay[:, n % 2, :], dtseq[:, :], ACT.Exp,
                                         scale=negA[:, n:n + 1]).then_inc(s_decay, 1)
                    if warm:
                        act.wait_ge(s_read, k - 1)
                    for h in range(HALVES):
                        act.wait_ge(s_cready, HALVES * k + h + 1)
                        nc.scalar.copy(crow[:, n % 2, h * T:(h + 1) * T], p_c[:, h, :]).then_inc(s_crow, 1)

            loop(act, B, body)

        @block.gpsimd
        def _(pool):
            def body(b):
                for n in range(NSTATE):
                    k = b * NSTATE + n
                    pool.wait_ge(s_state, k + 1)
                    pool.wait_ge(s_crow, HALVES * (k + 1))
                    if not is_first(b) or n >= READS:
                        pool.wait_ge(s_summed, k - READS + 1)
                    nc.gpsimd.tensor_tensor(read[:, n % READS, :], state[:, n % 2, :], crow[:, n % 2, :],
                                            ALU.mult).then_inc(s_read, 1)

            loop(pool, B, body)

        @block.vector
        def _(dve):
            dve.wait_ge(s_ea, 1)
            nc.vector.tensor_scalar(negA[:, :], alog[:, :], -1.0, None, ALU.mult).then_inc(s_a, 1)

            def body(b):
                def make_inject(n):
                    k = b * NSTATE + n
                    if not is_first(b) or n >= 2:
                        dve.wait_ge(s_state, k - 1)
                    for h in range(HALVES):
                        dve.wait_ge(s_bready, HALVES * k + h + 1)
                        nc.vector.tensor_tensor(inject[:, n % 2, h * T:(h + 1) * T], p_b[:, n % 2, h, :],
                                                dtx[:, bass.ds(b * S + h * T, T)], ALU.mult).then_inc(s_inject, 1)

                make_inject(0)
                for n in range(NSTATE):
                    k = b * NSTATE + n
                    if n + 1 < NSTATE:
                        make_inject(n + 1)
                    dve.wait_ge(s_inject, HALVES * (k + 1))
                    dve.wait_ge(s_decay, k + 1)
                    if not is_first(b) or n >= 2:
                        dve.wait_ge(s_read, k - 1)
                    nc.vector.tensor_tensor_scan(state[:, n % 2, :], decay[:, n % 2, :], inject[:, n % 2, :], 0.0,
                                                 ALU.mult, ALU.add).then_inc(s_state, 1)
                    if n == LAG - 1 and not is_first(b):
                        add_sums(b - 1)

            def add_sums(b):
                dve.wait_ge(s_summed, NSTATE * (b + 1))
                for h in range(HALVES):
                    x = seq_cols(X, b, h * T, T)
                    nc.vector.tensor_tensor(x, p_y[:, h, :], x, ALU.add).then_inc(s_yused, 1)

            loop(dve, B, body)
            add_sums(B - 1)


def layer_norm(nc, X, w, tag):
    with ExitStack() as ctx:
        sb, ps, sem = alloc(nc, ctx)
        mean_w = sb(tag + "mean_w", [D, D])
        eps = sb(tag + "eps", [D, 1])
        centred, square = sb(tag + "centred", [D, 2, 2, T]), sb(tag + "square", [D, 2, 2, T])
        logv, rstd = sb(tag + "logv", [D, 2, T]), sb(tag + "rstd", [D, 2, T])
        p_mean, p_var = ps(tag + "p_mean", [D, 2, T]), ps(tag + "p_var", [D, 2, T])
        s_w, s_eps = sem(tag + "weights"), sem(tag + "eps_set")
        s_mean, s_centred, s_square, s_var, s_log, s_rstd, s_out = (
            sem(tag + n) for n in ("mean", "centred", "square", "var", "log", "rstd", "out"))
        block = ctx.enter_context(nc.Block())

        def from_third(b):
            return not isinstance(b, int) or b > 1

        @block.sync
        def _(sp):
            sp.dma_start(mean_w[:, :], w["mean_w"][:, :]).then_inc(s_w, 16)

        @block.tensor
        def _(pe):
            pe.wait_ge(s_w, 16)

            def late(b, e):
                for h in range(HALVES):
                    pe.wait_ge(s_square, 2 * b + h + 1)
                    if started(b):
                        pe.wait_ge(s_log, 2 * b + h - 1)
                    nc.tensor.matmul(p_var[:, h, :], mean_w[:, :], square[:, e, h, :],
                                     start=True, stop=True).then_inc(s_var, 1)

            def step(b, e, i):
                for h in range(HALVES):
                    if started(b):
                        pe.wait_ge(s_centred, 2 * b + h - 1)
                    nc.tensor.matmul(p_mean[:, h, :], mean_w[:, :], seq_cols(X, b, h * T, T),
                                     start=True, stop=True).then_inc(s_mean, 1)
                if started(b):
                    late(b - 1, 1 - e)

            pipeline(pe, step, lambda b: late(b, b % 2))

        @block.scalar
        def _(act):
            nc.scalar.preload_act_table_set(LN_EXP)
            act.wait_ge(s_eps, 1)

            def late(b):
                for h in range(HALVES):
                    act.wait_ge(s_var, 2 * b + h + 1)
                    nc.scalar.activation(logv[:, h, :], p_var[:, h, :], ACT.Ln, bias=eps[:, 0:1]).then_inc(s_log, 1)
                    act.wait_ge(s_log, 2 * b + h + 1)
                    if started(b):
                        act.wait_ge(s_out, 2 * b + h - 1)
                    nc.scalar.activation(rstd[:, h, :], logv[:, h, :], ACT.Exp, scale=-0.5).then_inc(s_rstd, 1)

            def step(b, e, i):
                for h in range(HALVES):
                    act.wait_ge(s_centred, 2 * b + h + 1)
                    if from_third(b):
                        act.wait_ge(s_var, 2 * b + h - 3)
                    nc.scalar.activation(square[:, e, h, :], centred[:, e, h, :], ACT.Square).then_inc(s_square, 1)
                if started(b):
                    late(b - 1)

            pipeline(act, step, late)

        @block.vector
        def _(dve):
            nc.vector.memset(eps[:, :], EPS).then_inc(s_eps, 1)

            def late(b, e):
                for h in range(HALVES):
                    dve.wait_ge(s_rstd, 2 * b + h + 1)
                    dve.wait_ge(s_centred, 2 * b + h + 1)
                    nc.vector.tensor_tensor(seq_cols(X, b, h * T, T), centred[:, e, h, :], rstd[:, h, :],
                                            ALU.mult).then_inc(s_out, 1)

            def step(b, e, i):
                for h in range(HALVES):
                    dve.wait_ge(s_mean, 2 * b + h + 1)
                    if from_third(b):
                        dve.wait_ge(s_square, 2 * b + h - 3)
                        dve.wait_ge(s_out, 2 * b + h - 3)
                    nc.vector.tensor_tensor(centred[:, e, h, :], seq_cols(X, b, h * T, T), p_mean[:, h, :],
                                            ALU.subtract).then_inc(s_centred, 1)
                if started(b):
                    late(b - 1, 1 - e)

            pipeline(dve, step, lambda b: late(b, b % 2))


def ternary_ffn(nc, X, w):
    with ExitStack() as ctx:
        sb, ps, sem = alloc(nc, ctx)
        w1, w2 = sb("w1", [D, HID]), sb("w2", [D, HID])
        h1, h2, w3 = sb("h1", [128, KT, HID]), sb("h2", [128, KT, HID]), sb("w3", [128, KT, D])
        scales = sb("scales", [128, 4 * KT + 1])
        gate = sb("gate", [128, 2, KT, T])
        act0 = sb("act0", [128, 2, KT, T])
        p_hid = ps("p_hid", [128, 4, T])
        p_out = ps("p_out", [128, 2, T])
        s_w = sem("f_weights")
        s_g, s_u, s_gate, s_prod = sem("f_g"), sem("f_u"), sem("f_gate"), sem("f_prod")
        s_mm1, s_mm2, s_act1, s_act2, s_mm3, s_out = (sem("f_" + n) for n in ("mm1", "mm2", "act1", "act2", "mm3", "out"))
        block = ctx.enter_context(nc.Block())

        @block.sync
        def _(sp):
            sp.dma_start(w1[:, :], w["w1"][:, :]).then_inc(s_w, 16)
            sp.dma_start(w2[:, :], w["w2"][:, :]).then_inc(s_w, 16)
            sp.dma_start(h1[:, :, :], w["h1"].rearrange("(k p) n -> p k n", p=128)).then_inc(s_w, 16)
            sp.dma_start(h2[:, :, :], w["h2"].rearrange("(k p) n -> p k n", p=128)).then_inc(s_w, 16)
            sp.dma_start(w3[:, :, :], w["w3"].rearrange("(k p) n -> p k n", p=128)).then_inc(s_w, 16)
            sp.dma_start(scales[:, :], w["ffn_scales"][:, :]).then_inc(s_w, 16)

        N = 2 * KT

        @block.tensor
        def _(pe):
            pe.wait_ge(s_w, 96)

            def body(b):
                base = b * N
                for h in range(2):
                    x = seq_cols(X, b, h * T, T)
                    for m in range(KT):
                        i = h * KT + m
                        bank = 2 * (i % 2)
                        if i >= 2:
                            pe.wait_ge(s_gate, base + i - 1)
                            pe.wait_ge(s_prod, base + i - 1)
                        elif not is_first(b):
                            pe.wait_ge(s_act2, base)
                        nc.tensor.matmul(p_hid[:, bank, :], w1[:, m * 128:(m + 1) * 128], x,
                                         start=True, stop=True).then_inc(s_g, 1)
                        nc.tensor.matmul(p_hid[:, bank + 1, :], w2[:, m * 128:(m + 1) * 128], x,
                                         start=True, stop=True).then_inc(s_u, 1)
                for layer, (wt, src, s_src, s_mm, s_free) in enumerate((
                        (h1, act0, s_prod, s_mm1, s_act1), (h2, gate, s_act1, s_mm2, s_act2))):
                    for h in range(2):
                        pe.wait_ge(s_src, base + KT * (h + 1))
                        for m in range(KT):
                            i = h * KT + m
                            if i >= 4:
                                pe.wait_ge(s_free, base + i - 3)
                            elif layer == 0:
                                pe.wait_ge(s_gate, base + N)
                                pe.wait_ge(s_prod, base + N)
                            else:
                                pe.wait_ge(s_act1, base + N - 3 + i)
                            for k in range(KT):
                                mm = nc.tensor.matmul(p_hid[:, i % 4, :], wt[:, k, m * 128:(m + 1) * 128],
                                                      src[:, h, k, :], start=(k == 0), stop=(k == KT - 1))
                            mm.then_inc(s_mm, 1)
                for h in range(2):
                    pe.wait_ge(s_act2, base + KT * (h + 1))
                    if not is_first(b):
                        pe.wait_ge(s_out, 2 * b)
                    for k in range(KT):
                        mm = nc.tensor.matmul(p_out[:, h, :], w3[:, k, :], act0[:, h, k, :],
                                              start=(k == 0), stop=(k == KT - 1))
                    mm.then_inc(s_mm3, 1)

            loop(pe, B, body)

        @block.scalar
        def _(act):
            act.wait_ge(s_w, 96)

            def body(b):
                base = b * N
                for i in range(N):
                    h, m = i // KT, i % KT
                    act.wait_ge(s_g, base + i + 1)
                    if i == 0 and not is_first(b):
                        act.wait_ge(s_mm2, base)
                    nc.scalar.activation(gate[:, h, m, :], p_hid[:, 2 * (i % 2), :], ACT.Silu,
                                         scale=scales[:, m:m + 1]).then_inc(s_gate, 1)
                for i in range(N):
                    h, m = i // KT, i % KT
                    act.wait_ge(s_mm1, base + i + 1)
                    if i == 0:
                        act.wait_ge(s_prod, base + N)
                    nc.scalar.activation(gate[:, h, m, :], p_hid[:, i % 4, :], ACT.Gelu,
                                         scale=scales[:, 2 * KT + m:2 * KT + m + 1]).then_inc(s_act1, 1)
                for i in range(N):
                    h, m = i // KT, i % KT
                    act.wait_ge(s_mm2, base + i + 1)
                    if m == 0:
                        act.wait_ge(s_mm1, base + KT * (h + 1))
                    nc.scalar.activation(act0[:, h, m, :], p_hid[:, i % 4, :], ACT.Gelu,
                                         scale=scales[:, 3 * KT + m:3 * KT + m + 1]).then_inc(s_act2, 1)

            loop(act, B, body)

        @block.vector
        def _(dve):
            dve.wait_ge(s_w, 96)

            def body(b):
                base = b * N
                for i in range(N):
                    h, m = i // KT, i % KT
                    dve.wait_ge(s_u, base + i + 1)
                    dve.wait_ge(s_gate, base + i + 1)
                    if i == 0 and not is_first(b):
                        dve.wait_ge(s_mm3, 2 * b)
                    nc.vector.scalar_tensor_tensor(out=act0[:, h, m, :], in0=p_hid[:, 2 * (i % 2) + 1, :],
                                                   scalar=scales[:, KT + m:KT + m + 1], in1=gate[:, h, m, :],
                                                   op0=ALU.mult, op1=ALU.mult).then_inc(s_prod, 1)
                for h in range(2):
                    x = seq_cols(X, b, h * T, T)
                    dve.wait_ge(s_mm3, 2 * b + h + 1)
                    nc.vector.scalar_tensor_tensor(out=x, in0=p_out[:, h, :], scalar=scales[:, 4 * KT:4 * KT + 1],
                                                   in1=x, op0=ALU.mult, op1=ALU.add).then_inc(s_out, 1)

            loop(dve, B, body)


H = 4
DH = 32
CS = 32
NC_ = S // CS
CONV = 4
SHORT, LONG = 3, 31
PE_TAPS = 15
BRANCHES = 4
GH = 128
KB, Q, K, ATT, VB, INV = (DH * i for i in range(6))
REC = 6 * DH
HALF_B = 4


def delta_inputs(nc, X, V, L, w, scratch):
    chunks, recs = scratch["upper"], scratch["records"]
    with ExitStack() as ctx:
        sb, ps, sem = alloc(nc, ctx)
        wconv = sb("wconv", [D, 3, CONV, D])
        wproj = sb("wproj", [D, D])
        taps = sb("taps", [D, CONV, D])
        wbeta, headsum = sb("wbeta", [D, D]), sb("headsum", [D, D])
        ident, ltaps = sb("ident_c", [D, D]), sb("ltaps", [D, LONG])
        diag = sb("diag", [D, PE_TAPS, D])
        keep_lt, keep_le = sb("keep_lt", [D, CS]), sb("keep_le", [D, CS])
        tiny = sb("tiny", [D, 1])
        qs, ks, kn = sb("qs", [D, S]), sb("ks", [D, S]), sb("kn", [D, S])
        vs = sb("vs", [D, 2, DH + S])
        beta, rq, rk = sb("beta", [D, S]), sb("rq", [D, S]), sb("rk", [D, S])
        kdiag = sb("kdiag", [D, NC_, H, CS])
        rec = sb("rec", [D, NC_, INV])
        upper = sb("upper", [D, NC_, CS])
        umat, rmat = sb("umat", [D, CS, CS]), sb("rmat", [D, CS, CS])
        prod = sb("prod", [D, (CS - 1) * (CS - 1)])
        acc = sb("acc", [D, 2, S])
        p_z = ps("p_zc", [D, 2, T])
        p_att = ps("p_att", [D, 4, T])
        p_fir = ps("p_fir", [D, 2, T])
        s_w, s_raw, s_tap, s_ready = sem("c_weights"), sem("c_raw"), sem("c_tap"), sem("c_ready")
        s_z, s_zread, s_sq, s_rs = sem("c_z"), sem("c_zread"), sem("c_sq"), sem("c_rs")
        s_qn, s_kn, s_kb, s_vb, s_kt = (sem("c_" + n) for n in ("qn", "kn", "kb", "vb", "kt"))
        s_kfirst, s_kothers = sem("c_kfirst"), sem("c_kothers")
        s_att, s_masked, s_fir, s_joined, s_acc, s_long = (
            sem("c_" + n) for n in ("att", "masked", "fir", "joined", "acc", "long"))
        s_uout, s_uin, s_solve, s_rout, s_recout = (
            sem("c_" + n) for n in ("uout", "uin", "solve", "rout", "recout"))
        s_vout = [sem("c_vout0"), sem("c_vout1")]
        block = ctx.enter_context(nc.Block())
        SOLVE = 2 * (CS - 1)
        DVE_TAPS = LONG - PE_TAPS

        @block.sync
        def _(sp):
            loads = ((wbeta, w["b_proj"]), (headsum, w["headsum"]), (ident, w["ident"]), (ltaps, w["fir_long"]),
                     (keep_lt, w["keep_lt"]), (keep_le, w["keep_le"]))
            for dst, src in loads:
                sp.dma_start(dst[:, :], src[:, :]).then_inc(s_w, 16)
            sp.dma_start(rmat[:, :, :], w["eye32"].rearrange("p (j i) -> p j i", i=CS)).then_inc(s_w, 16)
            for p, n in enumerate("qkv"):
                if p:
                    sp.wait_ge(s_tap, CONV * p)
                sp.dma_start(wproj[:, :], w[n + "_proj"][:, :]).then_inc(s_raw, 16)
                sp.dma_start(taps[:, :, :], w[n + "_conv"].rearrange("p (j n) -> p j n", j=CONV)).then_inc(s_raw, 16)

            def inverse_out(b):
                sp.wait_ge(s_solve, SOLVE * (b + 1))
                for h in range(H):
                    dst = recs[:, h * CS:(h + 1) * CS, bass.ds(b * REC + INV, CS)]
                    sp.dma_start(dst, rmat[h * NC_:(h + 1) * NC_, :, :]).then_inc(s_rout, 16)

            def step(b, e, i):
                sp.wait_ge(s_zread, 12 * b + 6)
                sp.dma_start(V[:, bass.ds(b * ROW + PAD, S)], vs[:, e, DH:]).then_inc(s_vout[e], 16)
                if started(b):
                    inverse_out(b - 1)
                sp.wait_ge(s_masked, 8 * (b + 1))
                for h in range(H):
                    sp.dma_start(chunks[h].rearrange("n j i -> j n i"),
                                 upper[h * CS:(h + 1) * CS, :, :]).then_inc(s_uout, 16)
                sp.wait_ge(s_vb, b + 1)
                sp.wait_ge(s_kt, b + 1)
                dst = recs[:, :, bass.ds(b * REC, INV)].rearrange("n p c -> p n c")
                sp.dma_start(dst, rec[:, :, :]).then_inc(s_recout, 16)
                sp.wait_ge(s_uout, 64 * (b + 1))
                sp.dma_start(umat[:, :, :], chunks.rearrange("h n j i -> (h n) j i")).then_inc(s_uin, 16)

            pipeline(sp, step, inverse_out)
            for s, n in ((s_rout, 64 * B), (s_vout[0], 8 * B), (s_vout[1], 8 * B), (s_recout, 16 * B)):
                sp.wait_ge(s, n)

        @block.tensor
        def _(pe):
            pe.wait_ge(s_w, 112)
            pe.wait_ge(s_tap, 3 * CONV)

            def fir(b, e, h):
                if started(b):
                    pe.wait_ge(s_joined, 2 * (b - 1) + h + 1)
                for j in range(PE_TAPS):
                    lo = DH + h * T - (LONG - 1) + j
                    mm = nc.tensor.matmul(p_fir[:, h, :], diag[:, j, :], vs[:, e, lo:lo + T],
                                          start=(j == 0), stop=(j == PE_TAPS - 1))
                mm.then_inc(s_fir, 1)

            def step(b, e, i):
                first = is_first(b)

                def bank_free(i):
                    if i >= 2 or not first:
                        pe.wait_ge(s_zread, 12 * b + i - 1)

                for i in range(6):
                    bank_free(i)
                    p, h = i // 2, i % 2
                    for j in range(CONV):
                        mm = nc.tensor.matmul(p_z[:, i % 2, :], wconv[:, p, j, :],
                                              seq_cols(X, b, h * T - (CONV - 1) + j, T),
                                              start=(j == 0), stop=(j == CONV - 1))
                    mm.then_inc(s_z, 1)
                for h in range(2):
                    bank_free(6 + h)
                    nc.tensor.matmul(p_z[:, h, :], wbeta[:, :], seq_cols(X, b, h * T, T),
                                     start=True, stop=True).then_inc(s_z, 1)
                if not first:
                    fir(b - 1, 1 - e, 0)
                for i in range(8, 12):
                    bank_free(i)
                    pe.wait_ge(s_sq, 2 * b + (i - 8) // 2 + 1)
                    src = rq if i < 10 else rk
                    nc.tensor.matmul(p_z[:, i % 2, :], headsum[:, :], src[:, (i % 2) * T:(i % 2 + 1) * T],
                                     start=True, stop=True).then_inc(s_z, 1)
                if not first:
                    fir(b - 1, 1 - e, 1)
                if first:
                    pe.wait_ge(s_ready, 3 + PE_TAPS)
                pe.wait_ge(s_kfirst, b + 1)
                pe.wait_ge(s_kothers, (H - 1) * (b + 1))
                pe.wait_ge(s_kb, b + 1)
                pe.wait_ge(s_qn, b + 1)
                for g in range(4):
                    if not first:
                        pe.wait_ge(s_masked, 8 * b)
                    for c in range(8):
                        n = 8 * g + c
                        mm = nc.tensor.matmul(p_att[:, g, c * 64:(c + 1) * 64], kdiag[:, n, :, :],
                                              rec[:, n, KB:KB + 2 * DH], start=True, stop=True)
                    mm.then_inc(s_att, 1)

            def late(b):
                for h in range(2):
                    fir(b, b % 2, h)

            pipeline(pe, step, late)

        @block.scalar
        def _(act):
            def step(b, e, turn):
                first = is_first(b)
                for i in range(6):
                    p, h = i // 2, i % 2
                    act.wait_ge(s_z, 12 * b + i + 1)
                    if not first and i == 0:
                        act.wait_ge(s_qn, b)
                        act.wait_ge(s_kn, b)
                        act.wait_ge(s_kfirst, b)
                    if i == 4 and not (isinstance(b, int) and b < 2):
                        act.wait_ge(s_vb, b - 1)
                        act.wait_ge(s_fir, 2 * (b - 1))
                        act.wait_ge(s_acc, DVE_TAPS * (b - 1))
                        act.wait_ge(s_vout[e], 16 * turn)
                    dst = (qs[:, h * T:(h + 1) * T], ks[:, h * T:(h + 1) * T], vs[:, e, DH + h * T:DH + (h + 1) * T])[p]
                    nc.scalar.activation(dst, p_z[:, h, :], ACT.Silu).then_inc(s_zread, 1)
                for h in range(2):
                    act.wait_ge(s_z, 12 * b + 7 + h)
                    if not first and h == 0:
                        act.wait_ge(s_kb, b)
                        act.wait_ge(s_vb, b)
                    nc.scalar.activation(beta[:, h * T:(h + 1) * T], p_z[:, h, :], ACT.Sigmoid).then_inc(s_zread, 1)
                act.wait_ge(s_zread, 12 * b + 4)
                nc.scalar.activation(rq[:, :], qs[:, :], ACT.Square).then_inc(s_sq, 1)
                nc.scalar.activation(rk[:, :], ks[:, :], ACT.Square).then_inc(s_sq, 1)
                nc.scalar.preload_act_table_set(LN_EXP)
                for i in range(8, 12):
                    act.wait_ge(s_z, 12 * b + i + 1)
                    dst = (rq if i < 10 else rk)[:, (i % 2) * T:(i % 2 + 1) * T]
                    if i % 2 == 0:
                        act.wait_ge(s_z, 12 * b + i + 2)
                    nc.scalar.activation(dst, p_z[:, i % 2, :], ACT.Ln, bias=tiny[:, 0:1]).then_inc(s_zread, 1)
                act.wait_ge(s_zread, 12 * b + 12)
                nc.scalar.activation(rk[:, :], rk[:, :], ACT.Exp, scale=-0.5).then_inc(s_rs, 1)
                nc.scalar.activation(rq[:, :], rq[:, :], ACT.Exp, scale=-0.5).then_inc(s_rs, 1)
                act.wait_ge(s_kn, b + 1)
                if first:
                    act.wait_ge(s_ready, 1)
                for h in range(1, H):
                    r = slice(h * DH, (h + 1) * DH)
                    nc.scalar.copy(kdiag[r, :, h, :], kn[r, :].rearrange("p (n i) -> p n i", i=CS)).then_inc(s_kothers, 1)

            pipeline(act, step)

        @block.gpsimd
        def _(pool):
            nc.gpsimd.memset(kdiag[:, :, :, :], 0.0).then_inc(s_ready, 1)
            nc.gpsimd.memset(vs[:, :, 0:DH], 0.0).then_inc(s_ready, 1)
            nc.gpsimd.memset(V[:, :].rearrange("p (b c) -> p b c", c=ROW)[:, :, 0:PAD], 0.0).then_inc(s_ready, 1)
            pool.wait_ge(s_w, 112)
            for j in range(PE_TAPS):
                nc.gpsimd.tensor_scalar(diag[:, j, :], ident[:, :], ltaps[:, j:j + 1], None, ALU.mult).then_inc(s_ready, 1)
            pool.wait_ge(s_ready, 3 + PE_TAPS)

            def long_out(b):
                pool.wait_ge(s_acc, DVE_TAPS * (b + 1))
                pool.wait_ge(s_joined, 2 * (b + 1))
                nc.gpsimd.tensor_tensor(L[:, bass.ds(b * S, S)], acc[:, 0, :], acc[:, 1, :], ALU.add).then_inc(s_long, 1)

            def step(b, e, i):
                pool.wait_ge(s_rs, 2 * b + 1)
                if not is_first(b):
                    pool.wait_ge(s_att, 4 * b)
                if not (isinstance(b, int) and b < 2):
                    pool.wait_ge(s_long, b - 1)
                split = lambda t: t[0:DH, :].rearrange("p (n i) -> p n i", i=CS)
                nc.gpsimd.tensor_tensor(kdiag[0:DH, :, 0, :], split(ks), split(rk), ALU.mult).then_inc(s_kfirst, 1)
                if not is_first(b):
                    pool.wait_ge(s_kfirst, b + 1)
                    long_out(b - 1)

            pipeline(pool, step, long_out)

        @block.vector
        def _(dve):
            nc.vector.memset(tiny[:, :], 1e-12)
            dve.wait_ge(s_w, 112)
            for p in range(3):
                dve.wait_ge(s_raw, 32 * (p + 1))
                for j in range(CONV):
                    nc.vector.tensor_tensor(wconv[:, p, j, :], wproj[:, :], taps[:, j, :], ALU.mult).then_inc(s_tap, 1)
            slot = lambda at: rec[:, :, at:at + DH]
            chunked = lambda t: t.rearrange("p (n i) -> p n i", i=CS)

            def scaled(b, e):
                first = is_first(b)
                dve.wait_ge(s_rs, 2 * b + 1)
                if not first:
                    dve.wait_ge(s_recout, 16 * b)
                    dve.wait_ge(s_att, 4 * b)
                    dve.wait_ge(s_kt, b)
                nc.vector.tensor_tensor(kn[:, :], ks[:, :], rk[:, :], ALU.mult).then_inc(s_kn, 1)
                dve.wait_ge(s_rs, 2 * (b + 1))
                nc.vector.tensor_tensor(slot(Q), chunked(qs[:, :]), chunked(rq[:, :]), ALU.mult).then_inc(s_qn, 1)
                dve.wait_ge(s_kn, b + 1)
                dve.wait_ge(s_zread, 12 * b + 8)
                nc.vector.tensor_tensor(slot(KB), chunked(kn[:, :]), chunked(beta[:, :]), ALU.mult).then_inc(s_kb, 1)
                nc.vector.tensor_tensor(slot(VB), chunked(vs[:, e, DH:]), chunked(beta[:, :]), ALU.mult).then_inc(s_vb, 1)
                nc.vector.transpose(slot(K), chunked(kn[:, :])).then_inc(s_kt, 1)

            def masks(b):
                for g in range(4):
                    c = slice(8 * g, 8 * g + 8)
                    pa = p_att[:, g, :].rearrange("p (n c) -> p n c", c=64)
                    dve.wait_ge(s_att, 4 * b + g + 1)
                    if g == 0 and started(b):
                        dve.wait_ge(s_uout, 64 * b)
                    nc.vector.tensor_tensor(upper[:, c, :], pa[:, :, 0:CS],
                                            keep_lt[:, :].unsqueeze(1).broadcast_to([D, 8, CS]), ALU.mult).then_inc(s_masked, 1)
                    nc.vector.tensor_tensor(rec[:, c, ATT:ATT + CS], pa[:, :, CS:2 * CS],
                                            keep_le[:, :].unsqueeze(1).broadcast_to([D, 8, CS]), ALU.mult).then_inc(s_masked, 1)

            def fir(b, e):
                for k in range(DVE_TAPS):
                    j = PE_TAPS + k
                    lo = DH - (LONG - 1) + j
                    v = vs[:, e, lo:lo + S]
                    if k >= 2:
                        dve.wait_ge(s_acc, DVE_TAPS * b + k - 1)
                        nc.vector.scalar_tensor_tensor(out=acc[:, k % 2, :], in0=v, scalar=ltaps[:, j:j + 1],
                                                       in1=acc[:, k % 2, :], op0=ALU.mult, op1=ALU.add).then_inc(s_acc, 1)
                    else:
                        if k == 0 and started(b):
                            dve.wait_ge(s_long, b)
                        nc.vector.tensor_scalar(acc[:, k % 2, :], v, ltaps[:, j:j + 1], None, ALU.mult).then_inc(s_acc, 1)

            def solve(b):
                dve.wait_ge(s_uin, 16 * (b + 1))
                if started(b):
                    dve.wait_ge(s_rout, 64 * b)
                for n, j in enumerate(range(CS - 2, -1, -1)):
                    m = CS - 1 - j
                    p = prod[:, 0:m * m].rearrange("p (i l) -> p i l", l=m)
                    if n:
                        dve.wait_ge(s_solve, SOLVE * b + 2 * n)
                    nc.vector.tensor_tensor(p, umat[:, j, j + 1:CS].unsqueeze(1).broadcast_to([D, m, m]),
                                            rmat[:, j + 1:CS, j + 1:CS].rearrange("p l i -> p i l"),
                                            ALU.mult).then_inc(s_solve, 1)
                    dve.wait_ge(s_solve, SOLVE * b + 2 * n + 1)
                    nc.vector.tensor_reduce(rmat[:, j, j + 1:CS], p, AX.X, ALU.add, negate=True).then_inc(s_solve, 1)

            def join(b):
                for h in range(2):
                    c = slice(h * T, (h + 1) * T)
                    dve.wait_ge(s_acc, DVE_TAPS * (b + 1))
                    dve.wait_ge(s_fir, 2 * b + h + 1)
                    nc.vector.tensor_tensor(acc[:, 0, c], acc[:, 0, c], p_fir[:, h, :], ALU.add).then_inc(s_joined, 1)

            def step(b, e, i):
                if not is_first(b):
                    fir(b - 1, 1 - e)
                scaled(b, e)
                if not is_first(b):
                    solve(b - 1)
                    join(b - 1)
                masks(b)

            def late(b):
                fir(b, b % 2)
                solve(b)
                join(b)

            pipeline(dve, step, late)


def delta_scan(nc, O, w, scratch):
    recs = scratch["records"]
    with ExitStack() as ctx:
        sb, ps, sem = alloc(nc, ctx)
        inp = sb("scan_in", [D, 2, B, REC])
        sdiag, rdiag, udiag = (sb(n, [D, B, H, DH]) for n in ("sdiag", "rdiag", "udiag"))
        strans, resid, qpart = sb("strans", [D, B, DH]), sb("resid", [D, B, CS]), sb("qpart", [D, B, CS])
        osum = sb("osum", [D, 2, B, CS])
        p_s = [ps(f"p_s{g}", [D, HALF_B, 2 * CS]) for g in range(2)]
        p_u = [ps(f"p_u{g}", [D, HALF_B, CS]) for g in range(2)]
        p_k = [ps(f"p_k{g}", [D, HALF_B, 2 * CS]) for g in range(2)]
        s_zero, s_in, s_out = sem("d_zero"), [sem("d_in0"), sem("d_in1")], [sem("d_out0"), sem("d_out1")]
        s_ms, s_resid, s_rdiag, s_mu, s_udiag, s_mk, s_state, s_sdiag, s_qpart, s_osum = (
            [sem(f"d_{n}{g}") for g in range(2)]
            for n in ("ms", "resid", "rdiag", "mu", "udiag", "mk", "state", "sdiag", "qpart", "osum"))
        block = ctx.enter_context(nc.Block())
        STEPS = NC_ // 2
        seqs = [slice(HALF_B * g, HALF_B * (g + 1)) for g in range(2)]

        def pairs(eng, body):
            body(0)
            with eng.Fori(1, STEPS) as i:
                body(i)

        @block.sync
        def _(sp):
            def body(i):
                for e in range(2):
                    n = 2 * i + e
                    if not is_first(i):
                        for g in range(2):
                            sp.wait_ge(s_mk[g], n - 1)
                            sp.wait_ge(s_resid[g], n - 1)
                    sp.dma_start(inp[:, e, :, :], recs[bass.ds(n, 1), :, :].rearrange("n p (b c) -> (n p) b c", c=REC)
                                 ).then_inc(s_in[e], 16)

            pairs(sp, body)

        @block.gpsimd
        def _(pool):
            for t in (sdiag, rdiag, udiag):
                nc.gpsimd.memset(t[:, :, :, :], 0.0).then_inc(s_zero, 1)
            nc.gpsimd.memset(strans[:, :, :], 0.0).then_inc(s_zero, 1)

            def body(i):
                for e in range(2):
                    n = 2 * i + e
                    for g in range(2):
                        pool.wait_ge(s_osum[g], n + 1)
                    pool.dma_start(O[:, bass.ds(n * CS * B, CS * B)],
                                   osum[:, e, :, :].rearrange("p b c -> p (b c)")).then_inc(s_out[e], 16)

            pairs(pool, body)
            for e in range(2):
                pool.wait_ge(s_out[e], 16 * STEPS)

        @block.tensor
        def _(pe):
            pe.wait_ge(s_zero, 4)

            def body(i):
                for e in range(2):
                    n = 2 * i + e
                    start = is_first(i) and e == 0
                    pe.wait_ge(s_in[e], 16 * (i + 1))
                    for g in range(2):
                        if not start:
                            pe.wait_ge(s_sdiag[g], n * H)
                            pe.wait_ge(s_qpart[g], n)
                        for b in range(HALF_B):
                            bb = HALF_B * g + b
                            mm = nc.tensor.matmul(p_s[g][:, b, :], sdiag[:, bb, :, :], inp[:, e, bb, KB:KB + 2 * DH],
                                                  start=True, stop=True)
                        mm.then_inc(s_ms[g], 1)
                    for g in range(2):
                        pe.wait_ge(s_rdiag[g], (n + 1) * H)
                        if not start:
                            pe.wait_ge(s_udiag[g], n * H)
                        for b in range(HALF_B):
                            bb = HALF_B * g + b
                            mm = nc.tensor.matmul(p_u[g][:, b, :], rdiag[:, bb, :, :], inp[:, e, bb, INV:INV + CS],
                                                  start=True, stop=True)
                        mm.then_inc(s_mu[g], 1)
                    for g in range(2):
                        pe.wait_ge(s_udiag[g], (n + 1) * H)
                        if not start:
                            pe.wait_ge(s_state[g], n)
                            pe.wait_ge(s_osum[g], n)
                        for b in range(HALF_B):
                            bb = HALF_B * g + b
                            mm = nc.tensor.matmul(p_k[g][:, b, :], udiag[:, bb, :, :], inp[:, e, bb, K:K + 2 * DH],
                                                  start=True, stop=True)
                        mm.then_inc(s_mk[g], 1)

            pairs(pe, body)

        @block.scalar
        def _(act):
            def body(i):
                for e in range(2):
                    n = 2 * i + e
                    start = is_first(i) and e == 0
                    for g in range(2):
                        act.wait_ge(s_resid[g], n + 1)
                        if not start:
                            act.wait_ge(s_osum[g], n)
                        nc.scalar.copy(qpart[:, seqs[g], :], p_s[g][:, :, CS:2 * CS]).then_inc(s_qpart[g], 1)

            pairs(act, body)

        @block.vector
        def _(dve):
            dve.wait_ge(s_zero, 4)

            def to_diagonal(dst, src, done, g):
                for h in range(H):
                    r = slice(h * DH, (h + 1) * DH)
                    nc.vector.transpose(dst[r, seqs[g], h, :], src(r)).then_inc(done[g], 1)

            def body(i):
                for e in range(2):
                    n = 2 * i + e
                    start = is_first(i) and e == 0
                    dve.wait_ge(s_in[e], 16 * (i + 1))
                    for g in range(2):
                        dve.wait_ge(s_ms[g], n + 1)
                        if not start:
                            dve.wait_ge(s_mu[g], n)
                        nc.vector.tensor_tensor(resid[:, seqs[g], :], inp[:, e, seqs[g], VB:VB + CS],
                                                p_s[g][:, :, 0:CS], ALU.subtract).then_inc(s_resid[g], 1)
                        dve.wait_ge(s_resid[g], n + 1)
                        to_diagonal(rdiag, lambda r: resid[r, seqs[g], :], s_rdiag, g)
                    for g in range(2):
                        dve.wait_ge(s_mu[g], n + 1)
                        if not start:
                            dve.wait_ge(s_mk[g], n)
                        to_diagonal(udiag, lambda r: p_u[g][r, :, :], s_udiag, g)
                    for g in range(2):
                        dve.wait_ge(s_mk[g], n + 1)
                        nc.vector.tensor_tensor(strans[:, seqs[g], :], strans[:, seqs[g], :], p_k[g][:, :, 0:DH],
                                                ALU.add).then_inc(s_state[g], 1)
                        dve.wait_ge(s_state[g], n + 1)
                        dve.wait_ge(s_ms[g], n + 1)
                        to_diagonal(sdiag, lambda r: strans[r, seqs[g], :], s_sdiag, g)
                        dve.wait_ge(s_qpart[g], n + 1)
                        if not is_first(i):
                            dve.wait_ge(s_out[e], 16 * i)
                        nc.vector.tensor_tensor(osum[:, e, seqs[g], :], qpart[:, seqs[g], :], p_k[g][:, :, CS:2 * CS],
                                                ALU.add).then_inc(s_osum[g], 1)

            pairs(dve, body)


def gate_mix(nc, X, V, L, O, w):
    with ExitStack() as ctx:
        sb, ps, sem = alloc(nc, ctx)
        w1 = sb("fg1", [128, BRANCHES, GH])
        w2 = sb("fg2", [128, BRANCHES])
        b1, b2 = sb("fg1b", [128, 1]), sb("fg2b", [128, BRANCHES])
        temp = sb("temp", [128, 4])
        headmean, wo, onorm = sb("headmean", [D, D]), sb("wo", [D, D]), sb("onorm", [D, 1])
        ident, staps = sb("ident_g", [D, D]), sb("staps", [D, SHORT])
        eps = sb("eps_g", [D, 1])
        otile, short = sb("otile", [D, 2, S]), sb("short", [D, 2, S])
        hid = sb("hid_g", [128, S])
        NS = S // 128
        lg = sb("lg", [128, 4, NS * BRANCHES])
        small = sb("small", [128, 4, NS])
        flo = sb("flo", [128, NS])
        mix, part = sb("mix", [D, 2, T]), sb("part", [D, 2, BRANCHES, T])
        sq, rst = sb("sq_g", [D, 2, T]), sb("rst_g", [D, 2, T])
        p_a = ps("p_a", [D, 2, T])
        p_h = ps("p_h", [D, 2, T])
        p_w = ps("p_w", [D, BRANCHES, T])
        s_w, s_set, s_o = sem("g_weights"), sem("g_set"), [sem("g_o0"), sem("g_o1")]
        s_short, s_h, s_hid, s_lg, s_soft, s_exp, s_pw, s_part, s_mix, s_sq, s_mean, s_log, s_rst, s_norm, s_proj, s_out = (
            sem("g_" + n) for n in ("short", "h", "hid", "lg", "soft", "exp", "pw", "part", "mix", "sq", "mean",
                                    "log", "rst", "norm", "proj", "out"))
        block = ctx.enter_context(nc.Block())
        SOFT = 12
        W = 2 * BRANCHES
        half = [slice(h * T, (h + 1) * T) for h in range(HALVES)]

        def from_third(b):
            return not isinstance(b, int) or b > 1

        @block.sync
        def _(sp):
            loads = ((w1[:, :, :], w["fg1"].rearrange("p (k n) -> p k n", k=BRANCHES)), (w2[:, :], w["fg2"][:, :]),
                     (b1[:, :], w["fg_b1"][:, :]), (b2[:, :], w["fg_b2"][:, :]), (temp[:, 0:1], w["logit_temp"][:, :]),
                     (headmean[:, :], w["headmean"][:, :]), (wo[:, :], w["o_proj"][:, :]), (onorm[:, :], w["o_norm"][:, :]),
                     (ident[:, :], w["ident"][:, :]), (staps[:, :], w["fir_short"][:, :]))
            for dst, src in loads:
                sp.dma_start(dst, src).then_inc(s_w, 16)

            def step(b, e, i):
                if from_third(b):
                    sp.wait_ge(s_part, W * (b - 1))
                src = O[:, :].rearrange("p (n c) -> p n c", c=B * CS)[:, :, bass.ds(b * CS, CS)]
                sp.dma_start(otile[:, e, :].rearrange("p (n c) -> p n c", c=CS), src).then_inc(s_o[e], 16)

            pipeline(sp, step)

        @block.tensor
        def _(pe):
            pe.wait_ge(s_w, 160)
            pe.wait_ge(s_set, 4)

            def spread(b, h):
                pe.wait_ge(s_soft, SOFT * (b + 1))
                if started(b) or h:
                    pe.wait_ge(s_part, W * b + BRANCHES * h)
                for g in range(BRANCHES):
                    for s in range(T // 128):
                        c = (h * (T // 128) + s) * BRANCHES + g
                        mm = nc.tensor.matmul(p_w[:, g, s * 128:(s + 1) * 128],
                                              lg[:, 3, c:c + 1].broadcast_to([128, 128]), ident[:, :],
                                              start=True, stop=True)
                    mm.then_inc(s_pw, 1)

            def hidden(b, e, i, h):
                if h == 0:
                    pe.wait_ge(s_o[e], 16 * (i + 1))
                    if started(b):
                        pe.wait_ge(s_soft, SOFT * (b - 1) + 1)
                elif started(b):
                    pe.wait_ge(s_hid, 2 * b)
                srcs = (seq_cols(X, b, h * T, T), short[:, e, half[h]], L[:, bass.ds(b * S + h * T, T)], otile[:, e, half[h]])
                for k in (0, 2, 3, 1):
                    if k == 1 and h == 0:
                        pe.wait_ge(s_short, SHORT * (b + 1))
                    mm = nc.tensor.matmul(p_h[:, h, :], w1[:, k, :], srcs[k], start=(k == 0), stop=(k == 1))
                mm.then_inc(s_h, 1)

            def logits(b):
                pe.wait_ge(s_hid, 2 * (b + 1))
                for s in range(NS):
                    mm = nc.tensor.matmul(p_h[:, 0, s * BRANCHES:(s + 1) * BRANCHES], hid[:, s * 128:(s + 1) * 128],
                                          w2[:, :], start=True, stop=True)
                mm.then_inc(s_lg, 1)

            def mean(b, h):
                pe.wait_ge(s_sq, 2 * b + h + 1)
                if started(b):
                    pe.wait_ge(s_out, 2 * (b - 1) + h + 1)
                nc.tensor.matmul(p_a[:, h, :], headmean[:, :], sq[:, h, :], start=True, stop=True).then_inc(s_mean, 1)

            def project(b, h):
                pe.wait_ge(s_log, 2 * b + h + 1)
                pe.wait_ge(s_norm, 2 * b + h + 1)
                nc.tensor.matmul(p_a[:, h, :], wo[:, :], mix[:, h, :], start=True, stop=True).then_inc(s_proj, 1)

            def step(b, e, i):
                late = not is_first(b)
                if late:
                    spread(b - 1, 0)
                hidden(b, e, i, 0)
                if late:
                    spread(b - 1, 1)
                hidden(b, e, i, 1)
                if late:
                    mean(b - 1, 0)
                logits(b)
                if late:
                    mean(b - 1, 1)
                    project(b - 1, 0)
                    project(b - 1, 1)

            def late(b):
                for part_ in (spread, mean, project):
                    part_(b, 0)
                    part_(b, 1)

            pipeline(pe, step, late)

        @block.scalar
        def _(act):
            nc.scalar.preload_act_table_set(LN_EXP)
            act.wait_ge(s_w, 160)
            act.wait_ge(s_set, 4)
            nc.scalar.activation(temp[:, 1:2], temp[:, 0:1], ACT.Abs).then_inc(s_set, 1)
            act.wait_ge(s_set, 5)
            nc.scalar.activation(temp[:, 1:2], temp[:, 1:2], ACT.Exp, scale=-1.0).then_inc(s_set, 1)
            act.wait_ge(s_set, 6)
            nc.scalar.activation(temp[:, 2:3], temp[:, 1:2], ACT.Ln, bias=1.0).then_inc(s_set, 1)
            act.wait_ge(s_set, 10)

            def square(b, h):
                act.wait_ge(s_mix, 6 * b + 3 * (h + 1))
                if started(b):
                    act.wait_ge(s_mean, 2 * (b - 1) + h + 1)
                nc.scalar.activation(sq[:, h, :], mix[:, h, :], ACT.Square).then_inc(s_sq, 1)

            def factor(b, h):
                act.wait_ge(s_mean, 2 * b + h + 1)
                if started(b):
                    act.wait_ge(s_norm, 2 * (b - 1) + h + 1)
                nc.scalar.activation(rst[:, h, :], p_a[:, h, :], ACT.Ln, bias=eps[:, 0:1]).then_inc(s_log, 1)
                act.wait_ge(s_log, 2 * b + h + 1)
                nc.scalar.activation(rst[:, h, :], rst[:, h, :], ACT.Exp, scale=-0.5).then_inc(s_rst, 1)

            def step(b, e, i):
                late = not is_first(b)
                if late:
                    square(b - 1, 0)
                for h in range(HALVES):
                    act.wait_ge(s_h, 2 * b + h + 1)
                    if late:
                        act.wait_ge(s_lg, b)
                    nc.scalar.activation(hid[:, half[h]], p_h[:, h, :], ACT.Gelu, bias=b1[:, 0:1]).then_inc(s_hid, 1)
                nc.scalar.preload_act_table_set(LN_EXP)
                if late:
                    square(b - 1, 1)
                    factor(b - 1, 0)
                act.wait_ge(s_soft, SOFT * b + 3)
                nc.scalar.activation(lg[:, 1, :], lg[:, 0, :], ACT.Exp, scale=temp[:, 3:4]).then_inc(s_exp, 1)
                if late:
                    factor(b - 1, 1)

            def late(b):
                for h in range(HALVES):
                    square(b, h)
                for h in range(HALVES):
                    factor(b, h)

            pipeline(act, step, late)

        @block.gpsimd
        def _(pool):
            def late(b):
                for h in range(HALVES):
                    pool.wait_ge(s_part, W * b + BRANCHES * h + 2)
                    if started(b):
                        pool.wait_ge(s_proj, 2 * (b - 1) + h + 1)
                    nc.gpsimd.tensor_tensor(mix[:, h, :], part[:, h, 0, :], part[:, h, 1, :], ALU.add).then_inc(s_mix, 1)
                    pool.wait_ge(s_part, W * b + BRANCHES * (h + 1))
                    nc.gpsimd.tensor_tensor(part[:, h, 2, :], part[:, h, 2, :], part[:, h, 3, :], ALU.add).then_inc(s_mix, 1)
                    pool.wait_ge(s_mix, 6 * b + 3 * h + 2)
                    nc.gpsimd.tensor_tensor(mix[:, h, :], mix[:, h, :], part[:, h, 2, :], ALU.add).then_inc(s_mix, 1)

            def step(b, e, i):
                if not is_first(b):
                    late(b - 1)

            pipeline(pool, step, late)

        @block.vector
        def _(dve):
            nc.vector.memset(eps[:, :], EPS).then_inc(s_set, 1)
            dve.wait_ge(s_w, 160)
            for k in range(1, BRANCHES):
                nc.vector.tensor_scalar(w1[:, k, :], w1[:, k, :], 1.0 / H, None, ALU.mult).then_inc(s_set, 1)
            dve.wait_ge(s_set, 7)
            nc.vector.tensor_scalar(temp[:, 1:2], temp[:, 0:1], 0.0, None, ALU.max).then_inc(s_set, 1)
            dve.wait_ge(s_set, 8)
            nc.vector.scalar_tensor_tensor(out=temp[:, 2:3], in0=temp[:, 1:2], scalar=1e-4, in1=temp[:, 2:3],
                                           op0=ALU.add, op1=ALU.add).then_inc(s_set, 1)
            dve.wait_ge(s_set, 9)
            nc.vector.reciprocal(temp[:, 3:4], temp[:, 2:3]).then_inc(s_set, 1)
            view = lambda k: lg[:, k, :].rearrange("p (s g) -> p s g", g=BRANCHES)
            over = lambda x: x.unsqueeze(2).broadcast_to([128, NS, BRANCHES])
            step_ = [0]

            def chain(b, ins):
                step_[0] += 1
                ins.then_inc(s_soft, 1)
                dve.wait_ge(s_soft, SOFT * b + step_[0])

            def softmax_start(b):
                step_[0] = 0
                dve.wait_ge(s_lg, b + 1)
                logits = p_h[:, 0, 0:NS * BRANCHES].rearrange("p (s g) -> p s g", g=BRANCHES)
                chain(b, nc.vector.tensor_tensor(view(0), logits, b2[:, :].unsqueeze(1).broadcast_to([128, NS, BRANCHES]), ALU.add))
                chain(b, nc.vector.tensor_reduce(small[:, 0, :], view(0), AX.X, ALU.max))
                chain(b, nc.vector.tensor_tensor(view(0), view(0), over(small[:, 0, :]), ALU.subtract))

            def softmax_end(b):
                dve.wait_ge(s_exp, b + 1)
                chain(b, nc.vector.tensor_reduce(small[:, 1, :], view(1), AX.X, ALU.add))
                chain(b, nc.vector.reciprocal(small[:, 2, :], small[:, 1, :]))
                chain(b, nc.vector.tensor_tensor(view(2), view(1), over(small[:, 2, :]), ALU.mult))
                chain(b, nc.vector.tensor_scalar(flo[:, :], view(2)[:, :, 3], 0.05, None, ALU.mult))
                for g in range(2):
                    chain(b, nc.vector.tensor_tensor(view(2)[:, :, g], view(2)[:, :, g], flo[:, :], ALU.max))
                chain(b, nc.vector.tensor_reduce(small[:, 1, :], view(2), AX.X, ALU.add))
                chain(b, nc.vector.reciprocal(small[:, 3, :], small[:, 1, :]))
                if started(b):
                    dve.wait_ge(s_pw, W * b)
                chain(b, nc.vector.tensor_tensor(view(3), view(2), over(small[:, 3, :]), ALU.mult))

            def short_fir(b, e):
                if from_third(b):
                    dve.wait_ge(s_h, 2 * (b - 1))
                for j in range(SHORT):
                    v = seq_cols(V, b, j - (SHORT - 1), S)
                    if j:
                        dve.wait_ge(s_short, SHORT * b + j)
                        nc.vector.scalar_tensor_tensor(out=short[:, e, :], in0=v, scalar=staps[:, j:j + 1],
                                                       in1=short[:, e, :], op0=ALU.mult, op1=ALU.add).then_inc(s_short, 1)
                    else:
                        if from_third(b):
                            dve.wait_ge(s_part, W * (b - 1))
                        nc.vector.tensor_scalar(short[:, e, :], v, staps[:, j:j + 1], None, ALU.mult).then_inc(s_short, 1)

            def parts(b, e, h):
                srcs = (short[:, e, half[h]], L[:, bass.ds(b * S + h * T, T)], otile[:, e, half[h]], seq_cols(V, b, h * T, T))
                for g in range(BRANCHES):
                    dve.wait_ge(s_pw, W * b + BRANCHES * h + g + 1)
                    if g == 0 and h == 0:
                        dve.wait_ge(s_short, SHORT * (b + 1))
                    if g == 0 and started(b):
                        dve.wait_ge(s_mix, 6 * (b - 1) + 3 * (h + 1))
                    nc.vector.tensor_tensor(part[:, h, g, :], p_w[:, g, :], srcs[g], ALU.mult).then_inc(s_part, 1)

            def norm(b, h):
                dve.wait_ge(s_rst, 2 * b + h + 1)
                nc.vector.scalar_tensor_tensor(out=mix[:, h, :], in0=mix[:, h, :], scalar=onorm[:, 0:1],
                                               in1=rst[:, h, :], op0=ALU.mult, op1=ALU.mult).then_inc(s_norm, 1)

            def add(b, h):
                x = seq_cols(X, b, h * T, T)
                dve.wait_ge(s_proj, 2 * b + h + 1)
                nc.vector.tensor_tensor(x, x, p_a[:, h, :], ALU.add).then_inc(s_out, 1)

            def step(b, e, i):
                late = not is_first(b)
                short_fir(b, e)
                if late:
                    parts(b - 1, 1 - e, 0)
                    parts(b - 1, 1 - e, 1)
                softmax_start(b)
                if late:
                    norm(b - 1, 0)
                softmax_end(b)
                if late:
                    norm(b - 1, 1)
                    add(b - 1, 0)
                    add(b - 1, 1)

            def late(b):
                e = b % 2
                parts(b, e, 0)
                parts(b, e, 1)
                for part_ in (norm, add):
                    part_(b, 0)
                    part_(b, 1)

            pipeline(dve, step, late)


NE = 32
FI = 256
FK = FI // 128
NT = B * S // 128
TPB = S // 128
DEEP = 8
SLOTS = NT + NE


def logits(nc, X, XT, LG, w, scratch):
    with ExitStack() as ctx:
        sb, ps, sem = alloc(nc, ctx)
        gate_w, ident = sb("gate_w", [D, NE]), sb("ident_m", [D, D])
        zeros = sb("zeros", [128, 8 * D])
        xs = sb("xs", [D, 2, S])
        p_l = [ps(f"p_l{e}", [128, TPB, NE]) for e in range(2)]
        p_t = [ps(f"p_t{e}", [128, TPB, D]) for e in range(2)]
        s_w, s_zero, s_clear = sem("m_weights"), sem("m_zero"), sem("m_clear")
        s_xs, s_l, s_t, s_lg, s_xt = (sem("m_" + n) for n in ("xs", "l", "t", "lg", "xt"))
        block = ctx.enter_context(nc.Block())

        @block.sync
        def _(sp):
            sp.dma_start(gate_w[:, :], w["gate_w"][:, :]).then_inc(s_w, 16)
            sp.dma_start(ident[:, :], w["ident"][:, :]).then_inc(s_w, 16)
            sp.wait_ge(s_zero, 1)
            for i in range(SLOTS // 8):
                dst = scratch["slots"][i * 1024:(i + 1) * 1024, :].rearrange("(p r) d -> p (r d)", p=128)
                sp.dma_start(dst, zeros[:, :]).then_inc(s_clear, 16)
            sp.wait_ge(s_clear, 16 * (SLOTS // 8))

        @block.gpsimd
        def _(pool):
            nc.gpsimd.memset(zeros[:, :], 0.0).then_inc(s_zero, 1)

        @block.tensor
        def _(pe):
            pe.wait_ge(s_w, 32)
            for b in range(B):
                e = b % 2
                pe.wait_ge(s_xs, b + 1)
                if b >= 2:
                    pe.wait_ge(s_lg, b - 1)
                    pe.wait_ge(s_xt, b - 1)
                for s in range(TPB):
                    mm = nc.tensor.matmul(p_l[e][:, s, :], xs[:, e, s * 128:(s + 1) * 128], gate_w[:, :], start=True, stop=True)
                mm.then_inc(s_l, 1)
                for s in range(TPB):
                    mm = nc.tensor.transpose(p_t[e][:, s, :], xs[:, e, s * 128:(s + 1) * 128], ident[:, :])
                mm.then_inc(s_t, 1)

        @block.scalar
        def _(act):
            for b in range(B):
                e = b % 2
                if b >= 2:
                    act.wait_ge(s_t, b - 1)
                nc.scalar.copy(xs[:, e, :], seq_cols(X, b, 0, S)).then_inc(s_xs, 1)
                act.wait_ge(s_l, b + 1)
                nc.scalar.copy(LG[:, b * TPB:(b + 1) * TPB, :], p_l[e][:, :, :]).then_inc(s_lg, 1)

        @block.vector
        def _(dve):
            for b in range(B):
                dve.wait_ge(s_t, b + 1)
                nc.vector.tensor_copy(XT[:, b * TPB:(b + 1) * TPB, :], p_t[b % 2][:, :, :]).then_inc(s_xt, 1)


def scatter_and_shared(nc, X, Y, XS, SCORE, POS, w, scratch):
    with ExitStack() as ctx:
        sb, ps, sem = alloc(nc, ctx)
        wg, wu, wd = sb("swg", [D, FI]), sb("swu", [D, FI]), sb("swd", [128, FK, D])
        sg, hs = sb("sg", [128, 2, FK, T]), sb("hs", [128, 2, FK, T])
        p_g, p_u = ps("p_g", [128, FK, T]), ps("p_u2", [128, FK, T])
        p_d = [ps(f"p_d{h}", [128, T // 128, D]) for h in range(2)]
        s_w, s_sent, s_scaled = sem("h_weights"), sem("h_sent"), sem("h_scaled")
        s_g, s_u, s_sg, s_hs, s_d, s_y = (sem("h_" + n) for n in ("g", "u", "sg", "hs", "d", "y"))
        block = ctx.enter_context(nc.Block())

        @block.sync
        def _(sp):
            sp.dma_start(wg[:, :], w["sg"][:, :]).then_inc(s_w, 16)
            sp.dma_start(wu[:, :], w["su"][:, :]).then_inc(s_w, 16)
            sp.dma_start(wd[:, :, :], w["sd"].rearrange("(k p) n -> p k n", p=128)).then_inc(s_w, 16)

        @block.gpsimd
        def _(pool):
            for t in range(NT):
                if t % TPB == 0:
                    pool.wait_ge(s_scaled, t // TPB + 1)
                pool.indirect_dma_start(out=scratch["slots"][:, :],
                                        out_offset=bass.IndirectOffsetOnAxis(ap=POS[:, t:t + 1], axis=0),
                                        in_=XS[:, t, :], in_offset=None).then_inc(s_sent, 16)
            pool.wait_ge(s_sent, 16 * NT)

        @block.tensor
        def _(pe):
            pe.wait_ge(s_w, 48)

            def wide(b, h):
                for k in range(FK):
                    i = FK * (2 * b + h) + k
                    if not is_first(b) or h:
                        pe.wait_ge(s_hs, i - 1)
                    x = seq_cols(X, b, h * T, T)
                    nc.tensor.matmul(p_g[:, k, :], wg[:, k * 128:(k + 1) * 128], x, start=True, stop=True).then_inc(s_g, 1)
                    nc.tensor.matmul(p_u[:, k, :], wu[:, k * 128:(k + 1) * 128], x, start=True, stop=True).then_inc(s_u, 1)

            def last(b, h):
                t = 2 * b + h
                pe.wait_ge(s_hs, FK * (t + 1))
                if started(b):
                    pe.wait_ge(s_y, t - 1)
                for s in range(T // 128):
                    for k in range(FK):
                        mm = nc.tensor.matmul(p_d[h][:, s, :], hs[:, h, k, s * 128:(s + 1) * 128], wd[:, k, :],
                                              start=(k == 0), stop=(k == FK - 1))
                mm.then_inc(s_d, 1)

            def body(b):
                wide(b, 0)
                if started(b):
                    last(b - 1, 1)
                wide(b, 1)
                last(b, 0)

            loop(pe, B, body)
            last(B - 1, 1)

        @block.scalar
        def _(act):
            def body(b):
                for h in range(2):
                    for k in range(FK):
                        i = FK * (2 * b + h) + k
                        act.wait_ge(s_g, i + 1)
                        if not is_first(b):
                            act.wait_ge(s_hs, i - 3)
                        nc.scalar.activation(sg[:, h, k, :], p_g[:, k, :], ACT.Silu).then_inc(s_sg, 1)

            loop(act, B, body)

        @block.vector
        def _(dve):
            for b in range(B):
                c = slice(b * TPB, (b + 1) * TPB)
                nc.vector.tensor_tensor(XS[:, c, :], Y[:, c, :], SCORE[:, c].unsqueeze(2).broadcast_to([128, TPB, D]),
                                        ALU.mult).then_inc(s_scaled, 1)

            def gated(b, h):
                for k in range(FK):
                    i = FK * (2 * b + h) + k
                    dve.wait_ge(s_sg, i + 1)
                    dve.wait_ge(s_u, i + 1)
                    if not is_first(b):
                        dve.wait_ge(s_d, 2 * b + h - 1)
                    nc.vector.tensor_tensor(hs[:, h, k, :], sg[:, h, k, :], p_u[:, k, :], ALU.mult).then_inc(s_hs, 1)

            def add(b, h):
                dve.wait_ge(s_d, 2 * b + h + 1)
                at = bass.ds(b * TPB + h * (T // 128), T // 128)
                nc.vector.tensor_tensor(Y[:, at, :], Y[:, at, :], p_d[h][:, :, :], ALU.add).then_inc(s_y, 1)

            def body(b):
                gated(b, 0)
                if started(b):
                    add(b - 1, 1)
                gated(b, 1)
                add(b, 0)

            loop(dve, B, body)
            add(B - 1, 1)


def route(nc, SCORE, LG, POS, w, TE):
    with ExitStack() as ctx:
        sb, ps, sem = alloc(nc, ctx)
        N = NT * NE
        down = sb("down", [128, NE])
        before, ones = sb("before", [128, 128], BF16), sb("ones_b", [128, 128], BF16)
        restart = sb("restart", [128, NE, NT])
        top = sb("top", [128, NT])
        cand, oneh = sb("cand", [128, NT, NE]), sb("oneh", [128, NT, NE])
        onehb = sb("onehb", [128, NT, NE], BF16)
        best = sb("best", [128, NT])
        count, prefix = sb("count", [128, NE, NT]), sb("prefix", [128, NE, NT])
        tot, toti = sb("tot", [128, NE]), sb("toti", [128, NE], I32)
        padded, ends, begins, onef = (sb(n, [128, NE]) for n in ("padded", "ends", "begins", "onef"))
        posf = sb("posf", [128, NT])
        starts, cmp, tef = sb("starts", [1, SLOTS]), sb("cmp", [1, SLOTS, NE]), sb("tef", [1, SLOTS])
        p_r, p_c = ps("p_r", [128, NT, NE]), ps("p_c2", [128, NT, NE])
        s_w, s_one, s_r, s_c, s_score, s_d = (
            sem("r_" + n) for n in ("weights", "onehot", "rank", "count", "score", "dve"))
        block = ctx.enter_context(nc.Block())
        bc = lambda x: x.unsqueeze(2).broadcast_to([128, NT, NE])
        rows = lambda x: x.unsqueeze(1).broadcast_to([128, NT, NE])

        @block.sync
        def _(sp):
            loads = ((down[:, :], w["down"][:, :]), (before[:, :].bitcast(U16), w["before"][:, :]), (ones[:, :].bitcast(U16), w["ones"][:, :]),
                     (restart[:, :, :], w["restart"].rearrange("p (e t) -> p e t", t=NT)), (starts[:, :], w["starts"][:, :]))
            for dst, src in loads:
                sp.dma_start(dst, src).then_inc(s_w, 16)

        @block.tensor
        def _(pe):
            pe.wait_ge(s_one, 1)
            flat = lambda t: t[:, :, :].rearrange("p t e -> p (t e)")
            for q in range(N // T):
                c = slice(q * T, (q + 1) * T)
                mm = nc.tensor.matmul(flat(p_c)[:, c], ones[:, :], flat(onehb)[:, c], start=True, stop=True)
            mm.then_inc(s_c, 1)
            for q in range(N // T):
                c = slice(q * T, (q + 1) * T)
                mm = nc.tensor.matmul(flat(p_r)[:, c], before[:, :], flat(onehb)[:, c], start=True, stop=True)
            mm.then_inc(s_r, 1)

        @block.scalar
        def _(act):
            act.wait_ge(s_d, 1)
            nc.scalar.activation(SCORE[:, :], top[:, :], ACT.Sigmoid).then_inc(s_score, 1)

        @block.vector
        def _(dve):
            count_ = [0]

            def chain(ins):
                count_[0] += 1
                ins.then_inc(s_d, 1)
                dve.wait_ge(s_d, count_[0])

            dve.wait_ge(s_w, 80)
            chain(nc.vector.tensor_reduce(top[:, :], LG[:, :, :], AX.X, ALU.max))
            chain(nc.vector.tensor_tensor(cand[:, :, :], LG[:, :, :], bc(top[:, :]), ALU.is_equal))
            chain(nc.vector.tensor_tensor(cand[:, :, :], cand[:, :, :], rows(down[:, :]), ALU.mult))
            chain(nc.vector.tensor_reduce(best[:, :], cand[:, :, :], AX.X, ALU.max))
            chain(nc.vector.tensor_tensor(oneh[:, :, :], bc(best[:, :]), rows(down[:, :]), ALU.is_equal))
            nc.vector.tensor_copy(onehb[:, :, :], oneh[:, :, :]).then_inc(s_one, 1)
            chain(nc.vector.memset(onef[:, :], 1.0))
            dve.wait_ge(s_c, 1)
            chain(nc.vector.tensor_copy(count[:, :, :], p_c[:, :, :].rearrange("p t e -> p e t")))
            flat = lambda t: t[:, :, :].rearrange("p e t -> p (e t)")
            chain(nc.vector.tensor_tensor_scan(flat(prefix), flat(restart), flat(count), 0.0, ALU.mult, ALU.add))
            chain(nc.vector.tensor_scalar(tot[:, :], prefix[:, :, NT - 1], 127.0, None, ALU.add))
            chain(nc.vector.tensor_copy(toti[:, :], tot[:, :]))
            chain(nc.vector.tensor_scalar(toti[:, :], toti[:, :], 7, 7, ALU.arith_shift_right, ALU.logical_shift_left))
            chain(nc.vector.tensor_copy(padded[:, :], toti[:, :]))
            chain(nc.vector.tensor_tensor_scan(ends[:, :], onef[:, :], padded[:, :], 0.0, ALU.mult, ALU.add))
            chain(nc.vector.tensor_tensor(begins[:, :], ends[:, :], padded[:, :], ALU.subtract))
            chain(nc.vector.tensor_tensor(prefix[:, :, :], prefix[:, :, :], count[:, :, :], ALU.subtract))
            chain(nc.vector.tensor_tensor(prefix[:, :, :], prefix[:, :, :],
                                          begins[:, :].unsqueeze(2).broadcast_to([128, NE, NT]), ALU.add))
            dve.wait_ge(s_r, 1)
            chain(nc.vector.tensor_tensor(cand[:, :, :], p_r[:, :, :], prefix[:, :, :].rearrange("p e t -> p t e"), ALU.add))
            chain(nc.vector.tensor_tensor(cand[:, :, :], cand[:, :, :], oneh[:, :, :], ALU.mult))
            chain(nc.vector.tensor_reduce(posf[:, :], cand[:, :, :], AX.X, ALU.add))
            chain(nc.vector.tensor_copy(POS[:, :], posf[:, :]))
            chain(nc.vector.tensor_tensor(cmp[:, :, :], ends[0:1, :].unsqueeze(1).broadcast_to([1, SLOTS, NE]),
                                          starts[:, :].unsqueeze(2).broadcast_to([1, SLOTS, NE]), ALU.is_le))
            chain(nc.vector.tensor_reduce(tef[:, :], cmp[:, :, :], AX.X, ALU.add))
            chain(nc.vector.tensor_scalar(tef[:, :], tef[:, :], float(NE - 1), None, ALU.min))
            chain(nc.vector.tensor_copy(TE[:, :], tef[:, :]))


def experts(nc, w, scratch, TE):
    with ExitStack() as ctx:
        sb, ps, sem = alloc(nc, ctx)
        WE = 2 * FI + FK * D
        wts = sb("wts", [128, DEEP, WE])
        xin, xt = sb("xin", [128, DEEP, D]), sb("xt_e", [D, 2, 128])
        sg, hs, ys = sb("sg_e", [128, 2, FK, 128]), sb("hs_e", [128, 2, FK, 128]), sb("ys", [128, DEEP, D])
        ident = sb("ident_e", [D, D])
        p_t = [ps(f"p_te{i}", [128, T]) for i in range(2)]
        p_gu = [ps(f"p_gu{i}", [128, 2 * FK, 128]) for i in range(2)]
        p_y = [ps(f"p_ye{i}", [128, T]) for i in range(2)]
        s_id = sem("e_ident")
        s_w, s_x, s_out = ([sem(f"e_{n}{i}") for i in range(DEEP)] for n in ("w", "x", "out"))
        s_t, s_xt, s_gu, s_sg, s_hs, s_y, s_ys = (sem("e_" + n) for n in ("t", "xt", "gu", "sg", "hs", "y", "ys"))
        block = ctx.enter_context(nc.Block())

        def tiles(eng, step, late=None):
            for m in range(2 * DEEP):
                step(m, m % DEEP, m // DEEP)
            with eng.Fori(2, SLOTS // DEEP) as i:
                for e in range(DEEP):
                    step(DEEP * i + e, e, i)
            if late:
                late()

        def at_least(m, n):
            return not isinstance(m, int) or m >= n

        def back(m, e, i, n):
            return m - n, (e - n) % DEEP, i if e >= n else i - 1

        @block.sync
        def _(sp):
            sp.dma_start(ident[:, :], w["ident"][:, :]).then_inc(s_id, 16)

            def step(m, e, i):
                number = sp.value_load(TE[0:1, m:m + 1] if isinstance(m, int) else TE[0:1, bass.ds(m, 1)],
                                       min_val=0, max_val=NE - 1)
                if at_least(m, DEEP):
                    sp.wait_ge(s_y, m - (DEEP - 1))
                sp.dma_start(wts[:, e, :], w["experts"][bass.ds(number, 1), :, :].rearrange("e p c -> (e p) c")
                             ).then_inc(s_w[e], 16)
                sp.dma_start(xin[:, e, :], scratch["slots"][bass.ds(m * 128, 128), :]).then_inc(s_x[e], 16)

            tiles(sp, step)

        @block.tensor
        def _(pe):
            pe.wait_ge(s_id, 16)

            def turn(m, e, i):
                pe.wait_ge(s_x[e], 16 * (i + 1))
                if at_least(m, 2):
                    pe.wait_ge(s_xt, m - 1)
                nc.tensor.transpose(p_t[e % 2][:, 0:128], xin[:, e, :], ident[:, :]).then_inc(s_t, 1)

            def wide(m, e, i):
                pe.wait_ge(s_xt, m + 1)
                pe.wait_ge(s_w[e], 16 * (i + 1))
                if at_least(m, 2):
                    pe.wait_ge(s_hs, m - 1)
                for k in range(2 * FK):
                    mm = nc.tensor.matmul(p_gu[e % 2][:, k, :], wts[:, e, k * 128:(k + 1) * 128], xt[:, e % 2, :],
                                          start=True, stop=True)
                mm.then_inc(s_gu, 1)

            def last(m, e, i):
                pe.wait_ge(s_hs, m + 1)
                if at_least(m, 2):
                    pe.wait_ge(s_ys, m - 1)
                for k in range(FK):
                    mm = nc.tensor.matmul(p_y[e % 2][:, 0:D], hs[:, e % 2, k, :],
                                          wts[:, e, 2 * FI + k * D:2 * FI + (k + 1) * D],
                                          start=(k == 0), stop=(k == FK - 1))
                mm.then_inc(s_y, 1)

            def step(m, e, i):
                turn(m, e, i)
                if at_least(m, 1):
                    wide(*back(m, e, i, 1))
                if at_least(m, 2):
                    last(*back(m, e, i, 2))

            def late():
                turns = SLOTS // DEEP
                wide(SLOTS - 1, DEEP - 1, turns - 1)
                last(SLOTS - 2, DEEP - 2, turns - 1)
                last(SLOTS - 1, DEEP - 1, turns - 1)

            tiles(pe, step, late)

        @block.scalar
        def _(act):
            def gate(m, e):
                act.wait_ge(s_gu, m + 1)
                if at_least(m, 2):
                    act.wait_ge(s_hs, m - 1)
                nc.scalar.activation(sg[:, e % 2, :, :], p_gu[e % 2][:, 0:FK, :], ACT.Silu).then_inc(s_sg, 1)

            def result_out(m, e):
                act.wait_ge(s_ys, m + 1)
                act.dma_start(scratch["results"][bass.ds(m * 128, 128), :], ys[:, e, :]).then_inc(s_out[e], 16)

            def step(m, e, i):
                if at_least(m, 1):
                    gate(m - 1, (e - 1) % DEEP)
                if at_least(m, 3):
                    result_out(m - 3, (e - 3) % DEEP)

            def late():
                gate(SLOTS - 1, DEEP - 1)
                for n in (3, 2, 1):
                    result_out(SLOTS - n, DEEP - n)

            tiles(act, step, late)
            for e in range(DEEP):
                act.wait_ge(s_out[e], 16 * (SLOTS // DEEP))

        @block.vector
        def _(dve):
            def columns(m, e):
                dve.wait_ge(s_t, m + 1)
                if at_least(m, 2):
                    dve.wait_ge(s_gu, m - 1)
                nc.vector.tensor_copy(xt[:, e % 2, :], p_t[e % 2][:, 0:128]).then_inc(s_xt, 1)

            def gated(m, e):
                dve.wait_ge(s_sg, m + 1)
                if at_least(m, 2):
                    dve.wait_ge(s_y, m - 1)
                nc.vector.tensor_tensor(hs[:, e % 2, :, :], sg[:, e % 2, :, :], p_gu[e % 2][:, FK:2 * FK, :],
                                        ALU.mult).then_inc(s_hs, 1)

            def result(m, e, i):
                dve.wait_ge(s_y, m + 1)
                if at_least(m, DEEP):
                    dve.wait_ge(s_out[e], 16 * i)
                nc.vector.tensor_copy(ys[:, e, :], p_y[e % 2][:, 0:D]).then_inc(s_ys, 1)

            def step(m, e, i):
                columns(m, e)
                if at_least(m, 1):
                    gated(m - 1, (e - 1) % DEEP)
                if at_least(m, 2):
                    result(*back(m, e, i, 2))

            def late():
                gated(SLOTS - 1, DEEP - 1)
                result(SLOTS - 2, DEEP - 2, SLOTS // DEEP - 1)
                result(SLOTS - 1, DEEP - 1, SLOTS // DEEP - 1)

            tiles(dve, step, late)


def combine(nc, Y, POS, out, scratch):
    with ExitStack() as ctx:
        sb, _, sem = alloc(nc, ctx)
        G = sb("G", [128, NT, D])
        eps = sb("eps_o", [128, 1])
        sums, var, rstd = sb("sums", [128, 2, TPB]), sb("var", [128, 2, TPB]), sb("rstd_o", [128, 2, TPB])
        cen, sq = sb("cen", [128, 2, TPB, D]), sb("sq_o", [128, 2, TPB, D])
        s_g, s_eps, s_add, s_sum, s_cen, s_sq, s_var, s_ln, s_rstd, s_done = (
            sem("z_" + n) for n in ("gathered", "eps", "add", "sum", "cen", "sq", "var", "ln", "rstd", "done"))
        s_out = [sem("z_out0"), sem("z_out1")]
        block = ctx.enter_context(nc.Block())
        dst = out.rearrange("(b t p) d -> b p t d", t=TPB, p=128)
        over = lambda x: x.unsqueeze(2).broadcast_to([128, TPB, D])

        @block.gpsimd
        def _(pool):
            for t in range(NT):
                pool.indirect_dma_start(out=G[:, t, :], out_offset=None, in_=scratch["results"][:, :],
                                        in_offset=bass.IndirectOffsetOnAxis(ap=POS[:, t:t + 1], axis=0)).then_inc(s_g, 16)
                if t % TPB == TPB - 1:
                    pool.wait_ge(s_g, 16 * (t + 1))

        @block.sync
        def _(sp):
            for b in range(B):
                sp.wait_ge(s_done, b + 1)
                sp.dma_start(dst[b], cen[:, b % 2, :, :]).then_inc(s_out[b % 2], 16)
            for e in range(2):
                sp.wait_ge(s_out[e], 16 * B // 2)

        @block.scalar
        def _(act):
            act.wait_ge(s_eps, 1)
            for b in range(B):
                e = b % 2
                act.wait_ge(s_cen, b + 1)
                if b >= 2:
                    act.wait_ge(s_var, b - 1)
                nc.scalar.activation(sq[:, e, :, :], cen[:, e, :, :], ACT.Square).then_inc(s_sq, 1)
                act.wait_ge(s_var, b + 1)
                nc.scalar.activation(var[:, e, :], var[:, e, :], ACT.Ln, bias=eps[:, 0:1], scale=1.0 / D).then_inc(s_ln, 1)
                act.wait_ge(s_ln, b + 1)
                if b >= 2:
                    act.wait_ge(s_done, b - 1)
                nc.scalar.activation(rstd[:, e, :], var[:, e, :], ACT.Exp, scale=-0.5).then_inc(s_rstd, 1)

        @block.vector
        def _(dve):
            nc.vector.memset(eps[:, :], EPS).then_inc(s_eps, 1)

            def centre(b):
                e = b % 2
                c = slice(b * TPB, (b + 1) * TPB)
                dve.wait_ge(s_g, 16 * TPB * (b + 1))
                nc.vector.tensor_tensor(G[:, c, :], G[:, c, :], Y[:, c, :], ALU.add).then_inc(s_add, 1)
                dve.wait_ge(s_add, b + 1)
                nc.vector.tensor_reduce(sums[:, e, :], G[:, c, :], AX.X, ALU.add).then_inc(s_sum, 1)
                dve.wait_ge(s_sum, 2 * b + 1)
                nc.vector.tensor_scalar(sums[:, e, :], sums[:, e, :], 1.0 / D, None, ALU.mult).then_inc(s_sum, 1)
                dve.wait_ge(s_sum, 2 * b + 2)
                if b >= 2:
                    dve.wait_ge(s_out[e], 16 * (b // 2))
                nc.vector.tensor_tensor(cen[:, e, :, :], G[:, c, :], over(sums[:, e, :]), ALU.subtract).then_inc(s_cen, 1)

            def scale(b):
                e = b % 2
                dve.wait_ge(s_sq, b + 1)
                nc.vector.tensor_reduce(var[:, e, :], sq[:, e, :, :], AX.X, ALU.add).then_inc(s_var, 1)
                dve.wait_ge(s_rstd, b + 1)
                nc.vector.tensor_tensor(cen[:, e, :, :], cen[:, e, :, :], over(rstd[:, e, :]), ALU.mult).then_inc(s_done, 1)

            for b in range(B):
                centre(b)
                if b:
                    scale(b - 1)
            scale(B - 1)


def clear_semaphores(nc):
    nc.all_engine_barrier()
    nc.gpsimd.sem_clear(range(min(nc.free_semaphores), max(nc.free_semaphores) + 1))
    nc.all_engine_barrier()


def build(nc, w, out):
    with ExitStack() as ctx:
        X = ctx.enter_context(nc.sbuf_tensor("X", [D, B * ROW], F32))
        with ExitStack() as c1:
            sb, _, _ = alloc(nc, c1)
            dt, dtx, parts = sb("dt", [D, B * S]), sb("dtx", [D, B * S]), sb("parts", [96, B * S], BF16)
            scan_inputs(nc, X, dt, dtx, parts, w)
            selective_scan(nc, X, dt, dtx, parts, w)
        layer_norm(nc, X, w, "n1")
        ternary_ffn(nc, X, w)
        layer_norm(nc, X, w, "n2")
        scratch = {
            "upper": nc.dram_tensor("upper_scratch", (H, NC_, CS, CS), F32, kind="Internal").ap(),
            "records": nc.dram_tensor("record_scratch", (NC_, D, B * REC), F32, kind="Internal").ap(),
        }
        with ExitStack() as c3:
            sb, _, _ = alloc(nc, c3)
            V, L = sb("V", [D, B * ROW]), sb("L", [D, B * S])
            delta_inputs(nc, X, V, L, w, scratch)
            with ExitStack() as c4:
                O = c4.enter_context(nc.sbuf_tensor("O", [D, B * S], F32))
                delta_scan(nc, O, w, scratch)
                gate_mix(nc, X, V, L, O, w)
        layer_norm(nc, X, w, "n3")
        clear_semaphores(nc)
        scratch["slots"] = nc.dram_tensor("slot_scratch", (SLOTS * 128, D), F32, kind="Internal").ap()
        scratch["results"] = nc.dram_tensor("result_scratch", (SLOTS * 128, D), F32, kind="Internal").ap()
        with ExitStack() as c5:
            sb, _, _ = alloc(nc, c5)
            Y = sb("Y", [128, NT, D])
            POS, TE = sb("POS", [128, NT], U32), sb("TE", [1, SLOTS], I32)
            with ExitStack() as c6:
                sb, _, _ = alloc(nc, c6)
                XS, SCORE = sb("XS", [128, NT, D]), sb("SCORE", [128, NT])
                with ExitStack() as c7:
                    sb, _, _ = alloc(nc, c7)
                    LG = sb("LG", [128, NT, NE])
                    logits(nc, X, Y, LG, w, scratch)
                    route(nc, SCORE, LG, POS, w, TE)
                scatter_and_shared(nc, X, Y, XS, SCORE, POS, w, scratch)
            experts(nc, w, scratch, TE)
            combine(nc, Y, POS, out, scratch)


def bf16_ones(where):
    return np.where(where, 0x3F80, 0).astype(np.uint16)


def lay_out(inputs):
    g = {k: np.ascontiguousarray(v) for k, v in inputs.items()}
    col = lambda v: np.ascontiguousarray(v.reshape(-1, 128).T)
    T_ = lambda v: np.ascontiguousarray(v.T)
    a = {}
    a["x"] = T_(g["L0_attn_x"].reshape(B * S, D))
    wx = g["L0_attn_W_xproj"]
    a["bc"] = np.ascontiguousarray(np.concatenate([wx[:, :32]] * 3, axis=1))
    a["low"] = np.ascontiguousarray(wx[:, 32:])
    a["dt"] = g["L0_attn_W_dt"]
    a["b_dt"] = col(g["L0_attn_b_dt"])
    a["A_log"] = T_(g["L0_attn_A_log"])
    for n in ("w1", "w2", "h1", "h2", "w3"):
        a[n] = T_(g[f"L0_ffn_{n}_w"])
    a["ffn_scales"] = np.ascontiguousarray(np.concatenate([col(g[f"L0_ffn_{n}_s"]) for n in ("w1", "w2", "h1", "h2", "w3")], axis=1))
    rep = lambda v, n=128: np.ascontiguousarray(np.broadcast_to(v.reshape(1, -1), (n, v.size)))
    for n in "qkv":
        a[n + "_proj"] = T_(g[f"L1_attn_{n}_proj_w"])
        a[n + "_conv"] = rep(g[f"L1_attn_{n}_conv_w"].T)
    a["b_proj"] = np.ascontiguousarray(np.repeat(g["L1_attn_b_proj_w"].T, DH, axis=1))
    a["fir_long"] = np.ascontiguousarray(g["L1_attn_fir_long_w"].reshape(D, LONG))
    a["fir_short"] = np.ascontiguousarray(g["L1_attn_fir_short_w"].reshape(D, SHORT))
    fg = g["L1_attn_fg_w1"].T
    a["fg1"] = np.ascontiguousarray(np.concatenate([fg[:D]] + [np.tile(fg[D + DH * i:D + DH * (i + 1)], (H, 1)) for i in range(3)], axis=1))
    a["fg2"] = np.ascontiguousarray(g["L1_attn_fg_w2"].T)
    a["fg_b1"] = col(g["L1_attn_fg_b1"])
    a["fg_b2"] = rep(g["L1_attn_fg_b2"])
    a["logit_temp"] = rep(g["L1_attn_logit_temp"])
    a["o_proj"] = T_(g["L1_attn_o_proj_w"])
    a["o_norm"] = np.ascontiguousarray(np.tile(g["L1_attn_o_norm_w"], H).reshape(D, 1))
    a["gate_w"] = g["L1_ffn_gate_w"]
    a["sg"], a["su"], a["sd"] = (g[f"L1_ffn_shared_{n}_w"] for n in ("gate", "up", "down"))
    rd = g["L1_ffn_routed_down_w"].reshape(NE, FK, 128, D).transpose(0, 2, 1, 3).reshape(NE, 128, FK * D)
    a["experts"] = np.ascontiguousarray(np.concatenate([g["L1_ffn_routed_gate_w"], g["L1_ffn_routed_up_w"], rd], axis=2))
    i128 = np.arange(128)
    a["down"] = np.ascontiguousarray(np.broadcast_to((NE - np.arange(NE)).astype(np.float32), (128, NE)))
    a["before"] = bf16_ones(i128[:, None] < i128[None, :])
    a["ones"] = bf16_ones(np.ones((128, 128), bool))
    a["restart"] = np.ascontiguousarray(np.broadcast_to((np.arange(NE * NT) % NT != 0).astype(np.float32), (128, NE * NT)))
    a["starts"] = (128.0 * np.arange(SLOTS)).astype(np.float32).reshape(1, SLOTS)
    i32 = np.arange(32)
    a["keep_lt"] = np.tile((i32[:, None] < i32[None, :]).astype(np.float32), (H, 1))
    a["keep_le"] = np.tile((i32[:, None] <= i32[None, :]).astype(np.float32), (H, 1))
    a["headsum"] = np.kron(np.eye(H, dtype=np.float32), np.ones((DH, DH), np.float32))
    a["headmean"] = np.kron(np.eye(H, dtype=np.float32), np.full((DH, DH), 1.0 / DH, np.float32))
    a["eye32"] = np.ascontiguousarray(np.broadcast_to(np.eye(32, dtype=np.float32).reshape(1, -1), (128, 1024)))

    r = np.arange(96)
    a["select"] = np.ascontiguousarray(np.broadcast_to(bf16_ones((r[:, None] % 32 == np.arange(32)[None, :])[:, :, None]), (96, 32, 128)))
    a["ident"] = np.eye(128, dtype=np.float32)
    a["mean_w"] = np.full((128, 128), 1.0 / D, np.float32)
    return a


def kernel(**inputs):
    import concourse.bacc as bacc
    from concourse.bass_utils import run_bass_kernel_spmd

    a = lay_out(inputs)
    nc = bacc.Bacc("TRN2", target_bir_lowering=False, num_devices=1)
    w = {k: nc.dram_tensor("in_" + k, v.shape, mybir.dt.from_np(v.dtype), kind="ExternalInput").ap() for k, v in a.items()}
    out = nc.dram_tensor("out_x", (B * S, D), F32, kind="ExternalOutput").ap()
    build(nc, w, out)
    r = run_bass_kernel_spmd(nc, [{"in_" + k: v for k, v in a.items()}], core_ids=[0])
    return r.results[0]["out_x"].reshape(B, S, D)
```
